# Optimizing a Trainium2 kernel written in Bass

```python
import numpy as np
import jax
import jax.numpy as jnp

def _softmax(x, axis=-1):
    return jax.nn.softmax(x, axis=axis)

def _gelu(x):
    return jax.nn.gelu(x, approximate=True)

def _silu(x):
    return jax.nn.silu(x)

def _sigmoid(x):
    return jax.nn.sigmoid(x)

def _layernorm(x, axis=-1, eps=1e-05):
    m = jnp.mean(x, axis=axis, keepdims=True)
    v = jnp.var(x, axis=axis, keepdims=True)
    return (x - m) / jnp.sqrt(v + eps)

def _scatter_add(tgt, idx, src, axis=0):
    return tgt.at[idx].add(src)

def _segment_sum(src, seg, n):
    return jax.ops.segment_sum(src, seg, n)
kernel_name = 'mk_decoder_postln_d2_seqx_r4_1d9c9b'

def setup_inputs(seed: int=0):
    np.random.seed(seed)
    _w = jnp.asarray

    def _rec_inputs():
        import jax
        import jax.numpy as jnp
        _rk = jax.random.key(seed)
        x = -0.0002928 + 1 * jax.random.normal(jax.random.fold_in(_rk, 1), (4, 512, 256), jnp.float32)
        _lenS = 512 - jax.random.randint(jax.random.fold_in(_rk, 7), (4,), 0, max(1, 512 // 4) + 1, jnp.int32)
        _lenS2 = 512 - jax.random.randint(jax.random.fold_in(_rk, 8), (4,), 0, max(1, 512 // 4) + 1, jnp.int32)
        _ctx_1024P = jax.random.normal(jax.random.fold_in(_rk, 11), (4, 16, 256), jnp.float32)
        _ctx_1024c = jax.random.dirichlet(jax.random.fold_in(_rk, 511), 0.3 * jnp.ones((16,), jnp.float32), (4, 512))
        _ctx_1024t = jnp.einsum('bsk,bkd->bsd', _ctx_1024c, _ctx_1024P)
        _ctx_1024t = _ctx_1024t * jax.lax.rsqrt(jnp.mean(jnp.square(_ctx_1024t)) + 1e-12) * 0.953939
        ctx_1024 = -1.39393e-06 + 0.999914 * (_ctx_1024t + 0.3 * jax.random.normal(jax.random.fold_in(_rk, 611), (4, 512, 256), jnp.float32))
        return (x, ctx_1024)
    x, ctx_1024 = _rec_inputs()

    def _L0_attn_setup():
        import jax, jax.numpy as jnp
        import numpy as np
        EMBED_DIM = 256
        SEQ = 512
        BATCH = 8
        LN_EPS = 1e-05

        def _layernorm(h, gamma, beta):
            mu = jnp.mean(h, axis=-1, keepdims=True)
            var = jnp.mean(jnp.square(h - mu), axis=-1, keepdims=True)
            return (h - mu) * jax.lax.rsqrt(var + LN_EPS) * gamma + beta

        def _scan(inp, lam):

            def combine(c1, c2):
                a1, u1 = c1
                a2, u2 = c2
                return (a1 * a2, a2 * u1 + u2)
            _, h = jax.lax.associative_scan(combine, (lam, inp), axis=0)
            return h
        key = jax.random.key(seed)
        ks = jax.random.split(key, 11)
        d = EMBED_DIM
        s = 1.0 / np.sqrt(d)
        x = jax.random.normal(ks[0], (SEQ, BATCH, d), dtype=jnp.float32)
        W_in = jax.random.uniform(ks[1], (d, d), minval=-s, maxval=s)
        b_in = jax.random.uniform(ks[2], (d,), minval=-s, maxval=s)
        W_lam = jax.random.uniform(ks[3], (d, d), minval=-s, maxval=s)
        b_lam = jax.random.uniform(ks[4], (d,), minval=-s, maxval=s)
        W_gate = jax.random.uniform(ks[5], (d, d), minval=-s, maxval=s)
        b_gate = jax.random.uniform(ks[6], (d,), minval=-s, maxval=s)
        W_out = jax.random.uniform(ks[7], (d, d), minval=-s, maxval=s)
        b_out = jax.random.uniform(ks[8], (d,), minval=-s, maxval=s)
        gamma = jnp.ones((d,), dtype=jnp.float32)
        beta = jnp.zeros((d,), dtype=jnp.float32)
        return {'x': x, 'W_in': W_in, 'b_in': b_in, 'W_lam': W_lam, 'b_lam': b_lam, 'W_gate': W_gate, 'b_gate': b_gate, 'W_out': W_out, 'b_out': b_out, 'gamma': gamma, 'beta': beta}
    _L0_attn_all = _L0_attn_setup()
    _L0_attn_in = {k: v for k, v in _L0_attn_all.items() if k in ('W_in', 'b_in', 'W_lam', 'b_lam', 'W_gate', 'b_gate', 'W_out', 'b_out', 'gamma', 'beta')}
    del _L0_attn_all

    def _L0_xattn_setup():
        import jax, jax.numpy as jnp
        import numpy as np
        key = jax.random.key(seed)
        ks = jax.random.split(key, 8)
        B, T, S = (32, 128, 128)
        Din, H, C = (256, 256, 256)
        s = 0.02
        return {'x': jax.random.normal(ks[0], (B, T, Din), jnp.float32), 'context': jax.random.normal(ks[1], (B, S, C), jnp.float32), 'W_ih': jax.random.normal(ks[2], (4 * H, Din + H), jnp.float32) * s, 'W_hh': jax.random.normal(ks[3], (4 * H, H), jnp.float32) * s, 'b_ih': jnp.zeros((4 * H,), jnp.float32), 'b_hh': jnp.zeros((4 * H,), jnp.float32), 'Wq': jax.random.normal(ks[4], (C, H), jnp.float32) * s, 'Wout': jax.random.normal(ks[5], (H, C + H), jnp.float32) * s, 'b_out': jnp.zeros((H,), jnp.float32)}
    _L0_xattn_all = _L0_xattn_setup()
    _L0_xattn_in = {k: v for k, v in _L0_xattn_all.items() if k in ('W_ih', 'W_hh', 'b_ih', 'b_hh', 'Wq', 'Wout', 'b_out')}
    del _L0_xattn_all

    def _L0_ffn_setup():
        import jax, jax.numpy as jnp
        import numpy as np
        EMBED = 256
        NUM_EXPERTS = 8
        TOP_K = 2
        key = jax.random.key(seed)
        ks = jax.random.split(key, 6)
        scale = EMBED ** (-0.5)
        return {'x': jax.random.normal(ks[0], (4, 1024, EMBED), jnp.float32), 'router_w': jax.random.normal(ks[1], (EMBED, NUM_EXPERTS), jnp.float32) * scale, 'router_b': jnp.zeros((NUM_EXPERTS,), jnp.float32), 'we_gate': jax.random.normal(ks[2], (NUM_EXPERTS, EMBED, EMBED), jnp.float32) * scale, 'we_up': jax.random.normal(ks[3], (NUM_EXPERTS, EMBED, EMBED), jnp.float32) * scale, 'we_down': jax.random.normal(ks[4], (NUM_EXPERTS, EMBED, EMBED), jnp.float32) * scale}
    _L0_ffn_all = _L0_ffn_setup()
    _L0_ffn_in = {k: v for k, v in _L0_ffn_all.items() if k in ('router_w', 'router_b', 'we_gate', 'we_up', 'we_down')}
    del _L0_ffn_all

    def _L1_attn_setup():
        import jax, jax.numpy as jnp
        import numpy as np
        B, T, C, H = (2, 512, 256, 16)
        D = C // H
        RW, RA, RG = (64, 64, 128)
        EPS = 1e-05

        def _rwkv7_scan(r, log_w, k, v, a, b):
            Bn, Tn, Hn, Dn = r.shape

            def step(S, xs):
                r_t, w_t, k_t, v_t, a_t, b_t = xs
                sa = jnp.einsum('bhij,bhj->bhi', S, a_t)
                S = S * jnp.exp(w_t)[:, :, None, :] + sa[..., None] * b_t[:, :, None, :] + v_t[..., None] * k_t[:, :, None, :]
                o_t = jnp.einsum('bhij,bhj->bhi', S, r_t)
                return (S, o_t)
            S0 = jnp.zeros((Bn, Hn, Dn, Dn), r.dtype)
            xs = tuple((jnp.swapaxes(x, 0, 1) for x in (r, log_w, k, v, a, b)))
            _, o = jax.lax.scan(step, S0, xs)
            return jnp.swapaxes(o, 0, 1)
        key = jax.random.key(seed)
        ks = iter(jax.random.split(key, 40))
        n = lambda s, sc=0.02: jax.random.normal(next(ks), s, jnp.float32) * sc
        u = lambda s: jax.random.uniform(next(ks), s, jnp.float32)
        return dict(hidden_states=jax.random.normal(next(ks), (B, T, C), jnp.float32), x_r=u((C,)), x_w=u((C,)), x_k=u((C,)), x_v=u((C,)), x_a=u((C,)), x_g=u((C,)), k_k=u((C,)), k_a=u((C,)), r_k=n((H, D), 0.1), W_r=n((C, C)), W_k=n((C, C)), W_v=n((C, C)), W_o=n((C, C)), w_lora_a=n((C, RW)), w_lora_b=n((RW, C)), w_lora_bias=n((C,), 0.1), a_lora_a=n((C, RA)), a_lora_b=n((RA, C)), a_lora_bias=jnp.zeros((C,), jnp.float32), g_lora_a=n((C, RG)), g_lora_b=n((RG, C)), g_lora_bias=jnp.zeros((C,), jnp.float32), gn_weight=jnp.ones((C,), jnp.float32), gn_bias=jnp.zeros((C,), jnp.float32))
    _L1_attn_all = _L1_attn_setup()
    _L1_attn_in = {k: v for k, v in _L1_attn_all.items() if k in ('x_r', 'x_w', 'x_k', 'x_v', 'x_a', 'x_g', 'k_k', 'k_a', 'r_k', 'W_r', 'W_k', 'W_v', 'W_o', 'w_lora_a', 'w_lora_b', 'w_lora_bias', 'a_lora_a', 'a_lora_b', 'a_lora_bias', 'g_lora_a', 'g_lora_b', 'g_lora_bias', 'gn_weight', 'gn_bias')}
    del _L1_attn_all

    def _L1_xattn_setup():
        import jax, jax.numpy as jnp
        import numpy as np
        DIM = 256
        key = jax.random.key(seed)
        ks = jax.random.split(key, 8)
        B, S, D = (8, 512, DIM)
        scale = 1.0 / np.sqrt(D)
        x1 = jax.random.normal(ks[0], (B, S, D), dtype=jnp.float32)
        x2 = jax.random.normal(ks[1], (B, S, D), dtype=jnp.float32)
        Wq = jax.random.normal(ks[2], (D, D), dtype=jnp.float32) * scale
        bq = jnp.zeros((D,), dtype=jnp.float32)
        Wk = jax.random.normal(ks[3], (D, D), dtype=jnp.float32) * scale
        bk = jnp.zeros((D,), dtype=jnp.float32)
        Wv = jax.random.normal(ks[4], (D, D), dtype=jnp.float32) * scale
        bv = jnp.zeros((D,), dtype=jnp.float32)
        return {'x1': x1, 'x2': x2, 'Wq': Wq, 'bq': bq, 'Wk': Wk, 'bk': bk, 'Wv': Wv, 'bv': bv}
    _L1_xattn_all = _L1_xattn_setup()
    _L1_xattn_in = {k: v for k, v in _L1_xattn_all.items() if k in ('Wq', 'bq', 'Wk', 'bk', 'Wv', 'bv')}
    del _L1_xattn_all

    def _L1_ffn_setup():
        import jax, jax.numpy as jnp
        import numpy as np
        B, S, H, I, E, K = (4, 512, 256, 688, 4, 2)
        key = jax.random.key(seed)
        ks = jax.random.split(key, 8)
        inv_h = 1.0 / np.sqrt(H)
        inv_i = 1.0 / np.sqrt(I)
        return {'x': jax.random.normal(ks[0], (B, S, H), jnp.float32), 'gate_w': jax.random.normal(ks[1], (E, H), jnp.float32) * inv_h, 'eg': jax.random.normal(ks[2], (E, I, H), jnp.float32) * inv_h, 'eu': jax.random.normal(ks[3], (E, I, H), jnp.float32) * inv_h, 'ed': jax.random.normal(ks[4], (E, H, I), jnp.float32) * inv_i, 'sg': jax.random.normal(ks[5], (I, H), jnp.float32) * inv_h, 'su': jax.random.normal(ks[6], (I, H), jnp.float32) * inv_h, 'sd': jax.random.normal(ks[7], (H, I), jnp.float32) * inv_i}
    _L1_ffn_all = _L1_ffn_setup()
    _L1_ffn_in = {k: v for k, v in _L1_ffn_all.items() if k in ('gate_w', 'eg', 'eu', 'ed', 'sg', 'su', 'sd')}
    del _L1_ffn_all
    return {'x': x, 'ctx_1024': ctx_1024, 'L0_attn_W_in': _L0_attn_in['W_in'], 'L0_attn_b_in': _L0_attn_in['b_in'], 'L0_attn_W_lam': _L0_attn_in['W_lam'], 'L0_attn_b_lam': _L0_attn_in['b_lam'], 'L0_attn_W_gate': _L0_attn_in['W_gate'], 'L0_attn_b_gate': _L0_attn_in['b_gate'], 'L0_attn_W_out': _L0_attn_in['W_out'], 'L0_attn_b_out': _L0_attn_in['b_out'], 'L0_attn_gamma': _L0_attn_in['gamma'], 'L0_attn_beta': _L0_attn_in['beta'], 'L0_xattn_W_ih': _L0_xattn_in['W_ih'], 'L0_xattn_W_hh': _L0_xattn_in['W_hh'], 'L0_xattn_b_ih': _L0_xattn_in['b_ih'], 'L0_xattn_b_hh': _L0_xattn_in['b_hh'], 'L0_xattn_Wq': _L0_xattn_in['Wq'], 'L0_xattn_Wout': _L0_xattn_in['Wout'], 'L0_xattn_b_out': _L0_xattn_in['b_out'], 'L0_ffn_router_w': _L0_ffn_in['router_w'], 'L0_ffn_router_b': _L0_ffn_in['router_b'], 'L0_ffn_we_gate': _L0_ffn_in['we_gate'], 'L0_ffn_we_up': _L0_ffn_in['we_up'], 'L0_ffn_we_down': _L0_ffn_in['we_down'], 'L1_attn_x_r': _L1_attn_in['x_r'], 'L1_attn_x_w': _L1_attn_in['x_w'], 'L1_attn_x_k': _L1_attn_in['x_k'], 'L1_attn_x_v': _L1_attn_in['x_v'], 'L1_attn_x_a': _L1_attn_in['x_a'], 'L1_attn_x_g': _L1_attn_in['x_g'], 'L1_attn_k_k': _L1_attn_in['k_k'], 'L1_attn_k_a': _L1_attn_in['k_a'], 'L1_attn_r_k': _L1_attn_in['r_k'], 'L1_attn_W_r': _L1_attn_in['W_r'], 'L1_attn_W_k': _L1_attn_in['W_k'], 'L1_attn_W_v': _L1_attn_in['W_v'], 'L1_attn_W_o': _L1_attn_in['W_o'], 'L1_attn_w_lora_a': _L1_attn_in['w_lora_a'], 'L1_attn_w_lora_b': _L1_attn_in['w_lora_b'], 'L1_attn_w_lora_bias': _L1_attn_in['w_lora_bias'], 'L1_attn_a_lora_a': _L1_attn_in['a_lora_a'], 'L1_attn_a_lora_b': _L1_attn_in['a_lora_b'], 'L1_attn_a_lora_bias': _L1_attn_in['a_lora_bias'], 'L1_attn_g_lora_a': _L1_attn_in['g_lora_a'], 'L1_attn_g_lora_b': _L1_attn_in['g_lora_b'], 'L1_attn_g_lora_bias': _L1_attn_in['g_lora_bias'], 'L1_attn_gn_weight': _L1_attn_in['gn_weight'], 'L1_attn_gn_bias': _L1_attn_in['gn_bias'], 'L1_xattn_Wq': _L1_xattn_in['Wq'], 'L1_xattn_bq': _L1_xattn_in['bq'], 'L1_xattn_Wk': _L1_xattn_in['Wk'], 'L1_xattn_bk': _L1_xattn_in['bk'], 'L1_xattn_Wv': _L1_xattn_in['Wv'], 'L1_xattn_bv': _L1_xattn_in['bv'], 'L1_ffn_gate_w': _L1_ffn_in['gate_w'], 'L1_ffn_eg': _L1_ffn_in['eg'], 'L1_ffn_eu': _L1_ffn_in['eu'], 'L1_ffn_ed': _L1_ffn_in['ed'], 'L1_ffn_sg': _L1_ffn_in['sg'], 'L1_ffn_su': _L1_ffn_in['su'], 'L1_ffn_sd': _L1_ffn_in['sd']}

def reference(x, ctx_1024, L0_attn_W_in, L0_attn_b_in, L0_attn_W_lam, L0_attn_b_lam, L0_attn_W_gate, L0_attn_b_gate, L0_attn_W_out, L0_attn_b_out, L0_attn_gamma, L0_attn_beta, L0_xattn_W_ih, L0_xattn_W_hh, L0_xattn_b_ih, L0_xattn_b_hh, L0_xattn_Wq, L0_xattn_Wout, L0_xattn_b_out, L0_ffn_router_w, L0_ffn_router_b, L0_ffn_we_gate, L0_ffn_we_up, L0_ffn_we_down, L1_attn_x_r, L1_attn_x_w, L1_attn_x_k, L1_attn_x_v, L1_attn_x_a, L1_attn_x_g, L1_attn_k_k, L1_attn_k_a, L1_attn_r_k, L1_attn_W_r, L1_attn_W_k, L1_attn_W_v, L1_attn_W_o, L1_attn_w_lora_a, L1_attn_w_lora_b, L1_attn_w_lora_bias, L1_attn_a_lora_a, L1_attn_a_lora_b, L1_attn_a_lora_bias, L1_attn_g_lora_a, L1_attn_g_lora_b, L1_attn_g_lora_bias, L1_attn_gn_weight, L1_attn_gn_bias, L1_xattn_Wq, L1_xattn_bq, L1_xattn_Wk, L1_xattn_bk, L1_xattn_Wv, L1_xattn_bv, L1_ffn_gate_w, L1_ffn_eg, L1_ffn_eu, L1_ffn_ed, L1_ffn_sg, L1_ffn_su, L1_ffn_sd):
    import jax
    import jax.numpy as jnp

    def _L0_attn_ref(x, W_in, b_in, W_lam, b_lam, W_gate, b_gate, W_out, b_out, gamma, beta):
        import jax, jax.numpy as jnp
        import numpy as np
        EMBED_DIM = 256
        SEQ = 512
        BATCH = 8
        LN_EPS = 1e-05

        def _layernorm(h, gamma, beta):
            mu = jnp.mean(h, axis=-1, keepdims=True)
            var = jnp.mean(jnp.square(h - mu), axis=-1, keepdims=True)
            return (h - mu) * jax.lax.rsqrt(var + LN_EPS) * gamma + beta

        def _scan(inp, lam):

            def combine(c1, c2):
                a1, u1 = c1
                a2, u2 = c2
                return (a1 * a2, a2 * u1 + u2)
            _, h = jax.lax.associative_scan(combine, (lam, inp), axis=0)
            return h
        lower_bound = 0.0
        inp = jax.nn.silu(x @ W_in.T + b_in)
        gate = jax.nn.silu(x @ W_gate.T + b_gate)
        lam = lower_bound + (1.0 - lower_bound) * jax.nn.sigmoid(x @ W_lam.T + b_lam)
        inp = (1.0 - lam) * inp
        hiddens = _scan(inp, lam)
        hiddens = _layernorm(hiddens, gamma, beta)
        return hiddens * gate @ W_out.T + b_out

    def _L0_xattn_ref(x, context, W_ih, W_hh, b_ih, b_hh, Wq, Wout, b_out):
        import jax, jax.numpy as jnp
        import numpy as np
        B, T, Din = x.shape
        H = W_hh.shape[1]

        def attend(h):
            q = h @ Wq.T
            scores = jnp.einsum('bc,bsc->bs', q, context)
            alpha = jax.nn.softmax(scores, axis=-1)
            ctx = jnp.einsum('bs,bsc->bc', alpha, context)
            return jnp.tanh(jnp.concatenate([ctx, h], axis=-1) @ Wout.T + b_out)

        def step(carry, x_t):
            h, c, attn = carry
            inp = jnp.concatenate([x_t, attn], axis=-1)
            gates = inp @ W_ih.T + b_ih + h @ W_hh.T + b_hh
            i, f, g, o = jnp.split(gates, 4, axis=-1)
            c = jax.nn.sigmoid(f) * c + jax.nn.sigmoid(i) * jnp.tanh(g)
            h = jax.nn.sigmoid(o) * jnp.tanh(c)
            out = attn_out = attend(h)
            return ((h, c, attn_out), out)
        h0 = jnp.zeros((B, H), x.dtype)
        init = (h0, h0, h0)
        xs = jnp.swapaxes(x, 0, 1)
        _, outs = jax.lax.scan(step, init, xs)
        return jnp.swapaxes(outs, 0, 1)

    def _L0_ffn_ref(x, router_w, router_b, we_gate, we_up, we_down):
        import jax, jax.numpy as jnp
        import numpy as np
        EMBED = 256
        NUM_EXPERTS = 8
        TOP_K = 2
        x_shape = x.shape
        x_flat = x.reshape(-1, x_shape[-1])
        num_tokens = x_flat.shape[0]
        router_logits = x_flat @ router_w + router_b
        topk_weights, topk_indices = jax.lax.top_k(router_logits, k=TOP_K)
        topk_weights = jax.nn.softmax(topk_weights, axis=-1)
        token_idx_mesh = jnp.repeat(jnp.arange(num_tokens), TOP_K)
        expert_idx_mesh = topk_indices.reshape(-1)
        sort_permutation = jnp.argsort(expert_idx_mesh)
        sorted_expert_idx = expert_idx_mesh[sort_permutation]
        sorted_token_idx = token_idx_mesh[sort_permutation]
        group_sizes = jnp.bincount(sorted_expert_idx, length=NUM_EXPERTS)
        sorted_tokens = x_flat[sorted_token_idx]
        ff_gate = jax.lax.ragged_dot(sorted_tokens, we_gate, group_sizes)
        ff_up = jax.lax.ragged_dot(sorted_tokens, we_up, group_sizes)
        activated = jax.nn.silu(ff_gate) * ff_up
        ff_out = jax.lax.ragged_dot(activated, we_down, group_sizes)
        sorted_weights = topk_weights.reshape(-1)[sort_permutation]
        ff_out = ff_out * sorted_weights[:, None]
        output_flat = jnp.zeros_like(x_flat).at[sorted_token_idx].add(ff_out)
        return output_flat.reshape(x_shape)

    def _L1_attn_ref(hidden_states, x_r, x_w, x_k, x_v, x_a, x_g, k_k, k_a, r_k, W_r, W_k, W_v, W_o, w_lora_a, w_lora_b, w_lora_bias, a_lora_a, a_lora_b, a_lora_bias, g_lora_a, g_lora_b, g_lora_bias, gn_weight, gn_bias):
        import jax, jax.numpy as jnp
        import numpy as np
        B, T, C, H = (2, 512, 256, 16)
        D = C // H
        RW, RA, RG = (64, 64, 128)
        EPS = 1e-05

        def _rwkv7_scan(r, log_w, k, v, a, b):
            Bn, Tn, Hn, Dn = r.shape

            def step(S, xs):
                r_t, w_t, k_t, v_t, a_t, b_t = xs
                sa = jnp.einsum('bhij,bhj->bhi', S, a_t)
                S = S * jnp.exp(w_t)[:, :, None, :] + sa[..., None] * b_t[:, :, None, :] + v_t[..., None] * k_t[:, :, None, :]
                o_t = jnp.einsum('bhij,bhj->bhi', S, r_t)
                return (S, o_t)
            S0 = jnp.zeros((Bn, Hn, Dn, Dn), r.dtype)
            xs = tuple((jnp.swapaxes(x, 0, 1) for x in (r, log_w, k, v, a, b)))
            _, o = jax.lax.scan(step, S0, xs)
            return jnp.swapaxes(o, 0, 1)
        Bn, Tn, Cn = hidden_states.shape
        shifted = jnp.concatenate([jnp.zeros_like(hidden_states[:, :1]), hidden_states[:, :-1]], axis=1)
        delta = shifted - hidden_states
        xr = hidden_states + delta * x_r
        xw = hidden_states + delta * x_w
        xk = hidden_states + delta * x_k
        xv = hidden_states + delta * x_v
        xa = hidden_states + delta * x_a
        r = xr @ W_r
        log_w = -jax.nn.softplus(-(jnp.tanh(xw @ w_lora_a) @ w_lora_b + w_lora_bias)) - 0.5
        k = xk @ W_k
        v = xv @ W_v
        a = jax.nn.sigmoid(xa @ a_lora_a @ a_lora_b + a_lora_bias)
        g = jax.nn.sigmoid(r @ g_lora_a) @ g_lora_b + g_lora_bias
        kk = (k * k_k).reshape(Bn, Tn, H, D)
        kk = kk / jnp.maximum(jnp.linalg.norm(kk, axis=-1, keepdims=True), 1e-12)
        k = k * (1.0 + (a - 1.0) * k_a)
        rh = r.reshape(Bn, Tn, H, D)
        wh = log_w.reshape(Bn, Tn, H, D)
        kh = k.reshape(Bn, Tn, H, D)
        vh = v.reshape(Bn, Tn, H, D)
        ah = a.reshape(Bn, Tn, H, D)
        o = _rwkv7_scan(rh, wh, kh, vh, -kk, kk * ah)
        mu = o.mean(-1, keepdims=True)
        var = ((o - mu) ** 2).mean(-1, keepdims=True)
        o_flat = ((o - mu) * jax.lax.rsqrt(var + EPS)).reshape(Bn, Tn, C) * gn_weight + gn_bias
        bonus = ((rh * kh * r_k).sum(-1, keepdims=True) * vh).reshape(Bn, Tn, C)
        o_flat = o_flat + bonus
        return o_flat * g @ W_o

    def _L1_xattn_ref(x1, x2, Wq, bq, Wk, bk, Wv, bv):
        import jax, jax.numpy as jnp
        import numpy as np
        DIM = 256
        q = jnp.einsum('bsd,ed->bse', x1, Wq) + bq
        k = jnp.einsum('bsd,ed->bse', x2, Wk) + bk
        v = jnp.einsum('bsd,ed->bse', x2, Wv) + bv
        scale = jnp.asarray(q.shape[-1], q.dtype) ** (-0.5)
        attn = jnp.einsum('bqd,bkd->bqk', q, k) * scale
        attn = jax.nn.softmax(attn, axis=-1)
        return jnp.einsum('bqk,bkd->bqd', attn, v)

    def _L1_ffn_ref(x, gate_w, eg, eu, ed, sg, su, sd):
        import jax, jax.numpy as jnp
        import numpy as np
        B, S, H, I, E, K = (4, 512, 256, 688, 4, 2)
        xf = x.reshape(-1, x.shape[-1])
        scores = jax.nn.softmax(xf @ gate_w.T, axis=-1)
        topk_w, topk_idx = jax.lax.top_k(scores, K)
        topk_w = topk_w / (topk_w.sum(axis=-1, keepdims=True) + 1e-20)
        comb = jnp.sum(jax.nn.one_hot(topk_idx, E, dtype=x.dtype) * topk_w[..., None], axis=1)
        g = jax.nn.silu(jnp.einsum('nh,eih->eni', xf, eg))
        u = jnp.einsum('nh,eih->eni', xf, eu)
        y_exp = jnp.einsum('eni,ehi->enh', g * u, ed)
        y = jnp.einsum('enh,ne->nh', y_exp, comb)
        y = y + jax.nn.silu(xf @ sg.T) * (xf @ su.T) @ sd.T
        return y.reshape(x.shape)
    x = _layernorm(x + _L0_attn_ref(x, L0_attn_W_in, L0_attn_b_in, L0_attn_W_lam, L0_attn_b_lam, L0_attn_W_gate, L0_attn_b_gate, L0_attn_W_out, L0_attn_b_out, L0_attn_gamma, L0_attn_beta), axis=-1)
    x = _layernorm(x + _L0_xattn_ref(x, ctx_1024, L0_xattn_W_ih, L0_xattn_W_hh, L0_xattn_b_ih, L0_xattn_b_hh, L0_xattn_Wq, L0_xattn_Wout, L0_xattn_b_out), axis=-1)
    x = _layernorm(x + _L0_ffn_ref(x, L0_ffn_router_w, L0_ffn_router_b, L0_ffn_we_gate, L0_ffn_we_up, L0_ffn_we_down), axis=-1)
    x = _layernorm(x + _L1_attn_ref(x, L1_attn_x_r, L1_attn_x_w, L1_attn_x_k, L1_attn_x_v, L1_attn_x_a, L1_attn_x_g, L1_attn_k_k, L1_attn_k_a, L1_attn_r_k, L1_attn_W_r, L1_attn_W_k, L1_attn_W_v, L1_attn_W_o, L1_attn_w_lora_a, L1_attn_w_lora_b, L1_attn_w_lora_bias, L1_attn_a_lora_a, L1_attn_a_lora_b, L1_attn_a_lora_bias, L1_attn_g_lora_a, L1_attn_g_lora_b, L1_attn_g_lora_bias, L1_attn_gn_weight, L1_attn_gn_bias), axis=-1)
    x = _layernorm(x + _L1_xattn_ref(x, ctx_1024, L1_xattn_Wq, L1_xattn_bq, L1_xattn_Wk, L1_xattn_bk, L1_xattn_Wv, L1_xattn_bv), axis=-1)
    x = _layernorm(x + _L1_ffn_ref(x, L1_ffn_gate_w, L1_ffn_eg, L1_ffn_eu, L1_ffn_ed, L1_ffn_sg, L1_ffn_su, L1_ffn_sd), axis=-1)
    return x

_drawn_inputs = setup_inputs


def setup_inputs(seed=0):
    import zlib

    import numpy as np

    out = dict(_drawn_inputs(seed))
    spreads = {'L0_attn_gamma': (1.0, 0.2),
     'L0_attn_beta': (0.0, 0.1),
     'L0_xattn_b_ih': (0.0, 0.1),
     'L0_xattn_b_hh': (0.0, 0.1),
     'L0_xattn_b_out': (0.0, 0.1),
     'L0_ffn_router_b': (0.0, 0.1),
     'L1_attn_a_lora_bias': (0.0, 2.0),
     'L1_attn_g_lora_bias': (0.0, 0.1),
     'L1_attn_gn_weight': (1.0, 0.6),
     'L1_attn_gn_bias': (0.0, 0.547),
     'L1_xattn_bq': (0.0, 0.1),
     'L1_xattn_bk': (0.0, 2.0),
     'L1_xattn_bv': (0.0, 0.1)}
    factors = {'L0_attn_b_lam': 2.87,
     'L1_attn_x_w': 8.0,
     'L1_attn_x_a': 8.0,
     'L1_attn_k_k': 2.928,
     'L1_attn_r_k': 39.076,
     'L1_attn_w_lora_a': 8.0,
     'L1_attn_w_lora_b': 8.0,
     'L1_attn_w_lora_bias': 8.0,
     'L1_attn_a_lora_a': 8.0,
     'L1_attn_a_lora_b': 8.0,
     'L1_attn_g_lora_a': 8.0}
    for name, (base, spread) in spreads.items():
        noise = np.random.default_rng([zlib.crc32(name.encode()), seed]).standard_normal(out[name].shape)
        drawn = base * np.exp(spread * noise) if base else spread * noise
        out[name] = jnp.asarray(drawn.astype(out[name].dtype))
    for name, factor in factors.items():
        out[name] = (out[name] * factor).astype(out[name].dtype)
    return out
```

```python
import math
from contextlib import ExitStack

import numpy as np

import concourse.bass as bass
from concourse import mybir

F32 = mybir.dt.float32
ALU = mybir.AluOpType
ACT = mybir.ActivationFunctionType
AX_X = mybir.AxisListType.X

P = 128
BATCH, SEQ, DIM = 4, 512, 256
KC = DIM // P
TOK = BATCH * SEQ
NB = 512
BLOCKS = TOK // NB
SHIFT = BATCH
LN_EPS = 1e-5


class Scope:

    def __init__(self, nc):
        self.nc = nc
        self.stack = ExitStack()
        self.running = ExitStack()
        self.sems = []

    def __enter__(self):
        return self

    def __exit__(self, *exc):
        self.running.close()
        if self.sems:
            numbers = sorted(x.num for x in self.sems)
            with self.nc.Block() as block:
                @block.sync
                def _(sp):
                    first = numbers[0]
                    for n, after in zip(numbers, [*numbers[1:], None]):
                        if after != n + 1:
                            sp.sem_clear(range(first, n + 1))
                            first = after
        return self.stack.__exit__(*exc)

    def sb(self, name, shape):
        return self.stack.enter_context(self.nc.sbuf_tensor(name, shape, F32))

    def ps(self, name, shape):
        return self.stack.enter_context(self.nc.psum_tensor(name, shape, F32))

    def sem(self, name):
        self.sems.append(self.stack.enter_context(self.nc.semaphore(name)))
        return self.sems[-1]

    def block(self):
        return self.running.enter_context(self.nc.Block())


def over_chunks(ap, n=KC):
    return ap.unsqueeze(1).to_broadcast([ap.shape[0], n, ap.shape[1]])


class LayerNorm:

    def __init__(self, s, name, mean_ps, var_ps, width=NB):
        self.mean_ps, self.var_ps = mean_ps, var_ps
        self.d = s.sb(f"{name}_d", [P, KC, width])
        self.sq = s.sb(f"{name}_sq", [P, KC, width])
        self.rstd = s.sb(f"{name}_rstd", [P, width])
        self.y_ready = s.sem(f"{name}_y_ready")
        self.mean_ready = s.sem(f"{name}_mean_ready")
        self.d_ready = s.sem(f"{name}_d_ready")
        self.sq_ready = s.sem(f"{name}_sq_ready")
        self.var_ready = s.sem(f"{name}_var_ready")
        self.std_ready = s.sem(f"{name}_std_ready")
        self.rstd_ready = s.sem(f"{name}_rstd_ready")

    def tensor(self, pe, n, y, ones):
        pe.wait_ge(self.y_ready, n + 1)
        for k in range(KC):
            mm = pe.matmul(self.mean_ps, ones, y(k), start=(k == 0), stop=(k == KC - 1))
        mm.then_inc(self.mean_ready, 1)
        pe.wait_ge(self.sq_ready, n + 1)
        for k in range(KC):
            mm = pe.matmul(self.var_ps, ones, self.sq[:, k, :], start=(k == 0), stop=(k == KC - 1))
        mm.then_inc(self.var_ready, 1)

    def scalar(self, act, n, eps):
        act.wait_ge(self.d_ready, n + 1)
        act.activation(self.sq[:, :, :], self.d[:, :, :], ACT.Square).then_inc(self.sq_ready, 1)
        act.wait_ge(self.var_ready, n + 1)
        act.activation(self.rstd[:, :], self.var_ps, ACT.Sqrt, bias=eps).then_inc(self.std_ready, 1)

    def vector(self, dve, n, y, out):
        dve.wait_ge(self.mean_ready, n + 1)
        dve.tensor_tensor(self.d[:, :, :], y, over_chunks(self.mean_ps), ALU.subtract)\
           .then_inc(self.d_ready, 1)
        dve.wait_ge(self.std_ready, n + 1)
        dve.reciprocal(self.rstd[:, :], self.rstd[:, :]).then_inc(self.rstd_ready, 1)
        dve.wait_ge(self.rstd_ready, n + 1)
        return dve.tensor_tensor(out, self.d[:, :, :], over_chunks(self.rstd[:, :]), ALU.mult)


def recurrence_phase(nc, d, g):
    with Scope(nc) as s:
        w = {m: s.sb(f"rec_w_{m}", [P, KC, DIM]) for m in ("in", "gate", "lam", "out")}
        b = {m: s.sb(f"rec_b_{m}", [P, KC]) for m in ("in", "gate", "lam", "out")}
        gamma = s.sb("rec_gamma", [P, KC])
        beta = s.sb("rec_beta", [P, KC])
        inp = s.sb("rec_inp", [P, KC, NB])
        gate = s.sb("rec_gate", [P, KC, NB])
        lam = s.sb("rec_lam", [P, KC, NB])
        neg_u = s.sb("rec_neg_u", [P, KC, NB])
        hid = s.sb("rec_hid", [P, KC, NB])
        hn = s.sb("rec_hn", [P, KC, NB])
        hg = s.sb("rec_hg", [P, KC, NB])
        y = s.sb("rec_y", [P, KC, NB])
        proj_ps = {m: s.ps(f"rec_ps_{m}", [P, KC, NB]) for m in ("in", "gate", "lam")}
        stat_ps = s.ps("rec_stat_ps", [P, 2, NB])
        out_ps = proj_ps["in"]
        loaded = s.sem("rec_loaded")
        proj = s.sem("rec_proj")
        act_done = s.sem("rec_act_done")
        neg_u_done = s.sem("rec_neg_u_done")
        lam_zeroed = s.sem("rec_lam_zeroed")
        affine = s.sem("rec_affine")
        hg_ready = s.sem("rec_hg_ready")
        out_ready = s.sem("rec_out_ready")
        x_done = s.sem("rec_x_done")
        ln_h = LayerNorm(s, "rec_lnh", stat_ps[:, 0, :], stat_ps[:, 1, :])
        ln_y = LayerNorm(s, "rec_lny", stat_ps[:, 0, :], stat_ps[:, 1, :])
        LOADS = 12
        block = s.block()

        @block.sync
        def _(sp):
            sp.dma_start(g.xT[:, :, SHIFT:], d["xT"]).then_inc(loaded, 16)
            sp.dma_start(g.ctxT[:, :, :], d["ctxT"]).then_inc(loaded, 16)
            for m in ("in", "gate", "lam", "out"):
                sp.dma_start(w[m][:, :, :], d[f"rec_w_{m}"]).then_inc(loaded, 16)
                sp.dma_start(b[m][:, :], d[f"rec_b_{m}"]).then_inc(loaded, 16)
            sp.dma_start(gamma[:, :], d["rec_gamma"]).then_inc(loaded, 16)
            sp.dma_start(beta[:, :], d["rec_beta"]).then_inc(loaded, 16)

        @block.tensor
        def _(pe):
            pe.wait_ge(loaded, 16 * LOADS)
            pe.wait_ge(g.consts, 1)
            with pe.Fori(0, BLOCKS) as i:
                x_cols = bass.ds(SHIFT + i * NB, NB)
                pe.wait_ge(x_done, i + 1)
                for m in ("in", "gate", "lam"):
                    for o in range(KC):
                        for k in range(KC):
                            mm = pe.matmul(proj_ps[m][:, o, :], w[m][:, k, o * P:(o + 1) * P],
                                           g.xT[:, k, x_cols], start=(k == 0), stop=(k == KC - 1))
                    mm.then_inc(proj, 1)
                ln_h.tensor(pe, i, lambda k: hid[:, k, :], g.mean_mat[:, :])
                pe.wait_ge(hg_ready, i + 1)
                for o in range(KC):
                    for k in range(KC):
                        mm = pe.matmul(out_ps[:, o, :], w["out"][:, k, o * P:(o + 1) * P], hg[:, k, :],
                                       start=(k == 0), stop=(k == KC - 1))
                mm.then_inc(out_ready, 1)
                ln_y.tensor(pe, i, lambda k: y[:, k, :], g.mean_mat[:, :])

        @block.scalar
        def _(act):
            act.wait_ge(loaded, 16 * LOADS)
            act.wait_ge(g.consts, 2)
            with act.Fori(0, BLOCKS) as i:
                act.wait_ge(x_done, i + 1)
                for n, (m, dst, f) in enumerate((("in", inp, ACT.Silu), ("gate", gate, ACT.Silu),
                                                 ("lam", lam, ACT.Sigmoid))):
                    act.wait_ge(proj, 3 * i + n + 1)
                    for o in range(KC):
                        a = act.activation(dst[:, o, :], proj_ps[m][:, o, :], f, bias=b[m][:, o:o + 1])
                    a.then_inc(act_done, 1)
                ln_h.scalar(act, i, g.eps[:, :])
                ln_y.scalar(act, i, g.eps[:, :])

        @block.vector
        def _(dve):
            dve.wait_ge(loaded, 16 * LOADS)
            dve.memset(g.xT[:, :, 0:SHIFT], 0.0)
            dve.sem_inc(x_done, 1)
            with dve.Fori(0, BLOCKS) as i:
                x_cols = bass.ds(SHIFT + i * NB, NB)
                dve.wait_ge(act_done, 3 * i + 3)
                dve.scalar_tensor_tensor(out=neg_u[:, :, :], in0=lam[:, :, :], scalar=1.0, in1=inp[:, :, :],
                                         op0=ALU.subtract, op1=ALU.mult).then_inc(neg_u_done, 1)
                dve.wait_ge(neg_u_done, i + 1)
                dve.memset(lam[:, :, :].rearrange("p k (t b) -> p k t b", b=BATCH)[:, :, :, 0:1], 0.0)\
                   .then_inc(lam_zeroed, 1)
                dve.wait_ge(lam_zeroed, i + 1)
                dve.tensor_tensor_scan(hid[:, :, :].rearrange("p k n -> p (k n)"),
                                       lam[:, :, :].rearrange("p k n -> p (k n)"),
                                       neg_u[:, :, :].rearrange("p k n -> p (k n)"),
                                       0.0, ALU.mult, ALU.subtract).then_inc(ln_h.y_ready, 1)
                ln_h.vector(dve, i, hid[:, :, :], hn[:, :, :]).then_inc(affine, 1)
                dve.wait_ge(affine, 2 * i + 1)
                for o in range(KC):
                    a = dve.tensor_scalar(hn[:, o, :], hn[:, o, :], gamma[:, o:o + 1], beta[:, o:o + 1],
                                          ALU.mult, ALU.add)
                a.then_inc(affine, 1)
                dve.wait_ge(affine, 2 * i + 2)
                dve.tensor_tensor(hg[:, :, :], hn[:, :, :], gate[:, :, :], ALU.mult).then_inc(hg_ready, 1)
                dve.wait_ge(out_ready, i + 1)
                for o in range(KC):
                    a = dve.scalar_tensor_tensor(out=y[:, o, :], in0=out_ps[:, o, :], scalar=b["out"][:, o:o + 1],
                                                 in1=g.xT[:, o, x_cols], op0=ALU.add, op1=ALU.add)
                a.then_inc(ln_y.y_ready, 1)
                ln_y.vector(dve, i, y[:, :, :], g.xT[:, :, x_cols]).then_inc(x_done, 1)

        @block.gpsimd
        def _(pool):
            pool.memset(g.mean_mat[:, :], 1.0 / DIM).then_inc(g.consts, 1)
            pool.memset(g.eps[:, :], LN_EPS).then_inc(g.consts, 1)


HID = 256
GATES = 4
SRC = 512
SC = SRC // P
QUARTERS = 4
QW = HID // QUARTERS
STRIP = P // BATCH
UNROLL = 4
TILES = TOK // P
GATE_W = GATES * HID
XROWS = TOK + UNROLL * BATCH


def quarters(ap):
    return ap.rearrange("p (j c) -> p j c", j=QUARTERS)


def attention_lstm_phase(nc, d, g):
    xg_dram = nc.dram_tensor("xg_rows", [XROWS, GATE_W], F32, kind="Internal").ap()
    with Scope(nc) as s:
        w_attn = s.sb("lstm_w_attn", [P, KC, GATE_W])
        w_hid = s.sb("lstm_w_hid", [P, KC, GATE_W])
        w_out_h = s.sb("lstm_w_out_h", [P, KC, DIM])
        keys = s.sb("lstm_keys", [P, KC, TOK])
        values = s.sb("lstm_values", [P, BATCH * SC, DIM])
        sel_quarter = s.sb("lstm_sel_quarter", [P, 2, KC * BATCH])
        sel_batch = s.sb("lstm_sel_batch", [P, BATCH])
        ident = s.sb("lstm_ident", [P, BATCH])

        with Scope(nc) as q:
            w_x = q.sb("lstm_w_x", [P, KC, GATE_W])
            w_q = q.sb("lstm_w_q", [P, KC, HID])
            w_out_c = q.sb("lstm_w_out_c", [P, KC, DIM])
            b_out = q.sb("lstm_b_out", [P, DIM])
            b_x = q.sb("lstm_b_x", [P, GATE_W])
            b_h = q.sb("lstm_b_h", [P, GATE_W])
            x_tile = q.sb("lstm_x_tile", [P, 2, KC, P])
            xg_tile = q.sb("lstm_xg_tile", [P, 2, GATE_W])
            big_ps = q.ps("lstm_big_ps", [P, 2, NB])
            xg_ps = q.ps("lstm_xg_ps", [P, 2, GATE_W])
            loaded = q.sem("lstm_loaded")
            scaled = q.sem("lstm_scaled")
            bias_sum = q.sem("lstm_bias_sum")
            kv_ready = q.sem("lstm_kv_ready")
            keys_read = q.sem("lstm_keys_read")
            values_read = q.sem("lstm_values_read")
            x_copied = q.sem("lstm_x_copied")
            xg_ready = q.sem("lstm_xg_ready")
            xg_read = q.sem("lstm_xg_read")
            xg_stored = [q.sem(f"lstm_xg_stored{n}") for n in range(2)]
            bias_stored = q.sem("lstm_bias_stored")
            KV = KC * BATCH + BATCH * SC
            block = q.block()

            @block.sync
            def _(sp):
                loads = [(w_q[:, :, :], d["lstm_w_q"]), (w_out_c[:, :, :], d["lstm_w_out_c"]),
                         (b_out[:, :], d["lstm_b_out"].partition_broadcast(P)),
                         (b_x[:, :], d["lstm_b_ih"].partition_broadcast(P)),
                         (b_h[:, :], d["lstm_b_hh"].partition_broadcast(P)),
                         (w_x[:, :, :], d["lstm_w_x"]), (w_attn[:, :, :], d["lstm_w_attn"]),
                         (w_hid[:, :, :], d["lstm_w_hid"]), (w_out_h[:, :, :], d["lstm_w_out_h"]),
                         (sel_quarter[:, :, :], d["sel_quarter"]), (sel_batch[:, :], d["sel_batch"]),
                         (ident[:, :], d["ident"][:, 0:BATCH])]
                for dst, src in loads:
                    sp.dma_start(dst, src).then_inc(loaded, 16)
                assert len(loads) == 12
                sp.wait_ge(bias_sum, 2)
                sp.dma_start(xg_dram[TOK:XROWS, :], b_x[0:XROWS - TOK, :]).then_inc(bias_stored, 16)
                for u in range(2):
                    sp.sem_inc(xg_stored[u], 16)
                with sp.Fori(0, TILES // 2) as i:
                    for u in range(2):
                        sp.wait_ge(xg_read, 2 * i + u + 3)
                        sp.dma_start(xg_dram[bass.ds((2 * i + u) * P, P), :], xg_tile[:, u, :])\
                          .then_inc(xg_stored[u], 16)
                for u in range(2):
                    sp.wait_ge(xg_stored[u], 16 * (TILES // 2 + 1))
                sp.wait_ge(bias_stored, 16)

            @block.tensor
            def _(pe):
                pe.wait_ge(loaded, 16 * 12)
                n = 0
                for o in range(KC):
                    for b in range(BATCH):
                        if n >= 2:
                            pe.wait_ge(keys_read, n - 1)
                        for k in range(KC):
                            mm = pe.matmul(big_ps[:, n % 2, :], w_q[:, k, o * P:(o + 1) * P],
                                           g.ctxT[:, k, b * SRC:(b + 1) * SRC], start=(k == 0), stop=(k == KC - 1))
                        mm.then_inc(kv_ready, 1)
                        n += 1
                for c in range(BATCH * SC):
                    if c < 2:
                        pe.wait_ge(keys_read, n - 1)
                    else:
                        pe.wait_ge(values_read, c - 1)
                    for k in range(KC):
                        mm = pe.matmul(big_ps[:, n % 2, 0:DIM], g.ctxT[:, k, c * P:(c + 1) * P], w_out_c[:, k, :],
                                       start=(k == 0), stop=(k == KC - 1))
                    mm.then_inc(kv_ready, 1)
                    n += 1
                pe.wait_ge(scaled, 1)
                pe.sem_inc(xg_ready, 2)
                with pe.Fori(0, TILES // 2) as i:
                    for u in range(2):
                        pe.wait_ge(x_copied, 2 * i + u + 1)
                        pe.wait_ge(xg_read, 2 * i + 2)
                        for half in range(2):
                            for k in range(KC):
                                mm = pe.matmul(xg_ps[:, u, half * NB:(half + 1) * NB], x_tile[:, u, k, :],
                                               w_x[:, k, half * NB:(half + 1) * NB],
                                               start=(k == 0), stop=(k == KC - 1))
                        mm.then_inc(xg_ready, 1)

            @block.scalar
            def _(act):
                for n in range(KC * BATCH):
                    o, b = n // BATCH, n % BATCH
                    act.wait_ge(kv_ready, n + 1)
                    act.mul(keys[:, o, b * SRC:(b + 1) * SRC], big_ps[:, n % 2, :], 0.5).then_inc(keys_read, 1)

            @block.gpsimd
            def _(pool):
                with pool.Fori(0, TILES // 2) as i:
                    for u in range(2):
                        pool.wait_ge(xg_ready, 2 * i + 2)
                        pool.tensor_copy(x_tile[:, u, :, :], g.xT[:, :, bass.ds(SHIFT + (2 * i + u) * P, P)])\
                            .then_inc(x_copied, 1)

            @block.vector
            def _(dve):
                dve.wait_ge(loaded, 16 * 12)
                dve.tensor_tensor(b_x[:, :], b_x[:, :], b_h[:, :], ALU.add).then_inc(bias_sum, 1)
                for w, f in ((w_x, 0.5), (w_attn, 0.5), (w_hid, 0.25)):
                    for k in range(KC):
                        cols = quarters(w[:, k, :])[:, :, 0:3 * QW]
                        dve.tensor_scalar(cols, cols, f, None, ALU.mult)
                for k in range(KC):
                    cols = quarters(w_hid[:, k, :])[:, :, 3 * QW:]
                    dve.tensor_scalar(cols, cols, 0.5, None, ALU.mult)
                dve.tensor_scalar(w_out_h[:, :, :], w_out_h[:, :, :], 0.5, None, ALU.mult).then_inc(scaled, 1)
                dve.wait_ge(bias_sum, 1)
                cols = quarters(b_x[:, :])[:, :, 0:3 * QW]
                dve.tensor_scalar(cols, cols, 0.5, None, ALU.mult).then_inc(bias_sum, 1)
                for c in range(BATCH * SC):
                    n = KC * BATCH + c
                    dve.wait_ge(kv_ready, n + 1)
                    dve.tensor_tensor(values[:, c, :], big_ps[:, n % 2, 0:DIM], b_out[:, :], ALU.add).then_inc(values_read, 1)
                dve.wait_ge(bias_sum, 2)
                dve.sem_inc(xg_read, 2)
                with dve.Fori(0, TILES // 2) as i:
                    for u in range(2):
                        dve.wait_ge(xg_ready, 2 * i + u + 3)
                        dve.wait_ge(xg_stored[u], 16 * (i + 1))
                        dve.tensor_tensor(xg_tile[:, u, :], xg_ps[:, u, :], b_x[:, :], ALU.add).then_inc(xg_read, 1)

        with Scope(nc) as q:
            xg = q.sb("lstm_xg", [P, UNROLL, GATE_W])
            attn = q.sb("lstm_attn", [P, KC, BATCH])
            hid = q.sb("lstm_hid", [P, KC, BATCH])
            cell = q.sb("lstm_cell", [P, GATES + 1, QW])
            uv = q.sb("lstm_uv", [P, 2, QW])
            tanh_c = q.sb("lstm_tanh_c", [P, QW])
            h_row = q.sb("lstm_h_row", [P, QW])
            neg_max = q.sb("lstm_neg_max", [P, 1])
            expo = q.sb("lstm_expo", [P, SRC])
            total = q.sb("lstm_total", [P, 2])
            total_sum = q.sb("lstm_total_sum", [P, 1])
            inverse = q.sb("lstm_inverse", [P, 1])
            alpha = q.sb("lstm_alpha", [P, SC, BATCH])
            out_row = q.sb("lstm_out_row", [P, DIM])
            gate_ps = q.ps("lstm_gate_ps", [P, 2, NB])
            turn_ps = q.ps("lstm_turn_ps", [P, KC, NB])
            h_ps = turn_ps[:, 0, 0:KC * BATCH]
            attn_ps = turn_ps[:, :, KC * BATCH:(KC + 1) * BATCH]
            score_ps = q.ps("lstm_score_ps", [P, SRC])
            alpha_ps = q.ps("lstm_alpha_ps", [P, 2, NB])
            out_ps = q.ps("lstm_out_ps", [P, NB])
            xg_zeroed = q.sem("lstm_xg_zeroed")
            zeroed = q.sem("lstm_zeroed")
            xg_loaded = [q.sem(f"lstm_xg_loaded{n}") for n in range(UNROLL)]
            xg_used = q.sem("lstm_xg_used")
            gates_ready = q.sem("lstm_gates_ready")
            gates_tanh = q.sem("lstm_gates_tanh")
            uv_ready = q.sem("lstm_uv_ready")
            c_ready = q.sem("lstm_c_ready")
            c_tanh = q.sem("lstm_c_tanh")
            h_row_ready = q.sem("lstm_h_row_ready")
            h_turned = q.sem("lstm_h_turned")
            h_ready = q.sem("lstm_h_ready")
            scores_ready = q.sem("lstm_scores_ready")
            max_ready = q.sem("lstm_max_ready")
            exp_ready = q.sem("lstm_exp_ready")
            half_summed = q.sem("lstm_half_summed")
            total_ready = q.sem("lstm_total_ready")
            inverse_ready = q.sem("lstm_inverse_ready")
            alpha_turned = q.sem("lstm_alpha_turned")
            alpha_ready = q.sem("lstm_alpha_ready")
            out_ready = q.sem("lstm_out_ready")
            out_row_ready = q.sem("lstm_out_row_ready")
            attn_turned = q.sem("lstm_attn_turned")
            attn_ready = q.sem("lstm_attn_ready")
            attn_kept = q.sem("lstm_attn_kept")
            block = q.block()
            HALF_SRC = SRC // 2

            def x_rows(t):
                return xg_dram[bass.ds(t * BATCH, BATCH), :]

            @block.sync
            def _(sp):
                sp.wait_ge(xg_zeroed, 1)
                for u in range(UNROLL):
                    sp.dma_start(xg[0:BATCH, u, :], x_rows(u)).then_inc(xg_loaded[u], 16)
                with sp.Fori(0, SEQ // UNROLL) as i:
                    for u in range(UNROLL):
                        t = i * UNROLL + u
                        sp.wait_ge(xg_used, t + 1)
                        sp.dma_start(xg[0:BATCH, u, :], x_rows(t + UNROLL)).then_inc(xg_loaded[u], 16)
                for u in range(UNROLL):
                    sp.wait_ge(xg_loaded[u], 16 * (SEQ // UNROLL + 1))

            @block.tensor
            def _(pe):
                def quarter(u, j):
                    return gate_ps[j * STRIP:j * STRIP + BATCH, u % 2, 0:HID]

                def x_part(u):
                    for j in range(QUARTERS):
                        mm = pe.matmul(quarter(u, j), ident[:, :], xg[:, u % UNROLL, j * HID:(j + 1) * HID],
                                       start=True, stop=False)
                    mm.then_inc(xg_used, 1)

                def gate_part(u, w, col, k, last):
                    for j in range(QUARTERS):
                        mm = pe.matmul(quarter(u, j), col[:, k, :], w[:, k, j * HID:(j + 1) * HID],
                                       start=False, stop=last)
                    return mm

                def batch_rows(ps, n, b):
                    return ps[b * STRIP:b * STRIP + 1, 0:n]

                pe.wait_ge(zeroed, 1)
                pe.wait_ge(xg_loaded[0], 16)
                x_part(0)
                for k in range(KC):
                    gate_part(0, w_hid, hid, k, False)
                with pe.Fori(0, SEQ // UNROLL) as i:
                    for u in range(UNROLL):
                        t = i * UNROLL + u
                        pe.wait_ge(attn_ready, t + 1)
                        gate_part(u, w_attn, attn, 0, False)
                        gate_part(u, w_attn, attn, 1, True).then_inc(gates_ready, 1)
                        nxt = (u + 1) % UNROLL
                        pe.wait_ge(xg_loaded[nxt], 16 * (i + (2 if nxt == 0 else 1)))
                        x_part(u + 1)
                        pe.wait_ge(h_row_ready, t + 1)
                        for half in range(2):
                            mm = pe.matmul(h_ps[half * QW:(half + 1) * QW, :], h_row[:, :], sel_quarter[:, half, :], start=True, stop=True)
                        mm.then_inc(h_turned, 1)
                        pe.wait_ge(h_ready, t + 1)
                        for k in range(KC):
                            for b in range(BATCH):
                                mm = pe.matmul(batch_rows(score_ps, SRC, b), hid[:, k, b:b + 1],
                                               keys[:, k, b * SRC:(b + 1) * SRC], start=(k == 0), stop=(k == KC - 1))
                        mm.then_inc(scores_ready, 1)
                        for o in range(KC):
                            for k in range(KC):
                                pe.matmul(attn_ps[:, o, :], w_out_h[:, k, o * P:(o + 1) * P], hid[:, k, :],
                                          start=(k == 0), stop=False)
                        gate_part(u + 1, w_hid, hid, 0, False)
                        for half in range(2):
                            pe.wait_ge(exp_ready, 2 * t + half + 1)
                            for c in range(2):
                                lo = half * HALF_SRC + c * P
                                mm = pe.matmul(alpha_ps[:, half, c * BATCH:(c + 1) * BATCH], expo[:, lo:lo + P],
                                               sel_batch[:, :], start=True, stop=True)
                            mm.then_inc(alpha_turned, 1)
                        for half in range(2):
                            pe.wait_ge(alpha_ready, 2 * t + half + 1)
                            for c in (2 * half, 2 * half + 1):
                                for b in range(BATCH):
                                    mm = pe.matmul(batch_rows(out_ps, DIM, b), alpha[:, c, b:b + 1],
                                                   values[:, b * SC + c, :], start=(c == 0), stop=(c == SC - 1))
                        mm.then_inc(out_ready, 1)
                        gate_part(u + 1, w_hid, hid, 1, False)
                        for o in range(KC):
                            pe.wait_ge(out_row_ready, 2 * t + o + 1)
                            mm = pe.matmul(attn_ps[:, o, :], out_row[:, o * P:(o + 1) * P], sel_batch[:, :],
                                           start=False, stop=True)
                        mm.then_inc(attn_turned, 1)
                pe.wait_ge(attn_ready, SEQ + 1)
                for k in range(KC):
                    gate_part(SEQ, w_attn, attn, k, k == KC - 1)

            @block.scalar
            def _(act):
                act.wait_ge(zeroed, 1)
                act.sem_inc(attn_ready, 1)
                with act.Fori(0, SEQ // UNROLL) as i:
                    for u in range(UNROLL):
                        t = i * UNROLL + u
                        act.wait_ge(gates_ready, t + 1)
                        for lo, hi in ((1, GATES), (0, 1)):
                            act.activation(cell[:, lo:hi, :].rearrange("p n q -> p (n q)"),
                                           gate_ps[:, u % 2, lo * QW:hi * QW], ACT.Tanh).then_inc(gates_tanh, 1)
                        act.wait_ge(c_ready, t + 1)
                        act.activation(tanh_c[:, :], cell[:, GATES, :], ACT.Tanh, scale=0.5).then_inc(c_tanh, 1)
                        act.wait_ge(max_ready, t + 1)
                        act.activation(expo[:, 0:HALF_SRC], score_ps[:, 0:HALF_SRC], ACT.Exp, bias=neg_max[:, :])\
                           .then_inc(exp_ready, 1)
                        act.activation(expo[:, HALF_SRC:], score_ps[:, HALF_SRC:], ACT.Exp, bias=neg_max[:, :],
                                       accum_out=total[:, 1:2]).then_inc(exp_ready, 1)
                        act.wait_ge(attn_turned, t + 1)
                        act.wait_ge(attn_kept, t + 1)
                        act.activation(attn[:, :, :], attn_ps, ACT.Tanh).then_inc(attn_ready, 1)

            @block.vector
            def _(dve):
                for ps in (gate_ps[:, 0, :], gate_ps[:, 1, :], score_ps[:, :], out_ps[:, :]):
                    dve.memset(ps, 0.0)
                dve.memset(cell[:, :, :], 0.0)
                dve.memset(hid[:, :, :], 0.0)
                dve.memset(attn[:, :, :], 0.0).then_inc(zeroed, 1)
                with dve.Fori(0, SEQ // UNROLL) as i:
                    for u in range(UNROLL):
                        t = i * UNROLL + u
                        dve.wait_ge(gates_tanh, 2 * t + 1)
                        dve.scalar_tensor_tensor(out=uv[:, :, :], in0=cell[:, 1:3, :], scalar=1.0,
                                                 in1=cell[:, 3:5, :], op0=ALU.add, op1=ALU.mult).then_inc(uv_ready, 1)
                        dve.wait_ge(uv_ready, t + 1)
                        dve.scalar_tensor_tensor(out=cell[:, GATES, :], in0=uv[:, 1, :], scalar=0.5,
                                                 in1=uv[:, 0, :], op0=ALU.mult, op1=ALU.add).then_inc(c_ready, 1)
                        dve.wait_ge(c_tanh, t + 1)
                        dve.scalar_tensor_tensor(out=h_row[:, :], in0=cell[:, 0, :], scalar=1.0,
                                                 in1=tanh_c[:, :], op0=ALU.add, op1=ALU.mult).then_inc(h_row_ready, 1)
                        dve.wait_ge(h_turned, t + 1)
                        dve.tensor_copy(hid[:, :, :].rearrange("p k b -> p (k b)"), h_ps).then_inc(h_ready, 1)
                        dve.wait_ge(scores_ready, t + 1)
                        dve.tensor_reduce(neg_max[:, :], score_ps[:, :], AX_X, ALU.max, negate=True).then_inc(max_ready, 1)
                        dve.wait_ge(exp_ready, 2 * t + 1)
                        dve.tensor_reduce(total[:, 0:1], expo[:, 0:HALF_SRC], AX_X, ALU.add).then_inc(half_summed, 1)
                        for half in range(2):
                            dve.wait_ge(alpha_turned, 2 * t + half + 1)
                            dve.tensor_copy(alpha[:, 2 * half:2 * half + 2, :].rearrange("p c b -> p (c b)"),
                                            alpha_ps[:, half, 0:2 * BATCH]).then_inc(alpha_ready, 1)
                        dve.wait_ge(half_summed, t + 1)
                        dve.wait_ge(exp_ready, 2 * t + 2)
                        dve.tensor_tensor(total_sum[:, :], total[:, 0:1], total[:, 1:2], ALU.add).then_inc(total_ready, 1)
                        dve.wait_ge(total_ready, t + 1)
                        dve.reciprocal(inverse[:, :], total_sum[:, :]).then_inc(inverse_ready, 1)
                        dve.wait_ge(inverse_ready, t + 1)
                        dve.wait_ge(out_ready, t + 1)
                        for k in range(KC):
                            cols = slice(k * P, (k + 1) * P)
                            dve.tensor_scalar(out_row[:, cols], out_ps[:, cols], inverse[:, 0:1], None, ALU.mult)\
                               .then_inc(out_row_ready, 1)

            @block.gpsimd
            def _(pool):
                pool.memset(xg[:, :, :], 0.0).then_inc(xg_zeroed, 1)
                pool.sem_inc(attn_kept, 1)
                with pool.Fori(0, SEQ // UNROLL) as i:
                    for u in range(UNROLL):
                        t = i * UNROLL + u
                        cols = g.xT[:, :, bass.ds(SHIFT + t * BATCH, BATCH)]
                        pool.wait_ge(attn_ready, t + 2)
                        pool.tensor_tensor(cols, cols, attn[:, :, :], ALU.add).then_inc(attn_kept, 1)


def norm_phase(nc, g, name):
    with Scope(nc) as s:
        stat_ps = s.ps(f"{name}_stat_ps", [P, 2, NB])
        ln = LayerNorm(s, name, stat_ps[:, 0, :], stat_ps[:, 1, :])
        x_done = s.sem(f"{name}_x_done")
        block = s.block()

        def x_cols(i):
            return g.xT[:, :, bass.ds(SHIFT + i * NB, NB)]

        @block.tensor
        def _(pe):
            with pe.Fori(0, BLOCKS) as i:
                ln.tensor(pe, i, lambda k: g.xT[:, k, bass.ds(SHIFT + i * NB, NB)], g.mean_mat[:, :])

        @block.scalar
        def _(act):
            with act.Fori(0, BLOCKS) as i:
                ln.scalar(act, i, g.eps[:, :])

        @block.vector
        def _(dve):
            dve.sem_inc(ln.y_ready, BLOCKS)
            dve.sem_inc(x_done, 1)
            with dve.Fori(0, BLOCKS) as i:
                dve.wait_ge(x_done, i + 1)
                ln.vector(dve, i, x_cols(i), x_cols(i)).then_inc(x_done, 1)


EXPERTS0 = 8
TOP = 2
TB = NB // P


class Router:

    def __init__(self, s, name, experts, softmax_first, rows_ps, cols_ps):
        E = self.n = experts
        self.softmax_first = softmax_first
        self.rows_ps, self.cols_ps = rows_ps, cols_ps
        self.logit_rows = s.sb(f"{name}_logit_rows", [E, NB])
        self.logits = s.sb(f"{name}_logits", [P, TB, E])
        self.expo = s.sb(f"{name}_expo", [P, TB, E])
        self.above = s.sb(f"{name}_above", [P, TB, E, E])
        self.same = s.sb(f"{name}_same", [P, TB, E, E])
        self.before = s.sb(f"{name}_before", [P, E, E])
        self.rank = s.sb(f"{name}_rank", [P, TB, E])
        self.total = s.sb(f"{name}_total", [P, TB])
        self.weights = s.sb(f"{name}_weights", [P, TB, E])
        self.weight_rows = s.sb(f"{name}_weight_rows", [E, NB])
        self.filled = s.sem(f"{name}_filled")
        self.logit_rows_summed = s.sem(f"{name}_logit_rows_summed")
        self.logit_rows_ready = s.sem(f"{name}_logit_rows_ready")
        self.logits_turned = s.sem(f"{name}_logits_turned")
        self.shifted = s.sem(f"{name}_shifted")
        self.expo_ready = s.sem(f"{name}_expo_ready")
        self.step = s.sem(f"{name}_step")
        self.weights_ready = s.sem(f"{name}_weights_ready")
        self.weights_turned = s.sem(f"{name}_weights_turned")
        self.weight_rows_ready = s.sem(f"{name}_weight_rows_ready")
        self.STEPS = 14 if softmax_first else 10

    def gpsimd(self, pool):
        pool.memset(self.before[:, :, :], 0.0).then_inc(self.filled, 1)
        pool.wait_ge(self.filled, 1)
        for e in range(1, self.n):
            ins = pool.memset(self.before[:, e, 0:e], 1.0)
        ins.then_inc(self.filled, 1)

    def tensor(self, pe, n, w, x, ident):
        for k in range(KC):
            mm = pe.matmul(self.rows_ps, w[:, k, :], x(k), start=(k == 0), stop=(k == KC - 1))
        mm.then_inc(self.logit_rows_summed, 1)
        pe.wait_ge(self.logit_rows_ready, n + 1)
        for c in range(TB):
            mm = pe.matmul(self.cols_ps[:, c, :], self.logit_rows[:, c * P:(c + 1) * P],
                           ident[0:self.n, 0:self.n], start=True, stop=True)
        mm.then_inc(self.logits_turned, 1)
        pe.wait_ge(self.weights_ready, n + 1)
        for c in range(TB):
            mm = pe.matmul(self.rows_ps[:, c * P:(c + 1) * P], self.weights[:, c, :], ident, start=True, stop=True)
        mm.then_inc(self.weights_turned, 1)

    def scalar(self, act, n, bias):
        act.wait_ge(self.logit_rows_summed, n + 1)
        act.activation(self.logit_rows[:, :], self.rows_ps, ACT.Identity, bias=bias).then_inc(self.logit_rows_ready, 1)
        act.wait_ge(self.shifted, n + 1)
        act.activation(self.expo[:, :, :], self.expo[:, :, :], ACT.Exp).then_inc(self.expo_ready, 1)
        act.wait_ge(self.weights_turned, n + 1)
        act.copy(self.weight_rows[:, :], self.rows_ps).then_inc(self.weight_rows_ready, 1)

    def vector(self, dve, n):
        E, at = self.n, [0]

        def then(ins):
            at[0] += 1
            ins.then_inc(self.step, 1)
            dve.wait_ge(self.step, n * self.STEPS + at[0])

        def spread(ap):
            return ap.unsqueeze(2).to_broadcast([P, TB, E])

        def own(ap):
            return ap.unsqueeze(3).to_broadcast([P, TB, E, E])

        def other(ap):
            return ap.unsqueeze(2).to_broadcast([P, TB, E, E])

        dve.wait_ge(self.logits_turned, n + 1)
        then(dve.tensor_copy(self.logits[:, :, :], self.cols_ps))
        then(dve.tensor_reduce(self.total[:, :], self.logits[:, :, :], AX_X, ALU.max))
        dve.tensor_tensor(self.expo[:, :, :], self.logits[:, :, :], spread(self.total[:, :]), ALU.subtract)\
           .then_inc(self.shifted, 1)
        dve.wait_ge(self.expo_ready, n + 1)
        if self.softmax_first:
            then(dve.tensor_reduce(self.total[:, :], self.expo[:, :, :], AX_X, ALU.add))
            then(dve.reciprocal(self.total[:, :], self.total[:, :]))
            then(dve.tensor_tensor(self.expo[:, :, :], self.expo[:, :, :], spread(self.total[:, :]), ALU.mult))
        ranked = self.expo[:, :, :] if self.softmax_first else self.logits[:, :, :]
        dve.tensor_tensor(self.above[:, :, :, :], other(ranked), own(ranked), ALU.is_gt)
        then(dve.tensor_tensor(self.same[:, :, :, :], other(ranked), own(ranked), ALU.is_equal))
        then(dve.tensor_tensor(self.same[:, :, :, :], self.same[:, :, :, :],
                               self.before[:, :, :].unsqueeze(1).to_broadcast([P, TB, E, E]), ALU.mult))
        then(dve.tensor_tensor(self.above[:, :, :, :], self.above[:, :, :, :], self.same[:, :, :, :], ALU.add))
        then(dve.tensor_reduce(self.rank[:, :, :], self.above[:, :, :, :], AX_X, ALU.add))
        then(dve.tensor_scalar(self.rank[:, :, :], self.rank[:, :, :], float(TOP), None, ALU.is_lt))
        then(dve.tensor_tensor(self.weights[:, :, :], self.rank[:, :, :], self.expo[:, :, :], ALU.mult))
        then(dve.tensor_reduce(self.total[:, :], self.weights[:, :, :], AX_X, ALU.add))
        if self.softmax_first:
            then(dve.tensor_scalar(self.total[:, :], self.total[:, :], 1e-20, None, ALU.add))
        then(dve.reciprocal(self.total[:, :], self.total[:, :]))
        dve.tensor_tensor(self.weights[:, :, :], self.weights[:, :, :], spread(self.total[:, :]), ALU.mult)\
           .then_inc(self.weights_ready, 1)
        assert at[0] == self.STEPS


def mixture_phase(nc, d, g):
    E = EXPERTS0
    with Scope(nc) as s:
        w_gate = s.sb("mix_w_gate", [P, E, KC, DIM])
        w_up = s.sb("mix_w_up", [P, E, KC, DIM])
        w_down = s.sb("mix_w_down", [P, E, KC, DIM])
        w_router = s.sb("mix_w_router", [P, KC, E])
        b_router = s.sb("mix_b_router", [E, 1])
        pick = s.sb("mix_pick", [E, E, P])
        ident = s.sb("mix_ident", [P, P])
        act_g = s.sb("mix_act_g", [P, KC, NB])
        act_gu = s.sb("mix_act_gu", [P, 2, KC, NB])
        y = s.sb("mix_y", [P, KC, NB])
        gate_ps = s.ps("mix_gate_ps", [P, KC, NB])
        up_ps = s.ps("mix_up_ps", [P, KC, NB])
        spread_ps = s.ps("mix_spread_ps", [P, NB])
        aux_ps = s.ps("mix_aux_ps", [P, NB])
        down_ps = s.ps("mix_down_ps", [P, KC, NB])
        loaded = s.sem("mix_loaded")
        gate_ready = s.sem("mix_gate_ready")
        up_ready = s.sem("mix_up_ready")
        spread_ready = s.sem("mix_spread_ready")
        silu_ready = s.sem("mix_silu_ready")
        gu_ready = s.sem("mix_gu_ready")
        weighted = s.sem("mix_weighted")
        down_ready = s.sem("mix_down_ready")
        down_used = s.sem("mix_down_used")
        x_done = s.sem("mix_x_done")
        router = Router(s, "mix_router", E, False, aux_ps[0:E, :],
                        spread_ps[:, 0:TB * E].rearrange("p (c e) -> p c e", e=E))
        ln = LayerNorm(s, "mix_ln", aux_ps[:, :], spread_ps[:, :])
        block = s.block()
        LOADS = 4 + 3 * E

        @block.sync
        def _(sp):
            sp.dma_start(w_router[:, :, :], d["mix_w_router"]).then_inc(loaded, 16)
            sp.dma_start(b_router[:, :], d["mix_b_router"]).then_inc(loaded, 16)
            sp.dma_start(pick[:, :, :], d["pick"][0:E, 0:E, :]).then_inc(loaded, 16)
            sp.dma_start(ident[:, :], d["ident"]).then_inc(loaded, 16)
            for e in range(E):
                sp.dma_start(w_gate[:, e, :, :], d["mix_w_gate"][e]).then_inc(loaded, 16)
                sp.dma_start(w_up[:, e, :, :], d["mix_w_up"][e]).then_inc(loaded, 16)
                sp.dma_start(w_down[:, e, :, :], d["mix_w_down"][e]).then_inc(loaded, 16)

        @block.tensor
        def _(pe):
            pe.wait_ge(loaded, 16 * LOADS)

            def down(i, e):
                n = i * E + e
                pe.wait_ge(weighted, n + 1)
                for o in range(KC):
                    for k in range(KC):
                        mm = pe.matmul(down_ps[:, o, :], w_down[:, e, k, o * P:(o + 1) * P], act_gu[:, e % 2, k, :],
                                       start=(e == 0 and k == 0), stop=(e == E - 1 and k == KC - 1))
                if e == E - 1:
                    mm.then_inc(down_ready, 1)

            with pe.Fori(0, BLOCKS) as i:
                x_cols = bass.ds(SHIFT + i * NB, NB)

                def product(ps, w, e):
                    for o in range(KC):
                        for k in range(KC):
                            mm = pe.matmul(ps[:, o, :], w[:, e, k, o * P:(o + 1) * P], g.xT[:, k, x_cols],
                                           start=(k == 0), stop=(k == KC - 1))
                    return mm

                pe.wait_ge(x_done, i + 1)
                router.tensor(pe, i, w_router, lambda k: g.xT[:, k, x_cols], ident[:, :])
                pe.wait_ge(router.weight_rows_ready, i + 1)
                for e in range(E):
                    n = i * E + e
                    if e > 0:
                        pe.wait_ge(silu_ready, n)
                    product(gate_ps, w_gate, e).then_inc(gate_ready, 1)
                    if e > 0:
                        pe.wait_ge(weighted, n)
                    product(up_ps, w_up, e).then_inc(up_ready, 1)
                    pe.matmul(spread_ps[:, :], pick[:, e, :], router.weight_rows[:, :], start=True, stop=True)\
                      .then_inc(spread_ready, 1)
                    if e > 0:
                        down(i, e - 1)
                down(i, E - 1)
                ln.tensor(pe, i, lambda k: y[:, k, :], g.mean_mat[:, :])

        @block.scalar
        def _(act):
            act.wait_ge(loaded, 16 * LOADS)
            with act.Fori(0, BLOCKS) as i:
                router.scalar(act, i, b_router[:, :])
                for e in range(E):
                    n = i * E + e
                    act.wait_ge(gate_ready, n + 1)
                    if e > 0:
                        act.wait_ge(gu_ready, n)
                    act.activation(act_g[:, :, :], gate_ps[:, :, :], ACT.Silu).then_inc(silu_ready, 1)
                ln.scalar(act, i, g.eps[:, :])

        @block.vector
        def _(dve):
            dve.wait_ge(loaded, 16 * LOADS)
            dve.sem_inc(x_done, 1)
            dve.wait_ge(router.filled, 2)
            with dve.Fori(0, BLOCKS) as i:
                x_cols = bass.ds(SHIFT + i * NB, NB)
                router.vector(dve, i)
                for e in range(E):
                    n = i * E + e
                    gu = act_gu[:, e % 2, :, :]
                    dve.wait_ge(silu_ready, n + 1)
                    dve.wait_ge(up_ready, n + 1)
                    dve.tensor_tensor(gu, act_g[:, :, :], up_ps[:, :, :], ALU.mult).then_inc(gu_ready, 1)
                    dve.wait_ge(spread_ready, n + 1)
                    dve.wait_ge(gu_ready, n + 1)
                    dve.tensor_tensor(gu, gu, over_chunks(spread_ps[:, :]), ALU.mult).then_inc(weighted, 1)
                dve.wait_ge(down_ready, i + 1)
                dve.tensor_tensor(y[:, :, :], down_ps[:, :, :], g.xT[:, :, x_cols], ALU.add).then_inc(ln.y_ready, 1)
                ln.vector(dve, i, y[:, :, :], g.xT[:, :, x_cols]).then_inc(x_done, 1)

        @block.gpsimd
        def _(pool):
            router.gpsimd(pool)


HEADS, HD = 16, 16
HALF = HD // 2
LORA = 64
LORA_G = 128
STEPS = P // BATCH
NEG_A, DECAY, B_IN, KEY, RECV, VALUE = range(6)
SCAN_IN = 6
MIXES = 5


def rwkv_phase(nc, d, g):
    scan_dram = nc.dram_tensor("scan_in", [BATCH, HEADS, SCAN_IN, SEQ, HD], F32, kind="Internal").ap()
    o_dram = nc.dram_tensor("scan_out", [TOK, DIM], F32, kind="Internal").ap()
    with Scope(nc) as s:
        gate = s.sb("rw_gate", [P, TILES, DIM])
        bonus = s.sb("rw_bonus", [P, TILES, DIM])
        rwkv_project(nc, d, g, scan_dram, gate, bonus)
        rwkv_scan(nc, g, scan_dram, o_dram)
        rwkv_output(nc, d, g, o_dram, gate, bonus)


def heads(ap):
    return ap.rearrange("p (h j) -> p h j", j=HD)


def per_head(ap):
    return ap.unsqueeze(2).to_broadcast([P, HEADS, HD])


def rwkv_project(nc, d, g, scan_dram, gate, bonus):
    with Scope(nc) as s:
        mix_w = s.sb("rw_mix_w", [P, MIXES, KC])
        w = {m: s.sb(f"rw_w_{m}", [P, KC, DIM]) for m in ("r", "k", "v")}
        wa = {m: s.sb(f"rw_wa_{m}", [P, KC, n]) for m, n in (("w", LORA), ("a", LORA), ("g", LORA_G))}
        wb = {m: s.sb(f"rw_wb_{m}", [n, DIM]) for m, n in (("w", LORA), ("a", LORA), ("g", LORA_G))}
        rows = s.sb("rw_rows", [P, 6, DIM])
        W_BIAS, A_BIAS, G_BIAS, K_K, K_A, R_K = range(6)
        delta = s.sb("rw_delta", [P, KC, P])
        mixed = s.sb("rw_mixed", [P, MIXES, KC, P])
        r_col = s.sb("rw_r_col", [P, KC, P])
        lora_w = s.sb("rw_lora_w", [LORA, P])
        lora_a = s.sb("rw_lora_a", [LORA, P])
        lora_g = s.sb("rw_lora_g", [P, P])
        sig = s.sb("rw_sig", [P, 2, DIM])
        kk = s.sb("rw_kk", [P, DIM])
        sq = s.sb("rw_sq", [P, DIM])
        norm = s.sb("rw_norm", [P, HEADS])
        tmp = s.sb("rw_tmp", [P, DIM])
        rk = s.sb("rw_rk", [P, DIM])
        rk_sum = s.sb("rw_rk_sum", [P, HEADS])
        q = s.sb("rw_q", [P, SCAN_IN, DIM])
        rv_ps = s.ps("rw_rv_ps", [P, 2, DIM])
        k_ps = s.ps("rw_k_ps", [P, NB])
        wa_ps = s.ps("rw_wa_ps", [P, 2, DIM])
        g_ps = s.ps("rw_g_ps", [P, NB])
        col_ps = s.ps("rw_col_ps", [P, 4, P])
        lg_ps = s.ps("rw_lg_ps", [P, NB])
        loaded = s.sem("rw_loaded")
        delta_ready = s.sem("rw_delta_ready")
        mixed_ready = s.sem("rw_mixed_ready")
        cols_ready = s.sem("rw_cols_ready")
        rkv_ready = s.sem("rw_rkv_ready")
        inner_ready = s.sem("rw_inner_ready")
        outer_ready = s.sem("rw_outer_ready")
        lg_ready = s.sem("rw_lg_ready")
        lg_act = s.sem("rw_lg_act")
        g_ready = s.sem("rw_g_ready")
        z_ready = s.sem("rw_z_ready")
        sig_ready = s.sem("rw_sig_ready")
        decay_ready = s.sem("rw_decay_ready")
        rv_ready = s.sem("rw_rv_ready")
        kk_ready = s.sem("rw_kk_ready")
        sq_ready = s.sem("rw_sq_ready")
        ss_ready = s.sem("rw_ss_ready")
        norm_ready = s.sem("rw_norm_ready")
        step = s.sem("rw_step")
        done = s.sem("rw_done")
        stored = s.sem("rw_stored")
        block = s.block()
        LOADS = 1 + 3 + 6 + 6

        @block.sync
        def _(sp):
            sp.dma_start(mix_w[:, :, :], d["rw_mix_w"]).then_inc(loaded, 16)
            for m in ("r", "k", "v"):
                sp.dma_start(w[m][:, :, :], d[f"rw_w_{m}"]).then_inc(loaded, 16)
            for m in ("w", "a", "g"):
                sp.dma_start(wa[m][:, :, :], d[f"rw_wa_{m}"]).then_inc(loaded, 16)
                sp.dma_start(wb[m][:, :], d[f"rw_wb_{m}"]).then_inc(loaded, 16)
            for n, m in enumerate(("w_bias", "a_bias", "g_bias", "k_k", "k_a", "r_k")):
                sp.dma_start(rows[:, n, :], d[f"rw_{m}"].partition_broadcast(P)).then_inc(loaded, 16)
            sp.sem_inc(stored, 16)
            with sp.Fori(0, TILES) as i:
                sp.wait_ge(done, i + 2)
                for b in range(BATCH):
                    for n in range(SCAN_IN):
                        sp.dma_start(scan_dram[b, :, n, bass.ds(i * STEPS, STEPS), :].rearrange("h t j -> t h j"),
                                     heads(q[b:P:BATCH, n, :])).then_inc(stored, 16)
            sp.wait_ge(stored, 16 * (BATCH * SCAN_IN * TILES + 1))

        @block.tensor
        def _(pe):
            pe.wait_ge(loaded, 16 * LOADS)
            with pe.Fori(0, TILES) as i:
                pe.wait_ge(mixed_ready, i + 1)
                pe.wait_ge(done, i + 1)

                def rows_of(out, lhs, rhs):
                    for k in range(KC):
                        mm = pe.matmul(out, lhs(k), rhs(k), start=(k == 0), stop=(k == KC - 1))
                    return mm

                for o in range(KC):
                    rows_of(col_ps[:, o, :], lambda k: w["r"][:, k, o * P:(o + 1) * P], lambda k: mixed[:, 0, k, :])
                rows_of(col_ps[0:LORA, 2, :], lambda k: wa["w"][:, k, :], lambda k: mixed[:, 1, k, :])
                rows_of(col_ps[0:LORA, 3, :], lambda k: wa["a"][:, k, :], lambda k: mixed[:, 4, k, :]).then_inc(cols_ready, 1)
                rows_of(rv_ps[:, 0, :], lambda k: mixed[:, 0, k, :], lambda k: w["r"][:, k, :])
                rows_of(k_ps[:, 0:DIM], lambda k: mixed[:, 2, k, :], lambda k: w["k"][:, k, :])
                rows_of(rv_ps[:, 1, :], lambda k: mixed[:, 3, k, :], lambda k: w["v"][:, k, :]).then_inc(rkv_ready, 1)
                pe.wait_ge(inner_ready, i + 1)
                rows_of(lg_ps[:, 0:P], lambda k: wa["g"][:, k, :], lambda k: r_col[:, k, :]).then_inc(lg_ready, 1)
                pe.matmul(wa_ps[:, 0, :], lora_w[:, :], wb["w"][:, :], start=True, stop=True)
                pe.matmul(wa_ps[:, 1, :], lora_a[:, :], wb["a"][:, :], start=True, stop=True).then_inc(outer_ready, 1)
                pe.wait_ge(lg_act, i + 1)
                pe.matmul(g_ps[:, 0:DIM], lora_g[:, :], wb["g"][:, :], start=True, stop=True).then_inc(g_ready, 1)

        @block.scalar
        def _(act):
            with act.Fori(0, TILES) as i:
                act.wait_ge(cols_ready, i + 1)
                act.copy(r_col[:, :, :], col_ps[:, 0:KC, :])
                act.copy(lora_a[:, :], col_ps[0:LORA, 3, :])
                act.activation(lora_w[:, :], col_ps[0:LORA, 2, :], ACT.Tanh).then_inc(inner_ready, 1)
                act.wait_ge(rkv_ready, i + 1)
                act.wait_ge(stored, 16 * (BATCH * SCAN_IN * i + 1))
                act.copy(q[:, RECV, :], rv_ps[:, 0, :])
                act.copy(q[:, VALUE, :], rv_ps[:, 1, :]).then_inc(rv_ready, 1)
                act.wait_ge(lg_ready, i + 1)
                act.activation(lora_g[:, :], lg_ps[:, 0:P], ACT.Sigmoid).then_inc(lg_act, 1)
                act.wait_ge(z_ready, i + 1)
                act.activation(sig[:, :, :], sig[:, :, :], ACT.Sigmoid).then_inc(sig_ready, 1)
                act.wait_ge(sig_ready, i + 1)
                act.mul(q[:, DECAY, :], sig[:, 0, :], math.exp(-0.5)).then_inc(decay_ready, 1)
                act.wait_ge(kk_ready, i + 1)
                act.activation(sq[:, :], kk[:, :], ACT.Square).then_inc(sq_ready, 1)
                act.wait_ge(ss_ready, i + 1)
                act.activation(norm[:, :], norm[:, :], ACT.Sqrt).then_inc(norm_ready, 1)

        @block.vector
        def _(dve):
            dve.wait_ge(loaded, 16 * LOADS)
            dve.sem_inc(done, 1)
            CHAIN = 7
            with dve.Fori(0, TILES) as i:
                at = [0]

                def then(ins):
                    at[0] += 1
                    ins.then_inc(step, 1)
                    dve.wait_ge(step, i * CHAIN + at[0])

                x = g.xT[:, :, bass.ds(SHIFT + i * P, P)]
                dve.tensor_tensor(delta[:, :, :], g.xT[:, :, bass.ds(i * P, P)], x, ALU.subtract).then_inc(delta_ready, 1)
                dve.wait_ge(delta_ready, i + 1)
                for m in range(MIXES):
                    for k in range(KC):
                        ins = dve.scalar_tensor_tensor(out=mixed[:, m, k, :], in0=delta[:, k, :], scalar=mix_w[:, m, k:k + 1],
                                                       in1=g.xT[:, k, bass.ds(SHIFT + i * P, P)], op0=ALU.mult, op1=ALU.add)
                ins.then_inc(mixed_ready, 1)
                dve.wait_ge(rkv_ready, i + 1)
                dve.tensor_tensor(kk[:, :], k_ps[:, 0:DIM], rows[:, K_K, :], ALU.mult).then_inc(kk_ready, 1)
                dve.wait_ge(outer_ready, i + 1)
                dve.tensor_tensor(sig[:, 0, :], wa_ps[:, 0, :], rows[:, W_BIAS, :], ALU.add)
                dve.tensor_tensor(sig[:, 1, :], wa_ps[:, 1, :], rows[:, A_BIAS, :], ALU.add).then_inc(z_ready, 1)
                dve.wait_ge(sq_ready, i + 1)
                then(dve.tensor_reduce(norm[:, :], heads(sq[:, :]), AX_X, ALU.add))
                dve.tensor_scalar(norm[:, :], norm[:, :], 1e-24, None, ALU.max).then_inc(ss_ready, 1)
                dve.wait_ge(sig_ready, i + 1)
                dve.wait_ge(stored, 16 * (BATCH * SCAN_IN * i + 1))
                then(dve.scalar_tensor_tensor(out=tmp[:, :], in0=sig[:, 1, :], scalar=1.0, in1=rows[:, K_A, :],
                                              op0=ALU.subtract, op1=ALU.mult))
                dve.scalar_tensor_tensor(out=q[:, KEY, :], in0=tmp[:, :], scalar=1.0, in1=k_ps[:, 0:DIM],
                                         op0=ALU.add, op1=ALU.mult)
                dve.wait_ge(norm_ready, i + 1)
                then(dve.reciprocal(norm[:, :], norm[:, :]))
                then(dve.scalar_tensor_tensor(out=heads(q[:, NEG_A, :]), in0=heads(kk[:, :]), scalar=-1.0,
                                              in1=per_head(norm[:, :]), op0=ALU.mult, op1=ALU.mult))
                dve.scalar_tensor_tensor(out=q[:, B_IN, :], in0=q[:, NEG_A, :], scalar=-1.0, in1=sig[:, 1, :],
                                         op0=ALU.mult, op1=ALU.mult)
                dve.wait_ge(rv_ready, i + 1)
                then(dve.tensor_tensor(rk[:, :], q[:, RECV, :], q[:, KEY, :], ALU.mult))
                then(dve.tensor_tensor(rk[:, :], rk[:, :], rows[:, R_K, :], ALU.mult))
                then(dve.tensor_reduce(rk_sum[:, :], heads(rk[:, :]), AX_X, ALU.add))
                dve.tensor_tensor(heads(bonus[:, bass.ds(i, 1), :].rearrange("p o c -> p (o c)")), heads(q[:, VALUE, :]),
                                  per_head(rk_sum[:, :]), ALU.mult)
                dve.wait_ge(g_ready, i + 1)
                dve.wait_ge(decay_ready, i + 1)
                dve.tensor_tensor(gate[:, bass.ds(i, 1), :].rearrange("p o c -> p (o c)"), g_ps[:, 0:DIM], rows[:, G_BIAS, :], ALU.add)\
                   .then_inc(done, 1)
                assert at[0] == CHAIN


def rwkv_scan(nc, g, scan_dram, o_dram):
    with Scope(nc) as s:
        q = s.sb("sc_q", [P, 2, SCAN_IN, STEPS, HD])
        vk = s.sb("sc_vk", [P, 2, STEPS, HALF, HD])
        state = s.sb("sc_state", [P, STEPS + 1, HALF, HD])
        sa_terms = s.sb("sc_sa_terms", [P, HALF, HD])
        sa = s.sb("sc_sa", [P, HALF])
        sab = s.sb("sc_sab", [P, HALF, HD])
        kept = s.sb("sc_kept", [P, HALF, HD])
        kept_vk = s.sb("sc_kept_vk", [P, HALF, HD])
        o_terms = s.sb("sc_o_terms", [P, STEPS, HALF, HD])
        o = s.sb("sc_o", [P, 2, STEPS, HALF])
        loaded = [s.sem(f"sc_loaded{n}") for n in range(2)]
        vk_ready = s.sem("sc_vk_ready")
        sa_terms_ready = s.sem("sc_sa_terms_ready")
        sa_ready = s.sem("sc_sa_ready")
        sab_ready = s.sem("sc_sab_ready")
        kept_ready = s.sem("sc_kept_ready")
        kept_vk_ready = s.sem("sc_kept_vk_ready")
        state_ready = s.sem("sc_state_ready")
        o_terms_ready = s.sem("sc_o_terms_ready")
        o_ready = s.sem("sc_o_ready")
        carried = s.sem("sc_carried")
        stored = [s.sem(f"sc_stored{n}") for n in range(2)]
        CHUNKS = SEQ // STEPS
        block = s.block()
        BH = BATCH * HEADS

        def load(sp, c, u):
            src = scan_dram[:, :, :, bass.ds(c * STEPS, STEPS), :].rearrange("b h q t j -> (b h) q t j")
            for half in range(2):
                for n in range(SCAN_IN):
                    sp.dma_start(q[half * BH:(half + 1) * BH, u, n, :, :], src[:, n, :, :]).then_inc(loaded[u], 16)

        @block.sync
        def _(sp):
            load(sp, 0, 0)
            load(sp, 1, 1)
            with sp.Fori(0, CHUNKS // 2 - 1) as i:
                for u in range(2):
                    sp.wait_ge(o_ready, 2 * i + u + 1)
                    load(sp, 2 * i + u + 2, u)

        @block.scalar
        def _(act):
            for u in range(2):
                act.sem_inc(stored[u], 16)
            with act.Fori(0, CHUNKS // 2) as i:
                for u in range(2):
                    c = 2 * i + u
                    act.wait_ge(o_ready, c + 1)
                    rows = o_dram[bass.ds(c * P, P), :].rearrange("(t b) (h f j) -> f (b h) t j", b=BATCH, f=2, j=HALF)
                    for half in range(2):
                        act.dma_start(rows[half], o[half * BH:(half + 1) * BH, u, :, :]).then_inc(stored[u], 16)
            for u in range(2):
                act.wait_ge(stored[u], 16 * (2 * (CHUNKS // 2) + 1))

        def row(ap):
            return ap.unsqueeze(1).to_broadcast([P, HALF, HD])

        @block.gpsimd
        def _(pool):
            with pool.Fori(0, CHUNKS // 2) as i:
                for u in range(2):
                    c = 2 * i + u
                    pool.wait_ge(loaded[u], 16 * 2 * SCAN_IN * (i + 1))
                    for t in range(STEPS):
                        n = c * STEPS + t
                        pool.wait_ge(state_ready, n + 1)
                        if t == 0:
                            pool.wait_ge(carried, c + 1)
                        pool.tensor_tensor(kept[:, :, :], state[:, t, :, :], row(q[:, u, DECAY, t, :]), ALU.mult)\
                            .then_inc(kept_ready, 1)
                        pool.wait_ge(kept_ready, n + 1)
                        pool.wait_ge(vk_ready, c + 1)
                        pool.tensor_tensor(kept_vk[:, :, :], kept[:, :, :], vk[:, u, t, :, :], ALU.add).then_inc(kept_vk_ready, 1)

        @block.vector
        def _(dve):
            dve.memset(state[:, 0, :, :], 0.0).then_inc(carried, 1)
            dve.memset(sa[:, :], 0.0).then_inc(state_ready, 1)
            with dve.Fori(0, CHUNKS // 2) as i:
                for u in range(2):
                    c = 2 * i + u
                    dve.wait_ge(loaded[u], 16 * 2 * SCAN_IN * (i + 1))
                    for half in range(2):
                        lanes = slice(half * BH, (half + 1) * BH)
                        ins = dve.tensor_tensor(vk[lanes, u, :, :, :],
                            q[lanes, u, VALUE, :, half * HALF:(half + 1) * HALF].unsqueeze(3).to_broadcast([BH, STEPS, HALF, HD]),
                            q[lanes, u, KEY, :, :].unsqueeze(2).to_broadcast([BH, STEPS, HALF, HD]), ALU.mult)
                    ins.then_inc(vk_ready, 1)
                    for t in range(STEPS):
                        n = c * STEPS + t
                        dve.wait_ge(state_ready, n + 1)
                        if t == 0:
                            dve.wait_ge(carried, c + 1)
                        dve.tensor_tensor(sa_terms[:, :, :], state[:, t, :, :], row(q[:, u, NEG_A, t, :]), ALU.mult)\
                           .then_inc(sa_terms_ready, 1)
                        dve.wait_ge(sa_terms_ready, n + 1)
                        dve.tensor_reduce(sa[:, :], sa_terms[:, :, :], AX_X, ALU.add).then_inc(sa_ready, 1)
                        dve.wait_ge(sa_ready, n + 1)
                        dve.tensor_tensor(sab[:, :, :], sa[:, :].unsqueeze(2).to_broadcast([P, HALF, HD]),
                                          row(q[:, u, B_IN, t, :]), ALU.mult).then_inc(sab_ready, 1)
                        dve.wait_ge(sab_ready, n + 1)
                        dve.wait_ge(kept_vk_ready, n + 1)
                        dve.tensor_tensor(state[:, t + 1, :, :], sab[:, :, :], kept_vk[:, :, :], ALU.add).then_inc(state_ready, 1)
                    dve.wait_ge(state_ready, c * STEPS + STEPS + 1)
                    dve.tensor_tensor(o_terms[:, :, :, :], state[:, 1:, :, :],
                                      q[:, u, RECV, :, :].unsqueeze(2).to_broadcast([P, STEPS, HALF, HD]), ALU.mult)\
                       .then_inc(o_terms_ready, 1)
                    dve.tensor_copy(state[:, 0, :, :], state[:, STEPS, :, :]).then_inc(carried, 1)
                    dve.wait_ge(o_terms_ready, c + 1)
                    dve.wait_ge(stored[u], 16 * (2 * i + 1))
                    dve.tensor_reduce(o[:, u, :, :], o_terms[:, :, :, :], AX_X, ALU.add).then_inc(o_ready, 1)


def rwkv_output(nc, d, g, o_dram, gate, bonus):
    with Scope(nc) as s:
        w_o = s.sb("ro_w_o", [P, KC, DIM])
        gn = s.sb("ro_gn", [P, 2, DIM])
        ident = s.sb("ro_ident", [P, P])
        o = s.sb("ro_o", [P, 2, DIM])
        mean = s.sb("ro_mean", [P, HEADS])
        dev = s.sb("ro_dev", [P, DIM])
        sq = s.sb("ro_sq", [P, DIM])
        var = s.sb("ro_var", [P, HEADS])
        gated = s.sb("ro_gated", [P, DIM])
        col = s.sb("ro_col", [P, KC, P])
        col_ps = s.ps("ro_col_ps", [P, KC, P])
        y_ps = s.ps("ro_y_ps", [P, KC, P])
        w_loaded = s.sem("ro_w_loaded")
        o_loaded = [s.sem(f"ro_o_loaded{n}") for n in range(2)]
        dev_ready = s.sem("ro_dev_ready")
        sq_ready = s.sem("ro_sq_ready")
        var_ready = s.sem("ro_var_ready")
        std_ready = s.sem("ro_std_ready")
        step = s.sem("ro_step")
        gated_ready = s.sem("ro_gated_ready")
        turned = s.sem("ro_turned")
        col_ready = s.sem("ro_col_ready")
        y_ready = s.sem("ro_y_ready")
        x_done = s.sem("ro_x_done")
        block = s.block()

        @block.sync
        def _(sp):
            sp.dma_start(w_o[:, :, :], d["rw_w_o"]).then_inc(w_loaded, 16)
            sp.dma_start(ident[:, :], d["ident"]).then_inc(w_loaded, 16)
            sp.dma_start(gn[:, 0, :], d["rw_gn_w"].partition_broadcast(P)).then_inc(w_loaded, 16)
            sp.dma_start(gn[:, 1, :], d["rw_gn_b"].partition_broadcast(P)).then_inc(w_loaded, 16)
            for u in range(2):
                sp.dma_start(o[:, u, :], o_dram[u * P:(u + 1) * P, :]).then_inc(o_loaded[u], 16)
            with sp.Fori(0, TILES // 2 - 1) as i:
                for u in range(2):
                    sp.wait_ge(dev_ready, 2 * i + u + 1)
                    sp.dma_start(o[:, u, :], o_dram[bass.ds((2 * i + u + 2) * P, P), :]).then_inc(o_loaded[u], 16)

        @block.tensor
        def _(pe):
            pe.wait_ge(w_loaded, 16 * 4)
            with pe.Fori(0, TILES) as i:
                pe.wait_ge(gated_ready, i + 1)
                for k in range(KC):
                    mm = pe.transpose(col_ps[:, k, :], gated[:, k * P:(k + 1) * P], ident[:, :])
                mm.then_inc(turned, 1)
                pe.wait_ge(col_ready, i + 1)
                pe.wait_ge(x_done, i + 1)
                for o_ in range(KC):
                    for k in range(KC):
                        mm = pe.matmul(y_ps[:, o_, :], w_o[:, k, o_ * P:(o_ + 1) * P], col[:, k, :],
                                       start=(k == 0), stop=(k == KC - 1))
                mm.then_inc(y_ready, 1)

        @block.scalar
        def _(act):
            with act.Fori(0, TILES) as i:
                act.wait_ge(dev_ready, i + 1)
                act.activation(sq[:, :], dev[:, :], ACT.Square).then_inc(sq_ready, 1)
                act.wait_ge(var_ready, i + 1)
                act.activation(var[:, :], var[:, :], ACT.Sqrt, scale=1.0 / HD, bias=g.eps[:, :]).then_inc(std_ready, 1)
                act.wait_ge(turned, i + 1)
                act.copy(col[:, :, :], col_ps[:, :, :]).then_inc(col_ready, 1)

        @block.vector
        def _(dve):
            dve.wait_ge(w_loaded, 16 * 4)
            dve.sem_inc(x_done, 1)
            CHAIN = 6
            with dve.Fori(0, TILES // 2) as i:
                for u in range(2):
                    n, at = 2 * i + u, [0]

                    def then(ins):
                        at[0] += 1
                        ins.then_inc(step, 1)
                        dve.wait_ge(step, n * CHAIN + at[0])

                    def tile_of(ap):
                        return ap[:, bass.ds(n, 1), :].rearrange("p o c -> p (o c)")

                    dve.wait_ge(o_loaded[u], 16 * (i + 1))
                    then(dve.tensor_reduce(mean[:, :], heads(o[:, u, :]), AX_X, ALU.add))
                    dve.scalar_tensor_tensor(out=heads(dev[:, :]), in0=per_head(mean[:, :]), scalar=-1.0 / HD,
                                             in1=heads(o[:, u, :]), op0=ALU.mult, op1=ALU.add).then_inc(dev_ready, 1)
                    dve.wait_ge(sq_ready, n + 1)
                    dve.tensor_reduce(var[:, :], heads(sq[:, :]), AX_X, ALU.add).then_inc(var_ready, 1)
                    dve.wait_ge(std_ready, n + 1)
                    then(dve.reciprocal(var[:, :], var[:, :]))
                    dve.wait_ge(dev_ready, n + 1)
                    then(dve.tensor_tensor(heads(dev[:, :]), heads(dev[:, :]), per_head(var[:, :]), ALU.mult))
                    then(dve.tensor_tensor(dev[:, :], dev[:, :], gn[:, 0, :], ALU.mult))
                    then(dve.tensor_tensor(dev[:, :], dev[:, :], gn[:, 1, :], ALU.add))
                    then(dve.tensor_tensor(dev[:, :], dev[:, :], tile_of(bonus), ALU.add))
                    dve.tensor_tensor(gated[:, :], dev[:, :], tile_of(gate), ALU.mult).then_inc(gated_ready, 1)
                    dve.wait_ge(y_ready, n + 1)
                    x = g.xT[:, :, bass.ds(SHIFT + n * P, P)]
                    dve.tensor_tensor(x, x, y_ps[:, :, :], ALU.add).then_inc(x_done, 1)
                    assert at[0] == CHAIN


QC = SEQ // P
SCALE = float(DIM) ** -0.5


def cross_attention_phase(nc, d, g):
    with Scope(nc) as s:
        w = {m: s.sb(f"ca_w_{m}", [P, KC, DIM]) for m in ("q", "k", "v")}
        b = {m: s.sb(f"ca_b_{m}", [P, KC]) for m in ("q", "k", "v")}
        ident = s.sb("ca_ident", [P, P])
        ctx = s.sb("ca_ctx", [P, KC, SRC])
        x = s.sb("ca_x", [P, KC, SEQ])
        q = s.sb("ca_q", [P, KC, SEQ])
        k_ = s.sb("ca_k", [P, KC, SRC])
        v = s.sb("ca_v", [P, SC, DIM])
        neg_max = s.sb("ca_neg_max", [P, QC])
        total = s.sb("ca_total", [P, QC])
        prob = s.sb("ca_prob", [P, QC, SRC])
        prob_t = s.sb("ca_prob_t", [P, SC, SEQ])
        y = s.sb("ca_y", [P, KC, SEQ])
        qk_ps = s.ps("ca_qk_ps", [P, 2, NB])
        score_ps = s.ps("ca_score_ps", [P, 2, SRC])
        turn_ps = s.ps("ca_turn_ps", [P, 2, NB])
        out_ps = s.ps("ca_out_ps", [P, KC, SEQ])
        loaded = s.sem("ca_loaded")
        staged = s.sem("ca_staged")
        qk_ready = s.sem("ca_qk_ready")
        qk_kept = s.sem("ca_qk_kept")
        v_ready = s.sem("ca_v_ready")
        v_kept = s.sem("ca_v_kept")
        scores_ready = s.sem("ca_scores_ready")
        max_ready = s.sem("ca_max_ready")
        scaled_max = s.sem("ca_scaled_max")
        exp_ready = s.sem("ca_exp_ready")
        inverse_ready = s.sem("ca_inverse_ready")
        prob_ready = s.sem("ca_prob_ready")
        turned = s.sem("ca_turned")
        turn_kept = s.sem("ca_turn_kept")
        out_ready = s.sem("ca_out_ready")
        y_part = s.sem("ca_y_part")
        x_done = s.sem("ca_x_done")
        ln = LayerNorm(s, "ca_ln", qk_ps[:, 0, :], qk_ps[:, 1, :])
        block = s.block()
        LOADS = 7

        def x_of(i):
            return g.xT[:, :, bass.ds(SHIFT, TOK)].rearrange("p k (t b) -> p k t b", b=BATCH)[:, :, :, bass.ds(i, 1)]\
                    .rearrange("p k t o -> p k (t o)")

        @block.sync
        def _(sp):
            for m in ("q", "k", "v"):
                sp.dma_start(w[m][:, :, :], d[f"ca_w_{m}"]).then_inc(loaded, 16)
                sp.dma_start(b[m][:, :], d[f"ca_b_{m}"]).then_inc(loaded, 16)
            sp.dma_start(ident[:, :], d["ident"]).then_inc(loaded, 16)

        @block.gpsimd
        def _(pool):
            with pool.Fori(0, BATCH) as i:
                pool.wait_ge(x_done, i + 1)
                pool.tensor_copy(ctx[:, :, :], g.ctxT[:, :, bass.ds(i * SRC, SRC)])
                pool.tensor_copy(x[:, :, :], x_of(i)).then_inc(staged, 1)

        @block.tensor
        def _(pe):
            pe.wait_ge(loaded, 16 * LOADS)
            with pe.Fori(0, BATCH) as i:
                pe.wait_ge(staged, i + 1)
                for n, (wt, src) in enumerate(((w["q"], x), (w["k"], ctx))):
                    for o in range(KC):
                        if n > 0:
                            pe.wait_ge(qk_kept, 4 * i + 2 * n + o - 1)
                        for k in range(KC):
                            mm = pe.matmul(qk_ps[:, o, :], wt[:, k, o * P:(o + 1) * P], src[:, k, :],
                                           start=(k == 0), stop=(k == KC - 1))
                        mm.then_inc(qk_ready, 1)
                for c in range(SC):
                    if c >= 2:
                        pe.wait_ge(v_kept, SC * i + c - 1)
                    for k in range(KC):
                        mm = pe.matmul(turn_ps[:, c % 2, 0:DIM], ctx[:, k, c * P:(c + 1) * P], w["v"][:, k, :],
                                       start=(k == 0), stop=(k == KC - 1))
                    mm.then_inc(v_ready, 1)
                pe.wait_ge(qk_kept, 4 * i + 4)
                for c in range(QC):
                    if c >= 2:
                        pe.wait_ge(exp_ready, QC * i + c - 1)
                    for k in range(KC):
                        mm = pe.matmul(score_ps[:, c % 2, :], q[:, k, c * P:(c + 1) * P], k_[:, k, :],
                                       start=(k == 0), stop=(k == KC - 1))
                    mm.then_inc(scores_ready, 1)
                pe.wait_ge(v_kept, SC * i + SC)
                for c in range(QC):
                    pe.wait_ge(prob_ready, QC * i + c + 1)
                    if c >= 2:
                        pe.wait_ge(turn_kept, QC * i + c - 1)
                    for kc in range(SC):
                        mm = pe.transpose(turn_ps[:, c % 2, kc * P:(kc + 1) * P], prob[:, c, kc * P:(kc + 1) * P], ident[:, :])
                    mm.then_inc(turned, 1)
                pe.wait_ge(turn_kept, QC * i + QC)
                for o in range(KC):
                    for kc in range(SC):
                        mm = pe.matmul(out_ps[:, o, :], v[:, kc, o * P:(o + 1) * P], prob_t[:, kc, :],
                                       start=(kc == 0), stop=(kc == SC - 1))
                mm.then_inc(out_ready, 1)
                ln.tensor(pe, i, lambda k: y[:, k, :], g.mean_mat[:, :])

        @block.scalar
        def _(act):
            act.wait_ge(loaded, 16 * LOADS)
            with act.Fori(0, BATCH) as i:
                for n, (m, dst) in enumerate((("q", q), ("k", k_))):
                    for o in range(KC):
                        act.wait_ge(qk_ready, 4 * i + 2 * n + o + 1)
                        act.activation(dst[:, o, :], qk_ps[:, o, :], ACT.Identity, bias=b[m][:, o:o + 1]).then_inc(qk_kept, 1)
                for c in range(SC):
                    act.wait_ge(v_ready, SC * i + c + 1)
                    act.copy(v[:, c, :], turn_ps[:, c % 2, 0:DIM]).then_inc(v_kept, 1)
                for c in range(QC):
                    act.wait_ge(max_ready, QC * i + c + 1)
                    act.mul(neg_max[:, c:c + 1], neg_max[:, c:c + 1], SCALE).then_inc(scaled_max, 1)
                    act.wait_ge(scaled_max, QC * i + c + 1)
                    act.activation(prob[:, c, :], score_ps[:, c % 2, :], ACT.Exp, bias=neg_max[:, c:c + 1], scale=SCALE,
                                   accum_out=total[:, c:c + 1]).then_inc(exp_ready, 1)
                for c in range(QC):
                    act.wait_ge(turned, QC * i + c + 1)
                    act.copy(prob_t[:, :, c * P:(c + 1) * P], turn_ps[:, c % 2, :].rearrange("p (s q) -> p s q", s=SC))\
                       .then_inc(turn_kept, 1)
                ln.scalar(act, i, g.eps[:, :])

        @block.vector
        def _(dve):
            dve.wait_ge(loaded, 16 * LOADS)
            dve.sem_inc(x_done, 1)
            with dve.Fori(0, BATCH) as i:
                for c in range(QC):
                    dve.wait_ge(scores_ready, QC * i + c + 1)
                    dve.tensor_reduce(neg_max[:, c:c + 1], score_ps[:, c % 2, :], AX_X, ALU.max, negate=True).then_inc(max_ready, 1)
                    dve.wait_ge(exp_ready, QC * i + c + 1)
                    dve.reciprocal(total[:, c:c + 1], total[:, c:c + 1]).then_inc(inverse_ready, 1)
                    dve.wait_ge(inverse_ready, QC * i + c + 1)
                    dve.tensor_scalar(prob[:, c, :], prob[:, c, :], total[:, c:c + 1], None, ALU.mult).then_inc(prob_ready, 1)
                dve.wait_ge(out_ready, i + 1)
                for o in range(KC):
                    ins = dve.scalar_tensor_tensor(out=y[:, o, :], in0=out_ps[:, o, :], scalar=b["v"][:, o:o + 1],
                                                   in1=x[:, o, :], op0=ALU.add, op1=ALU.add)
                ins.then_inc(ln.y_ready, 1)
                ln.vector(dve, i, y[:, :, :], x_of(i)).then_inc(x_done, 1)


EXPERTS1 = 4
INNER = 688
IC = -(-INNER // P)
CH = -(-INNER // IC)
FULL = IC - 1


def shared_mixture_phase(nc, d, g):
    E = EXPERTS1
    ALL = E + 1
    with Scope(nc) as s:
        w_gate = s.sb("sm_w_gate", [P, ALL, KC, INNER])
        w_up = s.sb("sm_w_up", [P, ALL, KC, INNER])
        w_down = s.sb("sm_w_down", [P, ALL, IC, DIM])
        w_router = s.sb("sm_w_router", [P, KC, E])
        zero_bias = s.sb("sm_zero_bias", [E, 1])
        pick = s.sb("sm_pick", [E, E, P])
        ident = s.sb("sm_ident", [P, P])
        silu = s.sb("sm_silu", [P, 2, NB])
        gu = s.sb("sm_gu", [P, 2, NB])
        spread = s.sb("sm_spread", [P, E, NB])
        y = s.sb("sm_y", [P, KC, NB])
        out = s.sb("sm_out", [P, KC, NB])
        gate_ps = s.ps("sm_gate_ps", [P, 2, NB])
        up_ps = s.ps("sm_up_ps", [P, 2, NB])
        aux_ps = s.ps("sm_aux_ps", [P, 2, NB])
        down_ps = s.ps("sm_down_ps", [P, KC, NB])
        loaded = s.sem("sm_loaded")
        zeroed = s.sem("sm_zeroed")
        gate_ready = s.sem("sm_gate_ready")
        up_ready = s.sem("sm_up_ready")
        silu_ready = s.sem("sm_silu_ready")
        silu_weighted = s.sem("sm_silu_weighted")
        weighted = s.sem("sm_weighted")
        spread_turned = s.sem("sm_spread_turned")
        spread_ready = s.sem("sm_spread_ready")
        down_ready = s.sem("sm_down_ready")
        out_ready = s.sem("sm_out_ready")
        stored = s.sem("sm_stored")
        router = Router(s, "sm_router", E, True, aux_ps[0:E, 0, :],
                        aux_ps[:, 1, 0:TB * E].rearrange("p (c e) -> p c e", e=E))
        ln = LayerNorm(s, "sm_ln", aux_ps[:, 0, :], aux_ps[:, 1, :])
        block = s.block()
        LOADS = 3 + 4 * ALL
        N = ALL * IC

        def rows(c):
            return CH if c < FULL else INNER - FULL * CH

        @block.sync
        def _(sp):
            sp.dma_start(w_router[:, :, :], d["sm_w_router"]).then_inc(loaded, 16)
            sp.dma_start(pick[:, :, :], d["pick"][0:E, 0:E, :]).then_inc(loaded, 16)
            sp.dma_start(ident[:, :], d["ident"]).then_inc(loaded, 16)
            for e in range(ALL):
                sp.dma_start(w_gate[:, e, :, :], d["sm_w_gate"][e]).then_inc(loaded, 16)
                sp.dma_start(w_up[:, e, :, :], d["sm_w_up"][e]).then_inc(loaded, 16)
                down = d["sm_w_down"][e]
                sp.dma_start(w_down[0:CH, e, 0:FULL, :], down[0:FULL * CH, :].rearrange("(c p) n -> p c n", p=CH)).then_inc(loaded, 16)
                sp.dma_start(w_down[0:rows(FULL), e, FULL, :], down[FULL * CH:INNER, :]).then_inc(loaded, 16)
            sp.sem_inc(stored, 16)
            with sp.Fori(0, BLOCKS) as i:
                sp.wait_ge(out_ready, i + 2)
                sp.dma_start(d["out"][:, :, bass.ds(i * NB, NB)], out[:, :, :]).then_inc(stored, 16)
            sp.wait_ge(stored, 16 * (BLOCKS + 1))

        @block.tensor
        def _(pe):
            pe.wait_ge(loaded, 16 * LOADS)
            with pe.Fori(0, BLOCKS) as i:
                def x(k):
                    return g.xT[:, k, bass.ds(SHIFT + i * NB, NB)]

                def up_and_gate(n):
                    e, c = n // IC, n % IC
                    m = rows(c)
                    if n >= 2:
                        pe.wait_ge(weighted, i * N + n - 1)
                    for ps, w, ready in ((gate_ps, w_gate, gate_ready), (up_ps, w_up, up_ready)):
                        for k in range(KC):
                            mm = pe.matmul(ps[0:m, n % 2, :], w[:, e, k, c * CH:c * CH + m], x(k),
                                           start=(k == 0), stop=(k == KC - 1))
                        mm.then_inc(ready, 1)

                def down(n):
                    e, c = n // IC, n % IC
                    m = rows(c)
                    pe.wait_ge(weighted, i * N + n + 1)
                    for o in range(KC):
                        mm = pe.matmul(down_ps[:, o, :], w_down[0:m, e, c, o * P:(o + 1) * P], gu[0:m, n % 2, :],
                                       start=(n == 0), stop=(n == N - 1))
                    if n == N - 1:
                        mm.then_inc(down_ready, 1)

                pe.wait_ge(out_ready, i + 1)
                router.tensor(pe, i, w_router, x, ident[:, :])
                pe.wait_ge(router.weight_rows_ready, i + 1)
                for e in range(E):
                    if e >= 2:
                        pe.wait_ge(spread_ready, i * E + e - 1)
                    pe.matmul(aux_ps[:, e % 2, :], pick[:, e, :], router.weight_rows[:, :], start=True, stop=True)\
                      .then_inc(spread_turned, 1)
                for n in range(N):
                    up_and_gate(n)
                    if n > 0:
                        down(n - 1)
                down(N - 1)
                ln.tensor(pe, i, lambda k: y[:, k, :], g.mean_mat[:, :])

        @block.scalar
        def _(act):
            act.wait_ge(zeroed, 1)
            with act.Fori(0, BLOCKS) as i:
                router.scalar(act, i, zero_bias[:, :])
                for e in range(E):
                    act.wait_ge(spread_turned, i * E + e + 1)
                    act.copy(spread[:, e, :], aux_ps[:, e % 2, :]).then_inc(spread_ready, 1)
                for n in range(N):
                    m = rows(n % IC)
                    act.wait_ge(gate_ready, i * N + n + 1)
                    if n >= 2:
                        act.wait_ge(weighted, i * N + n - 1)
                    act.activation(silu[0:m, n % 2, :], gate_ps[0:m, n % 2, :], ACT.Silu).then_inc(silu_ready, 1)
                ln.scalar(act, i, g.eps[:, :])

        @block.vector
        def _(dve):
            dve.sem_inc(out_ready, 1)
            dve.wait_ge(router.filled, 2)
            with dve.Fori(0, BLOCKS) as i:
                router.vector(dve, i)
                for n in range(N):
                    e, m = n // IC, rows(n % IC)
                    dve.wait_ge(silu_ready, i * N + n + 1)
                    dve.wait_ge(up_ready, i * N + n + 1)
                    if n == 0:
                        dve.wait_ge(spread_ready, i * E + E)
                    if e < E:
                        dve.tensor_tensor(silu[0:m, n % 2, :], silu[0:m, n % 2, :], spread[0:m, e, :], ALU.mult)\
                           .then_inc(silu_weighted, 1)
                        dve.wait_ge(silu_weighted, i * E * IC + n + 1)
                    dve.tensor_tensor(gu[0:m, n % 2, :], silu[0:m, n % 2, :], up_ps[0:m, n % 2, :], ALU.mult)\
                       .then_inc(weighted, 1)
                dve.wait_ge(down_ready, i + 1)
                dve.tensor_tensor(y[:, :, :], down_ps[:, :, :], g.xT[:, :, bass.ds(SHIFT + i * NB, NB)], ALU.add)\
                   .then_inc(ln.y_ready, 1)
                dve.wait_ge(stored, 16 * (i + 1))
                ln.vector(dve, i, y[:, :, :], out[:, :, :]).then_inc(out_ready, 1)

        @block.gpsimd
        def _(pool):
            pool.memset(zero_bias[:, :], 0.0).then_inc(zeroed, 1)
            router.gpsimd(pool)


class Shared:
    pass


def decoder_program(nc, d):
    with Scope(nc) as s:
        g = Shared()
        g.xT = s.sb("xT", [P, KC, SHIFT + TOK])
        g.ctxT = s.sb("ctxT", [P, KC, BATCH * SRC])
        g.mean_mat = s.sb("mean_mat", [P, P])
        g.eps = s.sb("eps", [P, 1])
        g.consts = s.sem("consts")
        recurrence_phase(nc, d, g)
        attention_lstm_phase(nc, d, g)
        norm_phase(nc, g, "ln_lstm")
        mixture_phase(nc, d, g)
        rwkv_phase(nc, d, g)
        norm_phase(nc, g, "ln_rwkv")
        cross_attention_phase(nc, d, g)
        shared_mixture_phase(nc, d, g)



def feature_major(x):
    return np.ascontiguousarray(x.transpose(2, 1, 0).reshape(KC, P, TOK).transpose(1, 0, 2))


def rows_on_partitions(w):
    return np.ascontiguousarray(w.reshape(-1, P, w.shape[1]).transpose(1, 0, 2))


def on_partitions(b):
    return np.ascontiguousarray(b.reshape(-1, P).T)


def each(f, ws):
    return np.ascontiguousarray(np.stack([f(w) for w in ws]))


def by_quarter(w):
    w = w.reshape(*w.shape[:-1], GATES, QUARTERS, QW)[..., [3, 0, 1, 2], :, :]
    return np.ascontiguousarray(np.moveaxis(w, -2, -3).reshape(*w.shape[:-3], GATE_W))


def quarter_selector():
    sel = np.zeros((P, 2, KC * BATCH), np.float32)
    for j in range(QUARTERS):
        for b in range(BATCH):
            sel[j * STRIP + b, j % 2, j // 2 * BATCH + b] = 1
    return sel


def laid_out(inputs):
    i = {name: np.asarray(a) for name, a in inputs.items()}
    d = {"xT": feature_major(i["x"]),
         "ctxT": np.ascontiguousarray(i["ctx_1024"].transpose(2, 0, 1).reshape(KC, P, BATCH * SRC).transpose(1, 0, 2))}
    for m in ("in", "gate", "lam", "out"):
        d[f"rec_w_{m}"] = rows_on_partitions(i[f"L0_attn_W_{m}"].T)
        d[f"rec_b_{m}"] = on_partitions(i[f"L0_attn_b_{m}"])
    d["rec_gamma"] = on_partitions(i["L0_attn_gamma"])
    d["rec_beta"] = on_partitions(i["L0_attn_beta"])

    w_ih, w_out = i["L0_xattn_W_ih"], i["L0_xattn_Wout"]
    d["lstm_w_x"] = rows_on_partitions(by_quarter(w_ih[:, :DIM].T))
    d["lstm_w_attn"] = rows_on_partitions(by_quarter(w_ih[:, DIM:].T))
    d["lstm_w_hid"] = rows_on_partitions(by_quarter(i["L0_xattn_W_hh"].T))
    d["lstm_w_q"] = rows_on_partitions(i["L0_xattn_Wq"])
    d["lstm_w_out_c"] = rows_on_partitions(w_out[:, :DIM].T)
    d["lstm_w_out_h"] = rows_on_partitions(w_out[:, DIM:].T)
    d["lstm_b_ih"], d["lstm_b_hh"] = (by_quarter(i[f"L0_xattn_{b}"]) for b in ("b_ih", "b_hh"))
    d["lstm_b_out"] = i["L0_xattn_b_out"]

    d["mix_w_router"] = rows_on_partitions(i["L0_ffn_router_w"])
    d["mix_b_router"] = np.ascontiguousarray(i["L0_ffn_router_b"].reshape(EXPERTS0, 1))
    for m in ("gate", "up", "down"):
        d[f"mix_w_{m}"] = each(rows_on_partitions, i[f"L0_ffn_we_{m}"])

    rw = {name[len("L1_attn_"):]: a for name, a in i.items() if name.startswith("L1_attn_")}
    d["rw_mix_w"] = np.ascontiguousarray(np.stack([on_partitions(rw[f"x_{m}"]) for m in "rwkva"], 1))
    for m in ("r", "k", "v", "o"):
        d[f"rw_w_{m}"] = rows_on_partitions(rw[f"W_{m}"])
    for m in ("w", "a", "g"):
        d[f"rw_wa_{m}"] = rows_on_partitions(rw[f"{m}_lora_a"])
        d[f"rw_wb_{m}"] = rw[f"{m}_lora_b"]
        d[f"rw_{m}_bias"] = rw[f"{m}_lora_bias"]
    d["rw_k_k"], d["rw_k_a"], d["rw_r_k"] = rw["k_k"], rw["k_a"], rw["r_k"].reshape(-1)
    d["rw_gn_w"], d["rw_gn_b"] = rw["gn_weight"], rw["gn_bias"]

    for m in ("q", "k", "v"):
        d[f"ca_w_{m}"] = rows_on_partitions(i[f"L1_xattn_W{m}"].T)
        d[f"ca_b_{m}"] = on_partitions(i[f"L1_xattn_b{m}"])

    d["sm_w_router"] = rows_on_partitions(i["L1_ffn_gate_w"].T)
    d["sm_w_gate"] = each(lambda w: rows_on_partitions(w.T), [*i["L1_ffn_eg"], i["L1_ffn_sg"]])
    d["sm_w_up"] = each(lambda w: rows_on_partitions(w.T), [*i["L1_ffn_eu"], i["L1_ffn_su"]])
    d["sm_w_down"] = each(lambda w: w.T, [*i["L1_ffn_ed"], i["L1_ffn_sd"]])

    d["sel_quarter"] = quarter_selector()
    sel_batch = np.zeros((P, BATCH), np.float32)
    sel_batch[np.arange(BATCH) * STRIP, np.arange(BATCH)] = 1
    d["sel_batch"] = sel_batch
    d["ident"] = np.eye(P, dtype=np.float32)
    pick = np.zeros((EXPERTS0, EXPERTS0, P), np.float32)
    pick[np.arange(EXPERTS0), np.arange(EXPERTS0)] = 1
    d["pick"] = pick
    return d


def kernel(**inputs):
    import concourse.bacc as bacc
    from concourse.bass_utils import run_bass_kernel_spmd

    nc = bacc.Bacc("TRN2", target_bir_lowering=False, num_devices=1)
    arrays, d = {}, {}
    for name, a in laid_out(inputs).items():
        arrays[f"in_{name}"] = np.ascontiguousarray(a)
        d[name] = nc.dram_tensor(f"in_{name}", a.shape, F32, kind="ExternalInput").ap()
    d["out"] = nc.dram_tensor("out_xT", (P, KC, TOK), F32, kind="ExternalOutput").ap()
    decoder_program(nc, d)
    r = run_bass_kernel_spmd(nc, [arrays], core_ids=[0])
    got = np.asarray(r.results[0]["out_xT"])
    return np.ascontiguousarray(got.transpose(1, 0, 2).reshape(DIM, SEQ, BATCH).transpose(2, 1, 0))
```

```python
import math
from contextlib import ExitStack

import numpy as np

import concourse.bass as bass
from concourse import mybir

F32 = mybir.dt.float32
F32R = mybir.dt.float32r
ALU = mybir.AluOpType
ACT = mybir.ActivationFunctionType
AX_X = mybir.AxisListType.X

P = 128
BATCH, SEQ, DIM = 4, 512, 256
KC = DIM // P
TOK = BATCH * SEQ
NB = 512
BLOCKS = TOK // NB
SHIFT = BATCH
LN_EPS = 1e-5


class Scope:

    def __init__(self, nc):
        self.nc = nc
        self.stack = ExitStack()
        self.running = ExitStack()
        self.sems = []

    def __enter__(self):
        return self

    def __exit__(self, *exc):
        self.running.close()
        if self.sems:
            numbers = sorted(x.num for x in self.sems)
            with self.nc.Block() as block:
                @block.sync
                def _(sp):
                    first = numbers[0]
                    for n, after in zip(numbers, [*numbers[1:], None]):
                        if after != n + 1:
                            sp.sem_clear(range(first, n + 1))
                            first = after
        return self.stack.__exit__(*exc)

    def sb(self, name, shape, dtype=F32):
        return self.stack.enter_context(self.nc.sbuf_tensor(name, shape, dtype))

    def ps(self, name, shape):
        return self.stack.enter_context(self.nc.psum_tensor(name, shape, F32))

    def sem(self, name):
        self.sems.append(self.stack.enter_context(self.nc.semaphore(name)))
        return self.sems[-1]

    def block(self):
        return self.running.enter_context(self.nc.Block())


def over_chunks(ap, n=KC):
    return ap.unsqueeze(1).to_broadcast([ap.shape[0], n, ap.shape[1]])


class LayerNorm:

    def __init__(self, s, name, mean_ps, var_ps, width=NB):
        self.mean_ps, self.var_ps = mean_ps, var_ps
        self.d = s.sb(f"{name}_d", [P, KC, width])
        self.sq = s.sb(f"{name}_sq", [P, KC, width])
        self.rstd = s.sb(f"{name}_rstd", [P, width])
        self.y_ready = s.sem(f"{name}_y_ready")
        self.mean_ready = s.sem(f"{name}_mean_ready")
        self.d_ready = s.sem(f"{name}_d_ready")
        self.sq_ready = s.sem(f"{name}_sq_ready")
        self.var_ready = s.sem(f"{name}_var_ready")
        self.std_ready = s.sem(f"{name}_std_ready")
        self.rstd_ready = s.sem(f"{name}_rstd_ready")

    def tensor(self, pe, n, y, ones):
        pe.wait_ge(self.y_ready, n + 1)
        for k in range(KC):
            mm = pe.matmul(self.mean_ps, ones, y(k), start=(k == 0), stop=(k == KC - 1))
        mm.then_inc(self.mean_ready, 1)
        pe.wait_ge(self.sq_ready, n + 1)
        for k in range(KC):
            mm = pe.matmul(self.var_ps, ones, self.sq[:, k, :], start=(k == 0), stop=(k == KC - 1))
        mm.then_inc(self.var_ready, 1)

    def scalar(self, act, n, eps):
        act.wait_ge(self.d_ready, n + 1)
        act.activation(self.sq[:, :, :], self.d[:, :, :], ACT.Square).then_inc(self.sq_ready, 1)
        act.wait_ge(self.var_ready, n + 1)
        act.activation(self.rstd[:, :], self.var_ps, ACT.Sqrt, bias=eps).then_inc(self.std_ready, 1)

    def vector(self, dve, n, y, out):
        dve.wait_ge(self.mean_ready, n + 1)
        dve.tensor_tensor(self.d[:, :, :], y, over_chunks(self.mean_ps), ALU.subtract)\
           .then_inc(self.d_ready, 1)
        dve.wait_ge(self.std_ready, n + 1)
        dve.reciprocal(self.rstd[:, :], self.rstd[:, :]).then_inc(self.rstd_ready, 1)
        dve.wait_ge(self.rstd_ready, n + 1)
        return dve.tensor_tensor(out, self.d[:, :, :], over_chunks(self.rstd[:, :]), ALU.mult)


def recurrence_phase(nc, d, g):
    with Scope(nc) as s:
        w = {m: s.sb(f"rec_w_{m}", [P, KC, DIM]) for m in ("in", "gate", "lam", "out")}
        b = {m: s.sb(f"rec_b_{m}", [P, KC]) for m in ("in", "gate", "lam", "out")}
        gamma = s.sb("rec_gamma", [P, KC])
        beta = s.sb("rec_beta", [P, KC])
        inp = s.sb("rec_inp", [P, KC, NB])
        gate = s.sb("rec_gate", [P, KC, NB])
        lam = s.sb("rec_lam", [P, KC, NB])
        neg_u = s.sb("rec_neg_u", [P, KC, NB])
        hid = s.sb("rec_hid", [P, KC, NB])
        hn = s.sb("rec_hn", [P, KC, NB])
        hg = s.sb("rec_hg", [P, KC, NB])
        proj_ps = {m: s.ps(f"rec_ps_{m}", [P, KC, NB]) for m in ("in", "gate", "lam")}
        stat_ps = s.ps("rec_stat_ps", [P, 2, NB])
        out_ps = proj_ps["in"]
        loaded = s.sem("rec_loaded")
        proj = s.sem("rec_proj")
        act_done = s.sem("rec_act_done")
        neg_u_done = s.sem("rec_neg_u_done")
        lam_zeroed = s.sem("rec_lam_zeroed")
        affine = s.sem("rec_affine")
        hg_ready = s.sem("rec_hg_ready")
        out_ready = s.sem("rec_out_ready")
        x_done = s.sem("rec_x_done")
        ln_h = LayerNorm(s, "rec_lnh", stat_ps[:, 0, :], stat_ps[:, 1, :])
        LOADS = 12
        block = s.block()

        @block.sync
        def _(sp):
            sp.dma_start(g.xT[:, :, SHIFT:], d["xT"]).then_inc(loaded, 16)
            sp.dma_start(g.ctxT[:, :, :], d["ctxT"]).then_inc(loaded, 16)
            for m in ("in", "gate", "lam", "out"):
                sp.dma_start(w[m][:, :, :], d[f"rec_w_{m}"]).then_inc(loaded, 16)
                sp.dma_start(b[m][:, :], d[f"rec_b_{m}"]).then_inc(loaded, 16)
            sp.dma_start(gamma[:, :], d["rec_gamma"]).then_inc(loaded, 16)
            sp.dma_start(beta[:, :], d["rec_beta"]).then_inc(loaded, 16)

        @block.tensor
        def _(pe):
            pe.wait_ge(loaded, 16 * LOADS)
            pe.wait_ge(g.consts, 1)
            with pe.Fori(0, BLOCKS) as i:
                x_cols = bass.ds(SHIFT + i * NB, NB)
                pe.wait_ge(x_done, i + 1)
                for m in ("in", "gate", "lam"):
                    for o in range(KC):
                        for k in range(KC):
                            mm = pe.matmul(proj_ps[m][:, o, :], w[m][:, k, o * P:(o + 1) * P],
                                           g.xT[:, k, x_cols], start=(k == 0), stop=(k == KC - 1))
                    mm.then_inc(proj, 1)
                ln_h.tensor(pe, i, lambda k: hid[:, k, :], g.mean_mat[:, :])
                pe.wait_ge(hg_ready, i + 1)
                for o in range(KC):
                    for k in range(KC):
                        mm = pe.matmul(out_ps[:, o, :], w["out"][:, k, o * P:(o + 1) * P], hg[:, k, :],
                                       start=(k == 0), stop=(k == KC - 1))
                mm.then_inc(out_ready, 1)

        @block.scalar
        def _(act):
            act.wait_ge(loaded, 16 * LOADS)
            act.wait_ge(g.consts, 2)
            with act.Fori(0, BLOCKS) as i:
                act.wait_ge(x_done, i + 1)
                for n, (m, dst, f) in enumerate((("in", inp, ACT.Silu), ("gate", gate, ACT.Silu),
                                                 ("lam", lam, ACT.Sigmoid))):
                    act.wait_ge(proj, 3 * i + n + 1)
                    for o in range(KC):
                        a = act.activation(dst[:, o, :], proj_ps[m][:, o, :], f, bias=b[m][:, o:o + 1])
                    a.then_inc(act_done, 1)
                ln_h.scalar(act, i, g.eps[:, :])

        @block.vector
        def _(dve):
            dve.wait_ge(loaded, 16 * LOADS)
            dve.memset(g.xT[:, :, 0:SHIFT], 0.0)
            dve.sem_inc(x_done, 1)
            with dve.Fori(0, BLOCKS) as i:
                x_cols = bass.ds(SHIFT + i * NB, NB)
                dve.wait_ge(act_done, 3 * i + 3)
                dve.scalar_tensor_tensor(out=neg_u[:, :, :], in0=lam[:, :, :], scalar=1.0, in1=inp[:, :, :],
                                         op0=ALU.subtract, op1=ALU.mult).then_inc(neg_u_done, 1)
                dve.wait_ge(neg_u_done, i + 1)
                dve.memset(lam[:, :, :].rearrange("p k (t b) -> p k t b", b=BATCH)[:, :, :, 0:1], 0.0)\
                   .then_inc(lam_zeroed, 1)
                dve.wait_ge(lam_zeroed, i + 1)
                dve.tensor_tensor_scan(hid[:, :, :].rearrange("p k n -> p (k n)"),
                                       lam[:, :, :].rearrange("p k n -> p (k n)"),
                                       neg_u[:, :, :].rearrange("p k n -> p (k n)"),
                                       0.0, ALU.mult, ALU.subtract).then_inc(ln_h.y_ready, 1)
                ln_h.vector(dve, i, hid[:, :, :], hn[:, :, :]).then_inc(affine, 1)
                dve.wait_ge(affine, 2 * i + 1)
                for o in range(KC):
                    a = dve.tensor_scalar(hn[:, o, :], hn[:, o, :], gamma[:, o:o + 1], beta[:, o:o + 1],
                                          ALU.mult, ALU.add)
                a.then_inc(affine, 1)
                dve.wait_ge(affine, 2 * i + 2)
                dve.tensor_tensor(hg[:, :, :], hn[:, :, :], gate[:, :, :], ALU.mult).then_inc(hg_ready, 1)
                dve.wait_ge(out_ready, i + 1)
                for o in range(KC):
                    a = dve.scalar_tensor_tensor(out=g.xT[:, o, x_cols], in0=out_ps[:, o, :], scalar=b["out"][:, o:o + 1],
                                                 in1=g.xT[:, o, x_cols], op0=ALU.add, op1=ALU.add)
                a.then_inc(x_done, 1)

        @block.gpsimd
        def _(pool):
            pool.memset(g.mean_mat[:, :], 1.0 / DIM).then_inc(g.consts, 1)
            pool.memset(g.eps[:, :], LN_EPS).then_inc(g.consts, 1)


HID = 256
GATES = 4
SRC = 512
SC = SRC // P
QUARTERS = 4
QW = HID // QUARTERS
STRIP = P // BATCH
UNROLL = 4
TILES = TOK // P
GATE_W = GATES * HID
XROWS = TOK + UNROLL * BATCH


def quarters(ap):
    return ap.rearrange("p (j c) -> p j c", j=QUARTERS)


def attention_lstm_phase(nc, d, g, next_weights):
    xg_dram = nc.dram_tensor("xg_rows", [XROWS, GATE_W], F32, kind="Internal").ap()
    with Scope(nc) as s:
        w_attn = s.sb("lstm_w_attn", [P, KC, GATE_W])
        w_hid = s.sb("lstm_w_hid", [P, KC, GATE_W])
        w_out_h = s.sb("lstm_w_out_h", [P, KC, DIM])
        keys = s.sb("lstm_keys", [P, KC, TOK])
        values = s.sb("lstm_values", [P, BATCH * SC, DIM])
        ident = s.sb("lstm_ident", [P, P])
        sel_batch = s.sb("lstm_sel_batch", [P, BATCH])

        with Scope(nc) as q:
            w_x = q.sb("lstm_w_x", [P, KC, GATE_W])
            w_q = q.sb("lstm_w_q", [P, KC, HID])
            w_out_c = q.sb("lstm_w_out_c", [P, KC, DIM])
            b_out = q.sb("lstm_b_out", [P, DIM])
            b_x = q.sb("lstm_b_x", [P, GATE_W])
            b_h = q.sb("lstm_b_h", [P, GATE_W])
            x_tile = q.sb("lstm_x_tile", [P, 2, KC, P])
            xg_tile = q.sb("lstm_xg_tile", [P, 2, GATE_W])
            big_ps = q.ps("lstm_big_ps", [P, 2, NB])
            xg_ps = q.ps("lstm_xg_ps", [P, 2, GATE_W])
            loaded = q.sem("lstm_loaded")
            scaled = q.sem("lstm_scaled")
            bias_sum = q.sem("lstm_bias_sum")
            kv_ready = q.sem("lstm_kv_ready")
            keys_read = q.sem("lstm_keys_read")
            values_read = q.sem("lstm_values_read")
            x_copied = q.sem("lstm_x_copied")
            xg_ready = q.sem("lstm_xg_ready")
            xg_read = q.sem("lstm_xg_read")
            xg_stored = [q.sem(f"lstm_xg_stored{n}") for n in range(2)]
            bias_stored = q.sem("lstm_bias_stored")
            LOADS = 11
            block = q.block()

            @block.sync
            def _(sp):
                loads = [(w_q[:, :, :], d["lstm_w_q"]), (w_out_c[:, :, :], d["lstm_w_out_c"]),
                         (b_out[:, :], d["lstm_b_out"].partition_broadcast(P)),
                         (b_x[:, :], d["lstm_b_ih"].partition_broadcast(P)),
                         (b_h[:, :], d["lstm_b_hh"].partition_broadcast(P)),
                         (w_x[:, :, :], d["lstm_w_x"]), (w_attn[:, :, :], d["lstm_w_attn"]),
                         (w_hid[:, :, :], d["lstm_w_hid"]), (w_out_h[:, :, :], d["lstm_w_out_h"]),
                         (sel_batch[:, :], d["sel_batch"]),
                         (ident[:, :], d["ident"])]
                for dst, src in loads:
                    sp.dma_start(dst, src).then_inc(loaded, 16)
                assert len(loads) == LOADS
                sp.wait_ge(bias_sum, 2)
                sp.dma_start(xg_dram[TOK:XROWS, :], b_x[0:XROWS - TOK, :]).then_inc(bias_stored, 16)
                for u in range(2):
                    sp.sem_inc(xg_stored[u], 16)
                with sp.Fori(0, TILES // 2) as i:
                    for u in range(2):
                        sp.wait_ge(xg_read, 2 * i + u + 3)
                        sp.dma_start(xg_dram[bass.ds((2 * i + u) * P, P), :], xg_tile[:, u, :])\
                          .then_inc(xg_stored[u], 16)
                for u in range(2):
                    sp.wait_ge(xg_stored[u], 16 * (TILES // 2 + 1))
                sp.wait_ge(bias_stored, 16)

            @block.tensor
            def _(pe):
                pe.wait_ge(loaded, 16 * LOADS)
                n = 0
                for o in range(KC):
                    for b in range(BATCH):
                        if n >= 2:
                            pe.wait_ge(keys_read, n - 1)
                        for k in range(KC):
                            mm = pe.matmul(big_ps[:, n % 2, :], w_q[:, k, o * P:(o + 1) * P],
                                           g.ctxT[:, k, b * SRC:(b + 1) * SRC], start=(k == 0), stop=(k == KC - 1))
                        mm.then_inc(kv_ready, 1)
                        n += 1
                for c in range(BATCH * SC):
                    if c < 2:
                        pe.wait_ge(keys_read, n - 1)
                    else:
                        pe.wait_ge(values_read, c - 1)
                    for k in range(KC):
                        mm = pe.matmul(big_ps[:, n % 2, 0:DIM], g.ctxT[:, k, c * P:(c + 1) * P], w_out_c[:, k, :],
                                       start=(k == 0), stop=(k == KC - 1))
                    mm.then_inc(kv_ready, 1)
                    n += 1
                pe.wait_ge(scaled, 1)
                pe.sem_inc(xg_ready, 2)
                with pe.Fori(0, TILES // 2) as i:
                    for u in range(2):
                        pe.wait_ge(x_copied, 2 * i + u + 1)
                        pe.wait_ge(xg_read, 2 * i + 2)
                        for half in range(2):
                            for k in range(KC):
                                mm = pe.matmul(xg_ps[:, u, half * NB:(half + 1) * NB], x_tile[:, u, k, :],
                                               w_x[:, k, half * NB:(half + 1) * NB],
                                               start=(k == 0), stop=(k == KC - 1))
                        mm.then_inc(xg_ready, 1)

            @block.scalar
            def _(act):
                for n in range(KC * BATCH):
                    o, b = n // BATCH, n % BATCH
                    act.wait_ge(kv_ready, n + 1)
                    act.mul(keys[:, o, b * SRC:(b + 1) * SRC], big_ps[:, n % 2, :], 0.5).then_inc(keys_read, 1)

            @block.gpsimd
            def _(pool):
                with pool.Fori(0, TILES // 2) as i:
                    for u in range(2):
                        pool.wait_ge(xg_ready, 2 * i + 2)
                        pool.tensor_copy(x_tile[:, u, :, :], g.xT[:, :, bass.ds(SHIFT + (2 * i + u) * P, P)])\
                            .then_inc(x_copied, 1)

            @block.vector
            def _(dve):
                dve.wait_ge(loaded, 16 * LOADS)
                dve.tensor_tensor(b_x[:, :], b_x[:, :], b_h[:, :], ALU.add).then_inc(bias_sum, 1)
                for w, f in ((w_x, 0.5), (w_attn, 0.5), (w_hid, 0.25)):
                    for k in range(KC):
                        cols = quarters(w[:, k, :])[:, :, 0:3 * QW]
                        dve.tensor_scalar(cols, cols, f, None, ALU.mult)
                for k in range(KC):
                    cols = quarters(w_hid[:, k, :])[:, :, 3 * QW:]
                    dve.tensor_scalar(cols, cols, 0.5, None, ALU.mult)
                dve.tensor_scalar(w_out_h[:, :, :], w_out_h[:, :, :], 0.5, None, ALU.mult).then_inc(scaled, 1)
                dve.wait_ge(bias_sum, 1)
                cols = quarters(b_x[:, :])[:, :, 0:3 * QW]
                dve.tensor_scalar(cols, cols, 0.5, None, ALU.mult).then_inc(bias_sum, 1)
                for c in range(BATCH * SC):
                    n = KC * BATCH + c
                    dve.wait_ge(kv_ready, n + 1)
                    dve.tensor_tensor(values[:, c, :], big_ps[:, n % 2, 0:DIM], b_out[:, :], ALU.add).then_inc(values_read, 1)
                dve.wait_ge(bias_sum, 2)
                dve.sem_inc(xg_read, 2)
                with dve.Fori(0, TILES // 2) as i:
                    for u in range(2):
                        dve.wait_ge(xg_ready, 2 * i + u + 3)
                        dve.wait_ge(xg_stored[u], 16 * (i + 1))
                        dve.tensor_tensor(xg_tile[:, u, :], xg_ps[:, u, :], b_x[:, :], ALU.add).then_inc(xg_read, 1)

        HALF_SRC = SRC // 2
        with Scope(nc) as q:
            xg = q.sb("lstm_xg", [P, UNROLL, GATE_W])
            attn = q.sb("lstm_attn", [P, KC, BATCH])
            hid = q.sb("lstm_hid", [P, KC, STRIP])
            cell = q.sb("lstm_cell", [P, GATES + 1, QW])
            uv = q.sb("lstm_uv", [P, 2, QW])
            tanh_c = q.sb("lstm_tanh_c", [P, QW])
            h_row = q.sb("lstm_h_row", [P, QW])
            neg_max = q.sb("lstm_neg_max", [P, 2])
            neg_max_all = q.sb("lstm_neg_max_all", [P, 1])
            expo = q.sb("lstm_expo", [P, 2, HALF_SRC])
            total = q.sb("lstm_total", [P, 2])
            shrink = q.sb("lstm_shrink", [P, 2])
            shrunk = q.sb("lstm_shrunk", [P, 2])
            total_sum = q.sb("lstm_total_sum", [P, 1])
            inverse = q.sb("lstm_inverse", [P, 1])
            factor = q.sb("lstm_factor", [P, 2])
            first_row = q.sb("lstm_first_row", [P, DIM])
            alpha = q.sb("lstm_alpha", [P, SC, BATCH])
            out_row = q.sb("lstm_out_row", [P, DIM])
            ifg_ps = q.ps("lstm_ifg_ps", [P, NB])[:, 0:3 * QW]
            attn_banks = q.ps("lstm_attn_ps", [P, KC, NB])
            attn_ps = attn_banks[:, :, 0:BATCH]
            score_ps = q.ps("lstm_score_ps", [P, 2, NB])
            alpha_ps = q.ps("lstm_alpha_ps", [P, 2, HALF_SRC])
            out_ps = q.ps("lstm_out_ps", [P, 2, NB])
            o_gate_ps = out_ps[:, 0, DIM:DIM + QW]
            xg_zeroed = q.sem("lstm_xg_zeroed")
            zeroed = q.sem("lstm_zeroed")
            xg_loaded = [q.sem(f"lstm_xg_loaded{n}") for n in range(UNROLL)]
            xg_used = q.sem("lstm_xg_used")
            ifg_ready = q.sem("lstm_ifg_ready")
            ifg_tanh = q.sem("lstm_ifg_tanh")
            o_ready = q.sem("lstm_o_ready")
            o_tanh = q.sem("lstm_o_tanh")
            uv_ready = q.sem("lstm_uv_ready")
            c_ready = q.sem("lstm_c_ready")
            c_tanh = q.sem("lstm_c_tanh")
            h_row_ready = q.sem("lstm_h_row_ready")
            h_ready = q.sem("lstm_h_ready")
            scores_ready = q.sem("lstm_scores_ready")
            max_ready = q.sem("lstm_max_ready")
            exp_ready = q.sem("lstm_exp_ready")
            max_all_ready = q.sem("lstm_max_all_ready")
            shrink_ready = q.sem("lstm_shrink_ready")
            shrunk_ready = q.sem("lstm_shrunk_ready")
            factor_ready = q.sem("lstm_factor_ready")
            first_row_ready = q.sem("lstm_first_row_ready")
            total_ready = q.sem("lstm_total_ready")
            inverse_ready = q.sem("lstm_inverse_ready")
            alpha_turned = q.sem("lstm_alpha_turned")
            alpha_ready = q.sem("lstm_alpha_ready")
            out_ready = q.sem("lstm_out_ready")
            out_row_ready = q.sem("lstm_out_row_ready")
            attn_turned = q.sem("lstm_attn_turned")
            attn_ready = q.sem("lstm_attn_ready")
            attn_kept = q.sem("lstm_attn_kept")
            block = q.block()

            def x_rows(t):
                return xg_dram[bass.ds(t * BATCH, BATCH), :]

            @block.sync
            def _(sp):
                sp.wait_ge(xg_zeroed, 1)
                for u in range(UNROLL):
                    sp.dma_start(xg[0:BATCH, u, :], x_rows(u)).then_inc(xg_loaded[u], 16)
                for ei in range(2):
                    next_weights.load(sp, ei)
                with sp.Fori(0, SEQ // UNROLL) as i:
                    for u in range(UNROLL):
                        t = i * UNROLL + u
                        sp.wait_ge(xg_used, t + 1)
                        sp.dma_start(xg[0:BATCH, u, :], x_rows(t + UNROLL)).then_inc(xg_loaded[u], 16)
                for u in range(UNROLL):
                    sp.wait_ge(xg_loaded[u], 16 * (SEQ // UNROLL + 1))

            @block.tensor
            def _(pe):
                def rows_of(ps, j):
                    return ps[j * STRIP:j * STRIP + BATCH, :]

                def ifg(j):
                    return slice(j * HID + QW, (j + 1) * HID)

                def o_gate(j):
                    return slice(j * HID, j * HID + QW)

                def x_part(u):
                    for j in range(QUARTERS):
                        pe.matmul(rows_of(ifg_ps, j), ident[:, 0:BATCH], xg[:, u % UNROLL, ifg(j)],
                                  start=True, stop=False)

                def gate_part(u, w, col, k, last):
                    for j in range(QUARTERS):
                        mm = pe.matmul(rows_of(ifg_ps, j), col[:, k, 0:BATCH], w[:, k, ifg(j)],
                                       start=False, stop=last)
                    return mm

                def o_sums(u):
                    for j in range(QUARTERS):
                        mm = pe.matmul(rows_of(o_gate_ps, j), ident[:, 0:BATCH], xg[:, u, o_gate(j)], start=True, stop=False)
                    mm.then_inc(xg_used, 1)
                    for w, col in ((w_hid, hid), (w_attn, attn)):
                        for k in range(KC):
                            for j in range(QUARTERS):
                                mm = pe.matmul(rows_of(o_gate_ps, j), col[:, k, 0:BATCH], w[:, k, o_gate(j)],
                                               start=False, stop=w is w_attn and k == KC - 1)
                    mm.then_inc(o_ready, 1)

                def batch_rows(ps, n, b):
                    return ps[b * STRIP:b * STRIP + 1, 0:n]

                def output_part(o, k):
                    pe.matmul(attn_ps[:, o, :], w_out_h[:, k, o * P:(o + 1) * P], hid[:, k, 0:BATCH],
                              start=(k == 0), stop=False)

                def turn(t, half):
                    pe.wait_ge(exp_ready, 2 * t + half + 1)
                    for c in range(2):
                        mm = pe.transpose(alpha_ps[:, half, c * P:(c + 1) * P], expo[:, half, c * P:(c + 1) * P], ident[:, :])
                    mm.then_inc(alpha_turned, 1)

                def context_part(half, n):
                    c = 2 * half + n
                    for b in range(BATCH):
                        mm = pe.matmul(batch_rows(out_ps[:, half, :], DIM, b), alpha[:, c, b:b + 1],
                                       values[:, b * SC + c, :], start=(n == 0), stop=(n == 1))
                    return mm

                pe.wait_ge(zeroed, 1)
                pe.wait_ge(xg_loaded[0], 16)
                x_part(0)
                for k in range(KC):
                    gate_part(0, w_hid, hid, k, False)
                with pe.Fori(0, SEQ // UNROLL) as i:
                    for u in range(UNROLL):
                        t = i * UNROLL + u
                        pe.wait_ge(attn_ready, t + 1)
                        gate_part(u, w_attn, attn, 0, False)
                        gate_part(u, w_attn, attn, 1, True).then_inc(ifg_ready, 1)
                        o_sums(u)
                        nxt = (u + 1) % UNROLL
                        pe.wait_ge(xg_loaded[nxt], 16 * (i + (2 if nxt == 0 else 1)))
                        pe.wait_ge(ifg_tanh, t + 1)
                        x_part(u + 1)
                        pe.wait_ge(h_ready, t + 1)
                        for half in range(2):
                            for k in range(KC):
                                for b in range(BATCH):
                                    lo = b * SRC + half * HALF_SRC
                                    mm = pe.matmul(batch_rows(score_ps[:, half, :], HALF_SRC, b), hid[:, k, b:b + 1],
                                                   keys[:, k, lo:lo + HALF_SRC], start=(k == 0), stop=(k == KC - 1))
                            mm.then_inc(scores_ready, 1)
                        output_part(0, 0)
                        turn(t, 0)
                        output_part(0, 1)
                        output_part(1, 0)
                        pe.wait_ge(alpha_ready, 2 * t + 1)
                        context_part(0, 0)
                        turn(t, 1)
                        context_part(0, 1).then_inc(out_ready, 1)
                        pe.wait_ge(alpha_ready, 2 * t + 2)
                        context_part(1, 0)
                        context_part(1, 1).then_inc(out_ready, 1)
                        output_part(1, 1)
                        gate_part(u + 1, w_hid, hid, 0, False)
                        for o in range(KC):
                            pe.wait_ge(out_row_ready, 2 * t + o + 1)
                            mm = pe.matmul(attn_ps[:, o, :], out_row[:, o * P:(o + 1) * P], sel_batch[:, :],
                                           start=False, stop=True)
                        mm.then_inc(attn_turned, 1)
                        gate_part(u + 1, w_hid, hid, 1, False)
                pe.wait_ge(attn_ready, SEQ + 1)
                for k in range(KC):
                    gate_part(SEQ, w_attn, attn, k, k == KC - 1)

            @block.scalar
            def _(act):
                act.wait_ge(zeroed, 1)
                act.activation(tanh_c[:, :], cell[:, GATES, :], ACT.Tanh)
                act.sem_inc(attn_ready, 1)
                with act.Fori(0, SEQ // UNROLL) as i:
                    for u in range(UNROLL):
                        t = i * UNROLL + u
                        act.wait_ge(ifg_ready, t + 1)
                        act.activation(cell[:, 1:GATES, :].rearrange("p n q -> p (n q)"), ifg_ps, ACT.Tanh)\
                           .then_inc(ifg_tanh, 1)
                        act.wait_ge(o_ready, t + 1)
                        act.activation(cell[:, 0, :], o_gate_ps, ACT.Tanh).then_inc(o_tanh, 1)
                        act.wait_ge(c_ready, t + 1)
                        act.activation(tanh_c[:, :], cell[:, GATES, :], ACT.Tanh, scale=0.5).then_inc(c_tanh, 1)
                        for half in range(2):
                            act.wait_ge(max_ready, 2 * t + half + 1)
                            act.activation(expo[:, half, :], score_ps[:, half, 0:HALF_SRC], ACT.Exp, bias=neg_max[:, half:half + 1],
                                           accum_out=total[:, half:half + 1]).then_inc(exp_ready, 1)
                        act.wait_ge(max_all_ready, t + 1)
                        act.activation(shrink[:, :], neg_max[:, :], ACT.Exp, scale=-1.0, bias=neg_max_all[:, :])\
                           .then_inc(shrink_ready, 1)
                        act.wait_ge(attn_turned, t + 1)
                        act.wait_ge(attn_kept, t + 1)
                        act.activation(attn[:, :, :], attn_ps, ACT.Tanh).then_inc(attn_ready, 1)

            @block.vector
            def _(dve):
                def keep_turned(t, half):
                    dve.wait_ge(alpha_turned, 2 * t + half + 1)
                    turned = alpha_ps[:, half, :].rearrange("p (c b r) -> p c b r", b=BATCH, r=STRIP)
                    dve.tensor_copy(alpha[:, 2 * half:2 * half + 2, :], turned[:, :, :, 0]).then_inc(alpha_ready, 1)

                for ps in (ifg_ps, score_ps[:, :, :], out_ps[:, :, :]):
                    dve.memset(ps, 0.0)
                dve.memset(cell[:, :, :], 0.0)
                dve.memset(hid[:, :, :], 0.0)
                dve.memset(attn[:, :, :], 0.0).then_inc(zeroed, 1)
                with dve.Fori(0, SEQ // UNROLL) as i:
                    for u in range(UNROLL):
                        t = i * UNROLL + u
                        dve.wait_ge(ifg_tanh, t + 1)
                        dve.scalar_tensor_tensor(out=uv[:, :, :], in0=cell[:, 1:3, :], scalar=1.0,
                                                 in1=cell[:, 3:5, :], op0=ALU.add, op1=ALU.mult).then_inc(uv_ready, 1)
                        dve.wait_ge(uv_ready, t + 1)
                        dve.scalar_tensor_tensor(out=cell[:, GATES, :], in0=uv[:, 1, :], scalar=0.5,
                                                 in1=uv[:, 0, :], op0=ALU.mult, op1=ALU.add).then_inc(c_ready, 1)
                        dve.wait_ge(c_tanh, t + 1)
                        dve.wait_ge(o_tanh, t + 1)
                        dve.scalar_tensor_tensor(out=h_row[:, :], in0=cell[:, 0, :], scalar=1.0,
                                                 in1=tanh_c[:, :], op0=ALU.add, op1=ALU.mult).then_inc(h_row_ready, 1)
                        dve.wait_ge(h_row_ready, t + 1)
                        dve.transpose(hid[:, :, :], h_row[:, :].rearrange("p (k c) -> p k c", k=KC)).then_inc(h_ready, 1)
                        for half in range(2):
                            dve.wait_ge(scores_ready, 2 * t + half + 1)
                            dve.tensor_reduce(neg_max[:, half:half + 1], score_ps[:, half, 0:HALF_SRC], AX_X, ALU.max, negate=True)\
                               .then_inc(max_ready, 1)
                        keep_turned(t, 0)
                        dve.wait_ge(max_ready, 2 * t + 2)
                        dve.tensor_tensor(neg_max_all[:, :], neg_max[:, 0:1], neg_max[:, 1:2], ALU.min).then_inc(max_all_ready, 1)
                        dve.wait_ge(shrink_ready, t + 1)
                        dve.tensor_tensor(shrunk[:, :], total[:, :], shrink[:, :], ALU.mult).then_inc(shrunk_ready, 1)
                        dve.wait_ge(shrunk_ready, t + 1)
                        dve.tensor_tensor(total_sum[:, :], shrunk[:, 0:1], shrunk[:, 1:2], ALU.add).then_inc(total_ready, 1)
                        keep_turned(t, 1)
                        dve.wait_ge(total_ready, t + 1)
                        dve.reciprocal(inverse[:, :], total_sum[:, :]).then_inc(inverse_ready, 1)
                        dve.wait_ge(inverse_ready, t + 1)
                        dve.tensor_scalar(factor[:, :], shrink[:, :], inverse[:, 0:1], None, ALU.mult).then_inc(factor_ready, 1)
                        dve.wait_ge(out_ready, 2 * t + 1)
                        dve.wait_ge(factor_ready, t + 1)
                        dve.tensor_scalar(first_row[:, :], out_ps[:, 0, 0:DIM], factor[:, 0:1], None, ALU.mult)\
                           .then_inc(first_row_ready, 1)
                        dve.wait_ge(out_ready, 2 * t + 2)
                        dve.wait_ge(first_row_ready, t + 1)
                        for k in range(KC):
                            cols = slice(k * P, (k + 1) * P)
                            dve.scalar_tensor_tensor(out=out_row[:, cols], in0=out_ps[:, 1, cols], scalar=factor[:, 1:2],
                                                     in1=first_row[:, cols], op0=ALU.mult, op1=ALU.add).then_inc(out_row_ready, 1)

            @block.gpsimd
            def _(pool):
                pool.memset(xg[:, :, :], 0.0).then_inc(xg_zeroed, 1)
                pool.sem_inc(attn_kept, 1)
                with pool.Fori(0, SEQ // UNROLL) as i:
                    for u in range(UNROLL):
                        t = i * UNROLL + u
                        cols = g.xT[:, :, bass.ds(SHIFT + t * BATCH, BATCH)]
                        pool.wait_ge(attn_ready, t + 2)
                        pool.tensor_tensor(cols, cols, attn[:, :, :], ALU.add).then_inc(attn_kept, 1)


def norm_phase(nc, g, name, out=None):
    with Scope(nc) as s:
        stat_ps = s.ps(f"{name}_stat_ps", [P, BLOCKS, 2, NB])
        d = s.sb(f"{name}_d", [P, BLOCKS, KC, NB])
        sq = s.sb(f"{name}_sq", [P, BLOCKS, KC, NB])
        rstd = s.sb(f"{name}_rstd", [P, BLOCKS, NB])
        mean_ready = s.sem(f"{name}_mean_ready")
        d_ready = s.sem(f"{name}_d_ready")
        sq_ready = s.sem(f"{name}_sq_ready")
        var_ready = s.sem(f"{name}_var_ready")
        std_ready = s.sem(f"{name}_std_ready")
        rstd_ready = s.sem(f"{name}_rstd_ready")
        x_done = s.sem(f"{name}_x_done")
        stored = s.sem(f"{name}_stored")
        block = s.block()

        def x_cols(i):
            return g.xT[:, :, SHIFT + i * NB:SHIFT + (i + 1) * NB]

        @block.sync
        def _(sp):
            if out is not None:
                for i in range(BLOCKS):
                    sp.wait_ge(x_done, i + 1)
                    sp.dma_start(out[:, :, i * NB:(i + 1) * NB], x_cols(i)).then_inc(stored, 16)
                sp.wait_ge(stored, 16 * BLOCKS)

        @block.tensor
        def _(pe):
            def mean_of(ps, of, ready):
                for k in range(KC):
                    mm = pe.matmul(ps, g.mean_mat[:, :], of[:, k, :], start=(k == 0), stop=(k == KC - 1))
                mm.then_inc(ready, 1)

            for i in range(BLOCKS):
                mean_of(stat_ps[:, i, 0, :], x_cols(i), mean_ready)
            for i in range(BLOCKS):
                pe.wait_ge(sq_ready, i + 1)
                mean_of(stat_ps[:, i, 1, :], sq[:, i, :, :], var_ready)

        @block.scalar
        def _(act):
            for i in range(BLOCKS):
                act.wait_ge(d_ready, i + 1)
                act.activation(sq[:, i, :, :], d[:, i, :, :], ACT.Square).then_inc(sq_ready, 1)
            for i in range(BLOCKS):
                act.wait_ge(var_ready, i + 1)
                act.activation(rstd[:, i, :], stat_ps[:, i, 1, :], ACT.Sqrt, bias=g.eps[:, :]).then_inc(std_ready, 1)

        @block.vector
        def _(dve):
            for i in range(BLOCKS):
                dve.wait_ge(mean_ready, i + 1)
                dve.tensor_tensor(d[:, i, :, :], x_cols(i), over_chunks(stat_ps[:, i, 0, :]), ALU.subtract).then_inc(d_ready, 1)
            for i in range(BLOCKS):
                dve.wait_ge(std_ready, i + 1)
                dve.reciprocal(rstd[:, i, :], rstd[:, i, :]).then_inc(rstd_ready, 1)
                dve.wait_ge(rstd_ready, i + 1)
                dve.tensor_tensor(x_cols(i), d[:, i, :, :], over_chunks(rstd[:, i, :]), ALU.mult).then_inc(x_done, 1)


TOP = 2
TB = NB // P


class Router:

    def __init__(self, s, name, experts, softmax_first, rows_ps, cols_ps):
        E = self.n = experts
        self.softmax_first = softmax_first
        self.rows_ps, self.cols_ps = rows_ps, cols_ps
        self.logit_rows = s.sb(f"{name}_logit_rows", [E, NB])
        self.logits = s.sb(f"{name}_logits", [P, TB, E])
        self.expo = s.sb(f"{name}_expo", [P, TB, E])
        self.above = s.sb(f"{name}_above", [P, TB, E, E])
        self.same = s.sb(f"{name}_same", [P, TB, E, E])
        self.before = s.sb(f"{name}_before", [P, E, E])
        self.rank = s.sb(f"{name}_rank", [P, TB, E])
        self.total = s.sb(f"{name}_total", [P, TB])
        self.weights = s.sb(f"{name}_weights", [P, TB, E])
        self.weight_rows = s.sb(f"{name}_weight_rows", [E, TOK])
        self.filled = s.sem(f"{name}_filled")
        self.logit_rows_summed = s.sem(f"{name}_logit_rows_summed")
        self.logit_rows_ready = s.sem(f"{name}_logit_rows_ready")
        self.logits_turned = s.sem(f"{name}_logits_turned")
        self.shifted = s.sem(f"{name}_shifted")
        self.expo_ready = s.sem(f"{name}_expo_ready")
        self.step = s.sem(f"{name}_step")
        self.weights_ready = s.sem(f"{name}_weights_ready")
        self.weights_turned = s.sem(f"{name}_weights_turned")
        self.weight_rows_ready = s.sem(f"{name}_weight_rows_ready")
        self.STEPS = 14 if softmax_first else 10

    def gpsimd(self, pool):
        pool.memset(self.before[:, :, :], 0.0).then_inc(self.filled, 1)
        pool.wait_ge(self.filled, 1)
        for e in range(1, self.n):
            ins = pool.memset(self.before[:, e, 0:e], 1.0)
        ins.then_inc(self.filled, 1)

    def sum_logits(self, pe, n, w, x):
        for k in range(KC):
            mm = pe.matmul(self.rows_ps, w[:, k, :], x(k), start=(k == 0), stop=(k == KC - 1))
        mm.then_inc(self.logit_rows_summed, 1)

    def turn_logits(self, pe, n, ident):
        pe.wait_ge(self.logit_rows_ready, n + 1)
        for c in range(TB):
            mm = pe.matmul(self.cols_ps[:, c, :], self.logit_rows[:, c * P:(c + 1) * P],
                           ident[0:self.n, 0:self.n], start=True, stop=True)
        mm.then_inc(self.logits_turned, 1)

    def turn_weights(self, pe, n, ident):
        pe.wait_ge(self.weights_ready, n + 1)
        for c in range(TB):
            mm = pe.matmul(self.rows_ps[:, c * P:(c + 1) * P], self.weights[:, c, :], ident, start=True, stop=True)
        mm.then_inc(self.weights_turned, 1)

    def keep_logits(self, act, n, bias):
        act.wait_ge(self.logit_rows_summed, n + 1)
        act.activation(self.logit_rows[:, :], self.rows_ps, ACT.Identity, bias=bias).then_inc(self.logit_rows_ready, 1)

    def keep_weights(self, act, n):
        act.wait_ge(self.shifted, n + 1)
        act.activation(self.expo[:, :, :], self.expo[:, :, :], ACT.Exp).then_inc(self.expo_ready, 1)
        act.wait_ge(self.weights_turned, n + 1)
        act.copy(self.weight_rows[:, bass.ds(n * NB, NB)], self.rows_ps).then_inc(self.weight_rows_ready, 1)

    def vector(self, dve, n):
        E, at = self.n, [0]

        def then(ins):
            at[0] += 1
            ins.then_inc(self.step, 1)
            dve.wait_ge(self.step, n * self.STEPS + at[0])

        def spread(ap):
            return ap.unsqueeze(2).to_broadcast([P, TB, E])

        def own(ap):
            return ap.unsqueeze(3).to_broadcast([P, TB, E, E])

        def other(ap):
            return ap.unsqueeze(2).to_broadcast([P, TB, E, E])

        dve.wait_ge(self.logits_turned, n + 1)
        then(dve.tensor_copy(self.logits[:, :, :], self.cols_ps))
        then(dve.tensor_reduce(self.total[:, :], self.logits[:, :, :], AX_X, ALU.max))
        dve.tensor_tensor(self.expo[:, :, :], self.logits[:, :, :], spread(self.total[:, :]), ALU.subtract)\
           .then_inc(self.shifted, 1)
        dve.wait_ge(self.expo_ready, n + 1)
        if self.softmax_first:
            then(dve.tensor_reduce(self.total[:, :], self.expo[:, :, :], AX_X, ALU.add))
            then(dve.reciprocal(self.total[:, :], self.total[:, :]))
            then(dve.tensor_tensor(self.expo[:, :, :], self.expo[:, :, :], spread(self.total[:, :]), ALU.mult))
        ranked = self.expo[:, :, :] if self.softmax_first else self.logits[:, :, :]
        dve.tensor_tensor(self.above[:, :, :, :], other(ranked), own(ranked), ALU.is_gt)
        then(dve.tensor_tensor(self.same[:, :, :, :], other(ranked), own(ranked), ALU.is_equal))
        then(dve.tensor_tensor(self.same[:, :, :, :], self.same[:, :, :, :],
                               self.before[:, :, :].unsqueeze(1).to_broadcast([P, TB, E, E]), ALU.mult))
        then(dve.tensor_tensor(self.above[:, :, :, :], self.above[:, :, :, :], self.same[:, :, :, :], ALU.add))
        then(dve.tensor_reduce(self.rank[:, :, :], self.above[:, :, :, :], AX_X, ALU.add))
        then(dve.tensor_scalar(self.rank[:, :, :], self.rank[:, :, :], float(TOP), None, ALU.is_lt))
        then(dve.tensor_tensor(self.weights[:, :, :], self.rank[:, :, :], self.expo[:, :, :], ALU.mult))
        then(dve.tensor_reduce(self.total[:, :], self.weights[:, :, :], AX_X, ALU.add))
        if self.softmax_first:
            then(dve.tensor_scalar(self.total[:, :], self.total[:, :], 1e-20, None, ALU.add))
        then(dve.reciprocal(self.total[:, :], self.total[:, :]))
        dve.tensor_tensor(self.weights[:, :, :], self.weights[:, :, :], spread(self.total[:, :]), ALU.mult)\
           .then_inc(self.weights_ready, 1)
        assert at[0] == self.STEPS


class Experts:

    def __init__(self, name, routed, shared, inner, softmax_first):
        self.name, self.routed, self.softmax_first, self.inner = name, routed, softmax_first, inner
        self.order = [routed] * shared + list(range(routed))
        self.chunks = -(-inner // P)
        self.rows = -(-inner // self.chunks)
        self.last_rows = inner - (self.chunks - 1) * self.rows

    def rows_of(self, c):
        return self.rows if c < self.chunks - 1 else self.last_rows


class RawWeights:

    LOADS = 4

    def __init__(self, s, d, x):
        self.d, self.x = d, x
        self.gu = s.sb(f"{x.name}_raw_gu", [P, 2, 2, KC * x.inner])
        self.down = s.sb(f"{x.name}_raw_down", [P, 2, x.chunks * DIM])
        self.loaded = [s.sem(f"{x.name}_raw_loaded{n}") for n in range(2)]

    def load(self, sp, ei):
        x, buf, e = self.x, ei % 2, self.x.order[ei]
        for m, name in enumerate(("gate", "up")):
            sp.dma_start(self.gu[:, buf, m, :].rearrange("p (k n) -> p k n", k=KC), self.d[f"{x.name}_w_{name}"][e])\
              .then_inc(self.loaded[buf], 16)
        full = (x.chunks - 1) * x.rows
        down = self.d[f"{x.name}_w_down"][e]
        kept = self.down[:, buf, :].rearrange("p (c n) -> p c n", c=x.chunks)
        sp.dma_start(kept[0:x.rows, 0:x.chunks - 1, :], down[0:full, :].rearrange("(c p) n -> p c n", p=x.rows))\
          .then_inc(self.loaded[buf], 16)
        sp.dma_start(kept[0:x.last_rows, x.chunks - 1, :], down[full:x.inner, :]).then_inc(self.loaded[buf], 16)


def mixture_phase(nc, d, g, x, raw):
    E, IC, INNER = x.routed, x.chunks, x.inner
    PAIRS = BLOCKS // 2
    NP = 2 * IC
    HI, LO = range(2)
    with Scope(nc) as s:
        w_router = s.sb(f"{x.name}_w_router", [P, KC, E])
        b_router = s.sb(f"{x.name}_b_router", [E, 1])
        pick = s.sb(f"{x.name}_pick", [E, E, P])
        ident = s.sb(f"{x.name}_ident", [P, P])
        w_gu = s.sb(f"{x.name}_w_gu", [P, 2, 2, 2, KC * INNER], F32R)
        w_down = s.sb(f"{x.name}_w_down", [P, 2, 2, IC * DIM], F32R)
        x_in = s.sb(f"{x.name}_x_in", [P, 2, KC, TOK], F32R)
        gu = s.sb(f"{x.name}_gu", [P, 2, NB])
        gu_in = s.sb(f"{x.name}_gu_in", [P, 2, 2, NB], F32R)
        spread = s.sb(f"{x.name}_spread", [P, NB])
        part = s.sb(f"{x.name}_part", [P, KC, NB])
        gate_ps = s.ps(f"{x.name}_gate_ps", [P, 2, NB])
        up_ps = s.ps(f"{x.name}_up_ps", [P, 2, NB])
        down_ps = s.ps(f"{x.name}_down_ps", [P, KC, NB])
        aux_ps = s.ps(f"{x.name}_aux_ps", [P, 2, NB])
        loaded = s.sem(f"{x.name}_loaded")
        zeroed = s.sem(f"{x.name}_zeroed")
        w_hi = s.sem(f"{x.name}_w_hi")
        gu_w_lo = s.sem(f"{x.name}_gu_w_lo")
        down_w_lo = s.sem(f"{x.name}_down_w_lo")
        x_hi = s.sem(f"{x.name}_x_hi")
        x_lo = s.sem(f"{x.name}_x_lo")
        gate_ready = s.sem(f"{x.name}_gate_ready")
        up_ready = s.sem(f"{x.name}_up_ready")
        silu_ready = s.sem(f"{x.name}_silu_ready")
        gu_ready = s.sem(f"{x.name}_gu_ready")
        gu_hi = s.sem(f"{x.name}_gu_hi")
        gu_lo = s.sem(f"{x.name}_gu_lo")
        spread_turned = s.sem(f"{x.name}_spread_turned")
        spread_ready = s.sem(f"{x.name}_spread_ready")
        down_ready = s.sem(f"{x.name}_down_ready")
        down_used = s.sem(f"{x.name}_down_used")
        x_done = s.sem(f"{x.name}_x_done")
        router = Router(s, f"{x.name}_router", E, x.softmax_first, aux_ps[0:E, 0, :],
                        aux_ps[:, 1, 0:TB * E].rearrange("p (c e) -> p c e", e=E))
        spread_ps = aux_ps[:, 1, :]
        block = s.block()
        LOADS = 4 if f"{x.name}_b_router" in d else 3

        def down_parts(ap):
            full = (IC - 1) * DIM
            return ap[0:x.rows, 0:full], ap[0:x.last_rows, full:]

        def weighted(ei):
            return x.order[ei] < E

        def before(ei):
            return sum(weighted(n) for n in range(ei))

        def x_cols(i):
            return g.xT[:, :, bass.ds(SHIFT + i * NB, NB)]

        @block.sync
        def _(sp):
            sp.dma_start(w_router[:, :, :], d[f"{x.name}_w_router"]).then_inc(loaded, 16)
            sp.dma_start(pick[:, :, :], d["pick"][0:E, 0:E, :]).then_inc(loaded, 16)
            sp.dma_start(ident[:, :], d["ident"]).then_inc(loaded, 16)
            if LOADS == 4:
                sp.dma_start(b_router[:, :], d[f"{x.name}_b_router"]).then_inc(loaded, 16)
            for ei in range(2, len(x.order)):
                sp.wait_ge(gu_w_lo, 2 * (ei - 1))
                sp.wait_ge(down_w_lo, ei - 1)
                raw.load(sp, ei)

        @block.tensor
        def _(pe):
            PASSES = ((HI, HI), (HI, LO), (LO, HI))

            pe.wait_ge(loaded, 16 * LOADS)
            for ei, e in enumerate(x.order):
                buf = ei % 2

                def up_and_gate(i, n, gn):
                    c = n % IC
                    m = x.rows_of(c)
                    pe.wait_ge(gu_ready, gn + 1)
                    for which, ps, ready in ((0, gate_ps, gate_ready), (1, up_ps, up_ready)):
                        for w_part, x_part in PASSES:
                            for k in range(KC):
                                lo = k * INNER + c * x.rows
                                mm = pe.matmul(ps[0:m, n % 2, :], w_gu[:, buf, w_part, which, lo:lo + m],
                                               x_in[:, x_part, k, bass.ds(i * NB, NB)],
                                               start=(w_part == HI and x_part == HI and k == 0),
                                               stop=(w_part == LO and k == KC - 1))
                        mm.then_inc(ready, 1)

                def down(n, gn, blk):
                    c = n % IC
                    m = x.rows_of(c)
                    if c == 0:
                        pe.wait_ge(down_used, blk + 1)
                    pe.wait_ge(gu_hi, gn + 1)
                    for w_part, x_part in ((HI, HI), (LO, HI), (HI, LO)):
                        if x_part == LO:
                            pe.wait_ge(gu_lo, gn + 3)
                        for o in range(KC):
                            lo = c * DIM + o * P
                            mm = pe.matmul(down_ps[:, o, :], w_down[0:m, buf, w_part, lo:lo + P], gu_in[0:m, n % 2, x_part, :],
                                           start=(c == 0 and w_part == HI and x_part == HI),
                                           stop=(c == IC - 1 and x_part == LO))
                    if c == IC - 1:
                        mm.then_inc(down_ready, 1)

                def spread_weights(i, blk):
                    pe.wait_ge(spread_ready, blk + 1)
                    pe.matmul(spread_ps, pick[:, e, :], router.weight_rows[:, bass.ds(i * NB, NB)], start=True, stop=True)\
                      .then_inc(spread_turned, 1)

                pe.wait_ge(gu_w_lo, 2 * (ei + 1))
                pe.wait_ge(down_w_lo, ei + 1)
                with pe.Fori(0, PAIRS) as ii:
                    for u in range(2):
                        i = 2 * ii + u
                        blk = ei * BLOCKS + i
                        w_blk = before(ei) * BLOCKS + i
                        if ei == 0:
                            pe.wait_ge(x_lo, i + 1)
                        elif weighted(ei):
                            spread_weights(i, w_blk)
                        for c in range(IC):
                            n = u * IC + c
                            gn = (ei * PAIRS + ii) * NP + n
                            up_and_gate(i, n, gn)
                            if n > 0 and (ei > 0 or c > 0):
                                down(n - 1, gn - 1, blk if c > 0 else blk - 1)
                            if ei == 0 and c == 0:
                                router.sum_logits(pe, i, w_router, lambda k: g.xT[:, k, bass.ds(SHIFT + i * NB, NB)])
                            if ei == 0 and c == 1:
                                router.turn_logits(pe, i, ident[:, :])
                        if u == 1 or ei == 0:
                            down(u * IC + IC - 1, (ei * PAIRS + ii) * NP + u * IC + IC - 1, blk)
                        if ei == 0:
                            router.turn_weights(pe, i, ident[:, :])
                            pe.wait_ge(router.weight_rows_ready, i + 1)
                            if weighted(0):
                                spread_weights(i, w_blk)

        @block.scalar
        def _(act):
            def split_weights(ei):
                buf = ei % 2
                act.wait_ge(raw.loaded[buf], 16 * raw.LOADS * (ei // 2 + 1))
                for m in range(2):
                    act.copy(w_gu[:, buf, HI, m, :], raw.gu[:, buf, m, :]).then_inc(w_hi, 1)
                for high, of in zip(down_parts(w_down[:, buf, HI, :]), down_parts(raw.down[:, buf, :])):
                    ins = act.copy(high, of)
                ins.then_inc(w_hi, 1)

            split_weights(0)
            act.wait_ge(loaded, 16 * LOADS)
            act.wait_ge(zeroed, 1)
            act.sem_inc(spread_ready, 1)
            for ei in range(len(x.order)):
                def keep_spread(i):
                    w_blk = before(ei) * BLOCKS + i
                    act.wait_ge(spread_turned, w_blk + 1)
                    act.wait_ge(down_used, ei * BLOCKS + i + 1)
                    act.copy(spread[:, :], spread_ps).then_inc(spread_ready, 1)

                if ei + 1 < len(x.order):
                    if ei > 0:
                        act.wait_ge(down_used, ei * BLOCKS + 1)
                    split_weights(ei + 1)
                with act.Fori(0, PAIRS) as ii:
                    for u in range(2):
                        i = 2 * ii + u
                        for c in range(IC):
                            n = u * IC + c
                            m = x.rows_of(c)
                            gn = (ei * PAIRS + ii) * NP + n
                            act.wait_ge(gu_lo, gn + 1)
                            act.wait_ge(gate_ready, gn + 1)
                            act.activation(gu[0:m, n % 2, :], gate_ps[0:m, n % 2, :], ACT.Silu).then_inc(silu_ready, 1)
                            if ei == 0 and c == 0:
                                router.keep_logits(act, i, b_router[:, :])
                            if ei > 0 and weighted(ei) and c == 1:
                                keep_spread(i)
                        if ei == 0:
                            router.keep_weights(act, i)
                            if weighted(ei):
                                keep_spread(i)

        @block.vector
        def _(dve):
            def split_weights(ei):
                buf = ei % 2
                for m in range(2):
                    dve.wait_ge(w_hi, 3 * ei + m + 1)
                    dve.tensor_tensor(w_gu[:, buf, LO, m, :], raw.gu[:, buf, m, :], w_gu[:, buf, HI, m, :].bitcast(F32), ALU.subtract)\
                       .then_inc(gu_w_lo, 1)

            dve.sem_inc(gu_ready, 2)
            dve.sem_inc(down_used, 1)
            for i in range(BLOCKS):
                dve.tensor_copy(x_in[:, HI, :, i * NB:(i + 1) * NB], g.xT[:, :, SHIFT + i * NB:SHIFT + (i + 1) * NB]).then_inc(x_hi, 1)
            split_weights(0)
            dve.wait_ge(router.filled, 2)
            for ei in range(len(x.order)):
                def add_block(i):
                    blk = ei * BLOCKS + i
                    dve.wait_ge(down_ready, blk + 1)
                    if weighted(ei):
                        w_blk = before(ei) * BLOCKS + i
                        dve.wait_ge(spread_ready, w_blk + 2)
                        dve.wait_ge(x_done, w_blk + 1)
                        dve.tensor_tensor(part[:, :, :], down_ps[:, :, :], over_chunks(spread[:, :]), ALU.mult).then_inc(down_used, 1)
                    else:
                        dve.tensor_tensor(x_cols(i), down_ps[:, :, :], x_cols(i), ALU.add).then_inc(down_used, 1)

                if ei + 1 < len(x.order):
                    split_weights(ei + 1)
                with dve.Fori(0, PAIRS) as ii:
                    for u in range(2):
                        i = 2 * ii + u
                        for c in range(IC):
                            n = u * IC + c
                            m = x.rows_of(c)
                            gn = (ei * PAIRS + ii) * NP + n
                            dve.wait_ge(silu_ready, gn + 1)
                            dve.wait_ge(up_ready, gn + 1)
                            dve.tensor_tensor(gu[0:m, n % 2, :], gu[0:m, n % 2, :], up_ps[0:m, n % 2, :], ALU.mult)\
                               .then_inc(gu_ready, 1)
                            dve.wait_ge(gu_ready, gn + 3)
                            dve.tensor_copy(gu_in[0:m, n % 2, HI, :], gu[0:m, n % 2, :]).then_inc(gu_hi, 1)
                            if u == 1 and c == 0 and ei > 0:
                                add_block(i - 1)
                        if ei == 0:
                            router.vector(dve, i)
                        if u == 1 or ei == 0:
                            add_block(i)

        @block.gpsimd
        def _(pool):
            def low_part(low, whole, high):
                return pool.tensor_tensor(low, whole, high.bitcast(F32), ALU.subtract)

            def split_weights(ei):
                buf = ei % 2
                pool.wait_ge(w_hi, 3 * ei + 3)
                for parts in zip(*(down_parts(ap) for ap in (w_down[:, buf, LO, :], raw.down[:, buf, :], w_down[:, buf, HI, :]))):
                    ins = low_part(*parts)
                ins.then_inc(down_w_lo, 1)

            if LOADS == 3:
                pool.memset(b_router[:, :], 0.0).then_inc(zeroed, 1)
            else:
                pool.sem_inc(zeroed, 1)
            router.gpsimd(pool)
            pool.sem_inc(gu_lo, 2)
            pool.sem_inc(x_done, 1)
            for i in range(BLOCKS):
                pool.wait_ge(x_hi, i + 1)
                cols = slice(i * NB, (i + 1) * NB)
                low_part(x_in[:, LO, :, cols], g.xT[:, :, SHIFT + i * NB:SHIFT + (i + 1) * NB], x_in[:, HI, :, cols]).then_inc(x_lo, 1)
            split_weights(0)
            for ei in range(len(x.order)):
                def add_block(i):
                    blk = ei * BLOCKS + i
                    pool.wait_ge(down_used, blk + 2)
                    pool.tensor_tensor(x_cols(i), x_cols(i), part[:, :, :], ALU.add).then_inc(x_done, 1)

                if ei + 1 < len(x.order):
                    split_weights(ei + 1)
                with pool.Fori(0, PAIRS) as ii:
                    for u in range(2):
                        i = 2 * ii + u
                        for c in range(IC):
                            n = u * IC + c
                            m = x.rows_of(c)
                            gn = (ei * PAIRS + ii) * NP + n
                            pool.wait_ge(gu_hi, gn + 1)
                            low_part(gu_in[0:m, n % 2, LO, :], gu[0:m, n % 2, :], gu_in[0:m, n % 2, HI, :]).then_inc(gu_lo, 1)
                            if u == 1 and c == 0 and ei > 0 and weighted(ei):
                                add_block(i - 1)
                        if (u == 1 or ei == 0) and weighted(ei):
                            add_block(i)


HEADS, HD = 16, 16
HALF = HD // 2
LORA = 64
LORA_G = 128
STEPS = P // BATCH
UNIT_KEY, DECAY, B_IN, KEY, RECV, VALUE = range(6)
SCAN_IN = 6
MIXES = "rwkva"
OWN, LAST = range(2)


def heads(ap):
    return ap.rearrange("p (h j) -> p h j", j=HD)


def per_head(ap):
    return ap.unsqueeze(2).to_broadcast([P, HEADS, HD])


def each_row(ap):
    shape = list(ap.shape)
    return ap.unsqueeze(len(shape) - 1).to_broadcast([*shape[:-1], HALF, HD])


def rwkv_phase(nc, d, g):
    with Scope(nc) as s:
        mix_w = s.sb("rw_mix_w", [P, len(MIXES), KC])
        w = {m: s.sb(f"rw_w_{m}", [P, 2, KC, DIM]) for m in ("r", "k", "v", "kk")}
        wa = {m: s.sb(f"rw_wa_{m}", [P, 2, KC, LORA]) for m in "wa"}
        wa_g = s.sb("rw_wa_g", [P, KC, LORA_G])
        wb = {m: s.sb(f"rw_wb_{m}", [n, DIM]) for m, n in (("w", LORA), ("a", LORA), ("g", LORA_G))}
        w_o = s.sb("rw_w_o", [P, KC, DIM])
        rows = s.sb("rw_rows", [P, 8, DIM])
        W_BIAS, A_BIAS, G_BIAS, K_K, K_A, R_K, GN_W, GN_B = range(8)
        less_k_a = s.sb("rw_less_k_a", [P, DIM])
        ident = s.sb("rw_ident", [P, P])
        first = s.sb("rw_first", [P, P])
        x_in = s.sb("rw_x_in", [P, 2, KC, P])
        r_col = s.sb("rw_r_col", [P, KC, P])
        lora_w = s.sb("rw_lora_w", [LORA, P])
        lora_a = s.sb("rw_lora_a", [LORA, P])
        lora_g = s.sb("rw_lora_g", [P, P])
        sig = s.sb("rw_sig", [P, 2, DIM])
        k = s.sb("rw_k", [P, DIM])
        kk = s.sb("rw_kk", [P, DIM])
        kk_sq = s.sb("rw_kk_sq", [P, DIM])
        kk_norm = s.sb("rw_kk_norm", [P, HEADS])
        k_scale = s.sb("rw_k_scale", [P, DIM])
        rk = s.sb("rw_rk", [P, DIM])
        rk_sum = s.sb("rw_rk_sum", [P, HEADS])
        q = s.sb("rw_q", [P, SCAN_IN, DIM])
        gate = s.sb("rw_gate", [P, 2, DIM])
        bonus = s.sb("rw_bonus", [P, 2, DIM])
        sc = s.sb("rw_sc", [P, 2, SCAN_IN - 1, HD, STEPS])
        sc_value = s.sb("rw_sc_value", [P, 2, HALF, STEPS])
        vk = s.sb("rw_vk", [P, 2, STEPS, HALF, HD])
        state = s.sb("rw_state", [P, 2, STEPS + 1, HALF, HD])
        sa_terms = s.sb("rw_sa_terms", [P, HALF, HD])
        decayed = s.sb("rw_decayed", [P, HALF, HD])
        sa = s.sb("rw_sa", [P, HALF])
        sab = s.sb("rw_sab", [P, HALF, HD])
        kept = s.sb("rw_kept", [P, HALF, HD])
        o_terms = s.sb("rw_o_terms", [P, STEPS, HALF, HD])
        o_scan = s.sb("rw_o_scan", [P, HALF, STEPS])
        o = s.sb("rw_o", [P, DIM])
        mean = s.sb("rw_mean", [P, HEADS])
        dev = s.sb("rw_dev", [P, DIM])
        dev_sq = s.sb("rw_dev_sq", [P, DIM])
        var = s.sb("rw_var", [P, HEADS])
        gated = s.sb("rw_gated", [P, DIM])
        o_col = s.sb("rw_o_col", [P, KC, P])
        rv_ps = s.ps("rw_rv_ps", [P, 2, DIM])
        k_ps = s.ps("rw_k_ps", [P, 2, DIM])
        wa_ps = s.ps("rw_wa_ps", [P, 2, DIM])
        g_ps = s.ps("rw_g_ps", [P, NB])
        col_ps = s.ps("rw_col_ps", [P, 4, P])
        lg_ps = s.ps("rw_lg_ps", [P, NB])
        o_col_ps = s.ps("rw_o_col_ps", [P, KC, P])
        y_ps = s.ps("rw_y_ps", [P, KC, P])
        loaded = s.sem("rw_loaded")
        w_step = s.sem("rw_w_step")
        w_mixed = s.sem("rw_w_mixed")
        x_copied = s.sem("rw_x_copied")
        cols_ready = s.sem("rw_cols_ready")
        rkv_ready = s.sem("rw_rkv_ready")
        inner_ready = s.sem("rw_inner_ready")
        outer_ready = s.sem("rw_outer_ready")
        lg_ready = s.sem("rw_lg_ready")
        lg_act = s.sem("rw_lg_act")
        g_ready = s.sem("rw_g_ready")
        zeroed = s.sem("rw_zeroed")
        sig_ready = s.sem("rw_sig_ready")
        decay_ready = s.sem("rw_decay_ready")
        rv_ready = s.sem("rw_rv_ready")
        kk_ready = s.sem("rw_kk_ready")
        kk_sq_ready = s.sem("rw_kk_sq_ready")
        kk_sum_ready = s.sem("rw_kk_sum_ready")
        kk_floored = s.sem("rw_kk_floored")
        kk_norm_ready = s.sem("rw_kk_norm_ready")
        kk_inverse = s.sem("rw_kk_inverse")
        k_step = s.sem("rw_k_step")
        key_ready = s.sem("rw_key_ready")
        unit_key_ready = s.sem("rw_unit_key_ready")
        b_in_ready = s.sem("rw_b_in_ready")
        rk_ready = s.sem("rw_rk_ready")
        rk_summed = s.sem("rw_rk_summed")
        bonus_ready = s.sem("rw_bonus_ready")
        kv_turned = s.sem("rw_kv_turned")
        q_turned = s.sem("rw_q_turned")
        gate_ready = s.sem("rw_gate_ready")
        vk_ready = s.sem("rw_vk_ready")
        sa_terms_ready = s.sem("rw_sa_terms_ready")
        decayed_ready = s.sem("rw_decayed_ready")
        sa_ready = s.sem("rw_sa_ready")
        sab_ready = s.sem("rw_sab_ready")
        state_ready = s.sem("rw_state_ready")
        o_terms_ready = s.sem("rw_o_terms_ready")
        o_folded = s.sem("rw_o_folded")
        o_summed = s.sem("rw_o_summed")
        o_turned = s.sem("rw_o_turned")
        o_sum_ready = s.sem("rw_o_sum_ready")
        mean_ready = s.sem("rw_mean_ready")
        dev_ready = s.sem("rw_dev_ready")
        dev_sq_ready = s.sem("rw_dev_sq_ready")
        var_ready = s.sem("rw_var_ready")
        std_ready = s.sem("rw_std_ready")
        std_inverse = s.sem("rw_std_inverse")
        normed = s.sem("rw_normed")
        affine = s.sem("rw_affine")
        gated_ready = s.sem("rw_gated_ready")
        gated_turned = s.sem("rw_gated_turned")
        o_col_ready = s.sem("rw_o_col_ready")
        y_ready = s.sem("rw_y_ready")
        x_done = s.sem("rw_x_done")
        block = s.block()
        LOADS = 1 + 3 + 3 + 3 + 1 + 8 + 1

        def tiles(engine, tile):
            tile(0, 0, True, False)
            with engine.Fori(0, TILES // 2 - 1) as i:
                for u in (1, 2):
                    tile(2 * i + u, u % 2, True, True)
            tile(TILES - 1, 1, False, True)

        def tokens(c, before=0):
            cols = g.xT[:, :, bass.ds(SHIFT * (1 - before) + c * P, P)]
            return cols.rearrange("p k (t b) -> p k b t", b=BATCH)

        def by_batch(ap):
            return ap.rearrange("p k (b t) -> p k b t", b=BATCH)

        @block.sync
        def _(sp):
            sp.dma_start(mix_w[:, :, :], d["rw_mix_w"]).then_inc(loaded, 16)
            for m in "rkv":
                sp.dma_start(w[m][:, OWN, :, :], d[f"rw_w_{m}"]).then_inc(loaded, 16)
            for m in "wa":
                sp.dma_start(wa[m][:, OWN, :, :], d[f"rw_wa_{m}"]).then_inc(loaded, 16)
            sp.dma_start(wa_g[:, :, :], d["rw_wa_g"]).then_inc(loaded, 16)
            for m in "wag":
                sp.dma_start(wb[m][:, :], d[f"rw_wb_{m}"]).then_inc(loaded, 16)
            sp.dma_start(w_o[:, :, :], d["rw_w_o"]).then_inc(loaded, 16)
            for n, m in enumerate(("w_bias", "a_bias", "g_bias", "k_k", "k_a", "r_k", "gn_w", "gn_b")):
                sp.dma_start(rows[:, n, :], d[f"rw_{m}"].partition_broadcast(P)).then_inc(loaded, 16)
            sp.dma_start(ident[:, :], d["ident"]).then_inc(loaded, 16)

        @block.tensor
        def _(pe):
            def sums(out, lhs, rhs):
                for part in (OWN, LAST):
                    for k in range(KC):
                        mm = pe.matmul(out, lhs(part, k), rhs(part, k), start=(part == OWN and k == 0),
                                       stop=(part == LAST and k == KC - 1))
                return mm

            def x(part, k):
                return x_in[:, part, k, :]

            def project(m):
                pe.wait_ge(x_copied, m + 1)
                for o_ in range(KC):
                    sums(col_ps[:, o_, :], lambda part, k: w["r"][:, part, k, o_ * P:(o_ + 1) * P], x)
                sums(col_ps[0:LORA, 2, :], lambda part, k: wa["w"][:, part, k, :], x)
                sums(col_ps[0:LORA, 3, :], lambda part, k: wa["a"][:, part, k, :], x).then_inc(cols_ready, 1)
                for ps, name in ((k_ps[:, 0, :], "k"), (k_ps[:, 1, :], "kk"), (rv_ps[:, 0, :], "r"), (rv_ps[:, 1, :], "v")):
                    mm = sums(ps, x, lambda part, k: w[name][:, part, k, :])
                mm.then_inc(rkv_ready, 1)
                pe.wait_ge(inner_ready, m + 1)
                for k in range(KC):
                    mm = pe.matmul(lg_ps[:, 0:P], wa_g[:, k, :], r_col[:, k, :], start=(k == 0), stop=(k == KC - 1))
                mm.then_inc(lg_ready, 1)
                for n, (inner, m_) in enumerate(((lora_w, "w"), (lora_a, "a"))):
                    pe.matmul(wa_ps[:, n, :], first[:, :], rows[:, (W_BIAS, A_BIAS)[n], :], start=True, stop=False)
                    mm = pe.matmul(wa_ps[:, n, :], inner[:, :], wb[m_][:, :], start=False, stop=True)
                mm.then_inc(outer_ready, 1)
                pe.wait_ge(lg_act, m + 1)
                pe.matmul(g_ps[:, 0:DIM], first[:, :], rows[:, G_BIAS, :], start=True, stop=False)
                pe.matmul(g_ps[:, 0:DIM], lora_g[:, :], wb["g"][:, :], start=False, stop=True).then_inc(g_ready, 1)

            def output(c):
                pe.wait_ge(gated_ready, c + 1)
                for k in range(KC):
                    mm = pe.transpose(o_col_ps[:, k, :], gated[:, k * P:(k + 1) * P], ident[:, :])
                mm.then_inc(gated_turned, 1)
                pe.wait_ge(o_col_ready, c + 1)
                for o_ in range(KC):
                    for k in range(KC):
                        mm = pe.matmul(y_ps[:, o_, :], w_o[:, k, o_ * P:(o_ + 1) * P], o_col[:, k, :],
                                       start=(k == 0), stop=(k == KC - 1))
                mm.then_inc(y_ready, 1)

            def tile(c, parity, has_next, has_last):
                if has_next:
                    pe.wait_ge(gate_ready, c + 1)
                    project(c + 1)
                if has_last:
                    output(c - 1)

            pe.wait_ge(loaded, 16 * LOADS)
            pe.wait_ge(zeroed, 2)
            pe.wait_ge(w_mixed, 1)
            project(0)
            tiles(pe, tile)
            output(TILES - 1)

        @block.scalar
        def _(act):
            def copy_x(m):
                act.copy(by_batch(x_in[:, LAST, :, :]), tokens(m, before=1))
                act.copy(by_batch(x_in[:, OWN, :, :]), tokens(m)).then_inc(x_copied, 1)

            def project_products(m):
                act.wait_ge(cols_ready, m + 1)
                act.copy(r_col[:, :, :], col_ps[:, 0:KC, :])
                act.copy(lora_a[:, :], col_ps[0:LORA, 3, :])
                act.activation(lora_w[:, :], col_ps[0:LORA, 2, :], ACT.Tanh).then_inc(inner_ready, 1)
                act.wait_ge(rkv_ready, m + 1)
                act.copy(q[:, RECV, :], rv_ps[:, 0, :])
                act.copy(q[:, VALUE, :], rv_ps[:, 1, :]).then_inc(rv_ready, 1)
                act.activation(kk_sq[:, :], k_ps[:, 1, :], ACT.Square).then_inc(kk_sq_ready, 1)
                act.copy(k[:, :], k_ps[:, 0, :])
                act.copy(kk[:, :], k_ps[:, 1, :]).then_inc(kk_ready, 1)
                act.wait_ge(lg_ready, m + 1)
                act.activation(lora_g[:, :], lg_ps[:, 0:P], ACT.Sigmoid).then_inc(lg_act, 1)
                act.wait_ge(outer_ready, m + 1)
                act.activation(sig[:, :, :], wa_ps[:, :, :], ACT.Sigmoid).then_inc(sig_ready, 1)
                act.wait_ge(sig_ready, m + 1)
                act.mul(q[:, DECAY, :], sig[:, 0, :], math.exp(-0.5)).then_inc(decay_ready, 1)

            def project_norm(m):
                act.wait_ge(kk_floored, m + 1)
                act.activation(kk_norm[:, :], kk_norm[:, :], ACT.Sqrt).then_inc(kk_norm_ready, 1)

            def project_gate(m, parity):
                act.wait_ge(g_ready, m + 1)
                act.copy(gate[:, parity, :], g_ps[:, 0:DIM]).then_inc(gate_ready, 1)

            def output_square(c):
                act.wait_ge(o_sum_ready, c + 1)
                act.mul(mean[:, :], mean[:, :], 1.0 / HD).then_inc(mean_ready, 1)
                act.wait_ge(dev_ready, c + 1)
                act.activation(dev_sq[:, :], dev[:, :], ACT.Square).then_inc(dev_sq_ready, 1)

            def output_std(c):
                act.wait_ge(var_ready, c + 1)
                act.activation(var[:, :], var[:, :], ACT.Sqrt, scale=1.0 / HD, bias=g.eps[:, :]).then_inc(std_ready, 1)

            def output_columns(c):
                act.wait_ge(gated_turned, c + 1)
                act.copy(o_col[:, :, :], o_col_ps[:, :, :]).then_inc(o_col_ready, 1)

            def tile(c, parity, has_next, has_last):
                if has_next:
                    act.wait_ge(q_turned, c + 1)
                    act.wait_ge(bonus_ready, c + 1)
                    copy_x(c + 1)
                    project_products(c + 1)
                    project_norm(c + 1)
                if has_last:
                    output_square(c - 1)
                    output_std(c - 1)
                    output_columns(c - 1)
                if has_next:
                    project_gate(c + 1, 1 - parity)

            copy_x(0)
            project_products(0)
            project_norm(0)
            project_gate(0, 0)
            tiles(act, tile)
            output_square(TILES - 1)
            output_std(TILES - 1)
            output_columns(TILES - 1)

        @block.gpsimd
        def _(pool):
            def output_terms(c, parity, part):
                t = slice(part * STEPS // 2, (part + 1) * STEPS // 2)
                pool.wait_ge(state_ready, c * STEPS + t.stop + 1)
                after = state[:, parity, t.start + 1:t.stop + 1, :, :]
                pool.tensor_tensor(o_terms[:, t, :, :], after, each_row(sc[:, parity, RECV, :, t].rearrange("p j t -> p t j")),
                                   ALU.mult).then_inc(o_terms_ready, 1)
                for n, half in enumerate((HD // 2, HD // 4)):
                    pool.wait_ge(o_terms_ready, 4 * c + 2 * part + n + 1)
                    ins = pool.tensor_tensor(o_terms[:, t, :, 0:half], o_terms[:, t, :, 0:half], o_terms[:, t, :, half:2 * half], ALU.add)
                    ins.then_inc(o_terms_ready if n == 0 else o_folded, 1)

            def output_dev(c):
                pool.wait_ge(mean_ready, c + 1)
                pool.tensor_tensor(heads(dev[:, :]), heads(o[:, :]), per_head(mean[:, :]), ALU.subtract).then_inc(dev_ready, 1)

            def output_gate(c, parity):
                pool.wait_ge(std_inverse, c + 1)
                pool.tensor_tensor(heads(dev[:, :]), heads(dev[:, :]), per_head(var[:, :]), ALU.mult).then_inc(normed, 1)
                pool.wait_ge(normed, c + 1)
                steps = ((dev, dev, rows[:, GN_W, :], ALU.mult), (dev, dev, rows[:, GN_B, :], ALU.add),
                         (dev, dev, bonus[:, parity, :], ALU.add), (gated, dev, gate[:, parity, :], ALU.mult))
                for n, (out, a, b, op) in enumerate(steps):
                    ins = pool.tensor_tensor(out[:, :], a[:, :], b, op)
                    if n < len(steps) - 1:
                        ins.then_inc(affine, 1)
                        pool.wait_ge(affine, c * (len(steps) - 1) + n + 1)
                ins.then_inc(gated_ready, 1)

            def project_key(m):
                pool.wait_ge(sig_ready, m + 1)
                pool.tensor_tensor(k_scale[:, :], sig[:, 1, :], rows[:, K_A, :], ALU.mult).then_inc(k_step, 1)
                pool.wait_ge(k_step, 2 * m + 1)
                pool.tensor_tensor(k_scale[:, :], k_scale[:, :], less_k_a[:, :], ALU.add).then_inc(k_step, 1)
                pool.wait_ge(k_step, 2 * m + 2)
                pool.wait_ge(kk_ready, m + 1)
                pool.tensor_tensor(q[:, KEY, :], k_scale[:, :], k[:, :], ALU.mult).then_inc(key_ready, 1)
                pool.wait_ge(key_ready, m + 1)
                pool.wait_ge(rv_ready, m + 1)
                pool.tensor_tensor(rk[:, :], q[:, RECV, :], q[:, KEY, :], ALU.mult).then_inc(rk_ready, 1)
                pool.wait_ge(rk_ready, 2 * m + 1)
                pool.tensor_tensor(rk[:, :], rk[:, :], rows[:, R_K, :], ALU.mult).then_inc(rk_ready, 1)

            def project_unit_key(m):
                pool.wait_ge(kk_inverse, m + 1)
                pool.tensor_tensor(heads(q[:, UNIT_KEY, :]), heads(kk[:, :]), per_head(kk_norm[:, :]), ALU.mult).then_inc(unit_key_ready, 1)
                pool.wait_ge(unit_key_ready, m + 1)
                pool.tensor_tensor(q[:, B_IN, :], q[:, UNIT_KEY, :], sig[:, 1, :], ALU.mult).then_inc(b_in_ready, 1)

            def project_bonus(m, parity):
                pool.wait_ge(rk_summed, m + 1)
                pool.tensor_tensor(heads(bonus[:, parity, :]), heads(q[:, VALUE, :]), per_head(rk_sum[:, :]), ALU.mult)\
                    .then_inc(bonus_ready, 1)

            def project_vk(m, parity):
                pool.wait_ge(kv_turned, m + 1)
                pool.tensor_tensor(vk[:, parity, :, :, :],
                                   sc_value[:, parity, :, :].rearrange("p i t -> p t i").unsqueeze(3)
                                   .to_broadcast([P, STEPS, HALF, HD]),
                                   each_row(sc[:, parity, KEY, :, :].rearrange("p j t -> p t j")), ALU.mult).then_inc(vk_ready, 1)

            def tile(c, parity, has_next, has_last):
                if has_last:
                    output_terms(c - 1, 1 - parity, 1)
                if has_next:
                    project_key(c + 1)
                if has_last:
                    output_dev(c - 1)
                if has_next:
                    project_unit_key(c + 1)
                    project_vk(c + 1, 1 - parity)
                if has_last:
                    output_gate(c - 1, 1 - parity)
                if has_next:
                    project_bonus(c + 1, 1 - parity)
                output_terms(c, parity, 0)

            pool.memset(first[:, :], 0.0).then_inc(zeroed, 1)
            pool.wait_ge(zeroed, 1)
            pool.memset(first[0:1, :], 1.0).then_inc(zeroed, 1)
            pool.wait_ge(w_mixed, 1)
            project_key(0)
            project_unit_key(0)
            project_vk(0, 0)
            project_bonus(0, 0)
            tiles(pool, tile)
            output_terms(TILES - 1, 1, 1)
            output_dev(TILES - 1)
            output_gate(TILES - 1, 1)

        @block.vector
        def _(dve):
            def turn_blocks(parity, n):
                rows_of = q[:, n, :].rearrange("p (h j) -> p j h", j=HD).unsqueeze(2).to_broadcast([P, HD, 2, HEADS])
                return dve.transpose(sc[:, parity, n, :, :].rearrange("p j (f h) -> p j f h", f=2), rows_of)

            def project(t, m, parity):
                if t == 6:
                    dve.wait_ge(kk_sq_ready, m + 1)
                    dve.tensor_reduce(kk_norm[:, :], heads(kk_sq[:, :]), AX_X, ALU.add).then_inc(kk_sum_ready, 1)
                elif t == 7:
                    dve.wait_ge(kk_sum_ready, m + 1)
                    dve.tensor_scalar(kk_norm[:, :], kk_norm[:, :], 1e-24, None, ALU.max).then_inc(kk_floored, 1)
                elif t == 9:
                    dve.wait_ge(rv_ready, m + 1)
                    turn_blocks(parity, RECV)
                elif t == 10:
                    dve.wait_ge(kk_norm_ready, m + 1)
                    dve.reciprocal(kk_norm[:, :], kk_norm[:, :]).then_inc(kk_inverse, 1)
                elif t == 11:
                    rows_of = q[:, VALUE, :].rearrange("p (h f i) -> p i f h", f=2, i=HALF)
                    dve.transpose(sc_value[:, parity, :, :].rearrange("p i (f h) -> p i f h", f=2), rows_of)
                elif t == 12:
                    dve.wait_ge(key_ready, m + 1)
                    turn_blocks(parity, KEY).then_inc(kv_turned, 1)
                elif t == 13:
                    dve.wait_ge(rk_ready, 2 * m + 2)
                    dve.tensor_reduce(rk_sum[:, :], heads(rk[:, :]), AX_X, ALU.add).then_inc(rk_summed, 1)
                elif t == 15:
                    dve.wait_ge(decay_ready, m + 1)
                    turn_blocks(parity, DECAY)
                elif t == 17:
                    dve.wait_ge(b_in_ready, m + 1)
                    turn_blocks(parity, UNIT_KEY)
                elif t == 18:
                    turn_blocks(parity, B_IN).then_inc(q_turned, 1)

            def output(t, c):
                if t in (1, 7):
                    part = 0 if t == 1 else 1
                    dve.wait_ge(o_folded, 2 * c + part + 1)
                    steps = slice(part * STEPS // 2, (part + 1) * STEPS // 2)
                    dve.tensor_reduce(o_scan[:, :, steps].rearrange("p i t -> p t i"), o_terms[:, steps, :, 0:HD // 4], AX_X, ALU.add)\
                       .then_inc(o_summed, 1)
                elif t == 8:
                    dve.wait_ge(o_summed, 2 * c + 2)
                    dve.transpose(o[:, :].rearrange("p (h f i) -> p i f h", f=2, i=HALF),
                                  o_scan[:, :, :].rearrange("p i (f h) -> p i f h", f=2)).then_inc(o_turned, 1)
                elif t == 9:
                    dve.wait_ge(o_turned, c + 1)
                    dve.tensor_reduce(mean[:, :], heads(o[:, :]), AX_X, ALU.add).then_inc(o_sum_ready, 1)
                elif t == 14:
                    dve.wait_ge(dev_sq_ready, c + 1)
                    dve.tensor_reduce(var[:, :], heads(dev_sq[:, :]), AX_X, ALU.add).then_inc(var_ready, 1)
                elif t == 17:
                    dve.wait_ge(std_ready, c + 1)
                    dve.reciprocal(var[:, :], var[:, :]).then_inc(std_inverse, 1)
                elif t == 31:
                    dve.wait_ge(y_ready, c + 1)
                    x = tokens(c)
                    dve.tensor_tensor(x, x, by_batch(y_ps[:, :, :]), ALU.add).then_inc(x_done, 1)

            def tile(c, parity, has_next, has_last):
                dve.wait_ge(q_turned, c + 1)
                dve.wait_ge(vk_ready, c + 1)
                for t in range(STEPS):
                    n = c * STEPS + t
                    before = state[:, 1 - parity, STEPS, :, :] if t == 0 else state[:, parity, t, :, :]
                    dve.wait_ge(state_ready, n + 1)
                    dve.tensor_tensor(sa_terms[:, :, :], before, each_row(sc[:, parity, UNIT_KEY, :, t]), ALU.mult)\
                       .then_inc(sa_terms_ready, 1)
                    dve.tensor_tensor(decayed[:, :, :], before, each_row(sc[:, parity, DECAY, :, t]), ALU.mult)\
                       .then_inc(decayed_ready, 1)
                    if has_next:
                        project(t, c + 1, 1 - parity)
                    dve.wait_ge(sa_terms_ready, n + 1)
                    dve.tensor_reduce(sa[:, :], sa_terms[:, :, :], AX_X, ALU.add).then_inc(sa_ready, 1)
                    dve.wait_ge(decayed_ready, n + 1)
                    dve.tensor_tensor(kept[:, :, :], decayed[:, :, :], vk[:, parity, t, :, :], ALU.add)
                    dve.wait_ge(sa_ready, n + 1)
                    dve.tensor_tensor(sab[:, :, :], sa[:, :].unsqueeze(2).to_broadcast([P, HALF, HD]),
                                      each_row(sc[:, parity, B_IN, :, t]), ALU.mult).then_inc(sab_ready, 1)
                    if has_last:
                        output(t, c - 1)
                    dve.wait_ge(sab_ready, n + 1)
                    dve.tensor_tensor(state[:, parity, t + 1, :, :], kept[:, :, :], sab[:, :, :], ALU.subtract).then_inc(state_ready, 1)

            dve.wait_ge(loaded, 16 * LOADS)
            for n, name in enumerate(MIXES):
                of = w[name] if name in w else wa[name]
                for k_ in range(KC):
                    dve.tensor_scalar(of[:, LAST, k_, :], of[:, OWN, k_, :], mix_w[:, n, k_:k_ + 1], None, ALU.mult)
            dve.tensor_scalar(less_k_a[:, :], rows[:, K_A, :], -1.0, 1.0, ALU.mult, ALU.add).then_inc(w_step, 1)
            dve.wait_ge(w_step, 1)
            for name in MIXES:
                of = w[name] if name in w else wa[name]
                ins = dve.tensor_tensor(of[:, OWN, :, :], of[:, OWN, :, :], of[:, LAST, :, :], ALU.subtract)
            ins.then_inc(w_step, 1)
            dve.wait_ge(w_step, 2)
            ins = dve.tensor_tensor(w["kk"][:, :, :, :].rearrange("p a k n -> p (a k) n"), w["k"][:, :, :, :].rearrange("p a k n -> p (a k) n"),
                                    over_chunks(rows[:, K_K, :], 2 * KC), ALU.mult)
            ins.then_inc(w_mixed, 1)
            dve.memset(state[:, 1, STEPS, :, :], 0.0).then_inc(state_ready, 1)
            for t in range(STEPS):
                project(t, 0, 0)
            tiles(dve, tile)
            for t in range(STEPS):
                output(t, TILES - 1)


QC = SEQ // P
SCALE = float(DIM) ** -0.5


def cross_attention_phase(nc, d, g, next_weights):
    with Scope(nc) as s:
        w = {m: s.sb(f"ca_w_{m}", [P, KC, DIM]) for m in ("q", "k", "v")}
        b = {m: s.sb(f"ca_b_{m}", [P, KC]) for m in ("q", "k", "v")}
        ident = s.sb("ca_ident", [P, P])
        ctx_all = s.sb("ca_ctx_all", [P, KC, BATCH * SRC])
        ctx = s.sb("ca_ctx", [P, KC, SRC])
        x = s.sb("ca_x", [P, KC, SEQ])
        q = s.sb("ca_q", [P, KC, SEQ])
        k_ = s.sb("ca_k", [P, KC, SRC])
        v = s.sb("ca_v", [P, SC, DIM])
        neg_max = s.sb("ca_neg_max", [P, QC])
        total = s.sb("ca_total", [P, QC])
        prob = s.sb("ca_prob", [P, QC, SRC])
        prob_t = s.sb("ca_prob_t", [P, SC, SEQ])
        qk_ps = s.ps("ca_qk_ps", [P, 2, NB])
        score_ps = s.ps("ca_score_ps", [P, 2, SRC])
        turn_ps = s.ps("ca_turn_ps", [P, 2, NB])
        out_ps = s.ps("ca_out_ps", [P, KC, SEQ])
        loaded = s.sem("ca_loaded")
        staged = s.sem("ca_staged")
        qk_ready = s.sem("ca_qk_ready")
        qk_kept = s.sem("ca_qk_kept")
        v_ready = s.sem("ca_v_ready")
        v_kept = s.sem("ca_v_kept")
        scores_ready = s.sem("ca_scores_ready")
        max_ready = s.sem("ca_max_ready")
        scaled_max = s.sem("ca_scaled_max")
        exp_ready = s.sem("ca_exp_ready")
        inverse_ready = s.sem("ca_inverse_ready")
        prob_ready = s.sem("ca_prob_ready")
        turned = s.sem("ca_turned")
        turn_kept = s.sem("ca_turn_kept")
        out_ready = s.sem("ca_out_ready")
        y_part = s.sem("ca_y_part")
        x_done = s.sem("ca_x_done")
        block = s.block()
        LOADS = 8

        def x_of(i):
            return g.xT[:, :, bass.ds(SHIFT, TOK)].rearrange("p k (t b) -> p k t b", b=BATCH)[:, :, :, bass.ds(i, 1)]\
                    .rearrange("p k t o -> p k (t o)")

        @block.sync
        def _(sp):
            sp.dma_start(ctx_all[:, :, :], d["ctxT"]).then_inc(loaded, 16)
            for m in ("q", "k", "v"):
                sp.dma_start(w[m][:, :, :], d[f"ca_w_{m}"]).then_inc(loaded, 16)
                sp.dma_start(b[m][:, :], d[f"ca_b_{m}"]).then_inc(loaded, 16)
            sp.dma_start(ident[:, :], d["ident"]).then_inc(loaded, 16)
            for ei in range(2):
                next_weights.load(sp, ei)

        @block.gpsimd
        def _(pool):
            pool.wait_ge(loaded, 16 * LOADS)
            with pool.Fori(0, BATCH) as i:
                pool.wait_ge(x_done, i + 1)
                pool.tensor_copy(ctx[:, :, :], ctx_all[:, :, bass.ds(i * SRC, SRC)])
                pool.tensor_copy(x[:, :, :], x_of(i)).then_inc(staged, 1)

        @block.tensor
        def _(pe):
            pe.wait_ge(loaded, 16 * LOADS)
            with pe.Fori(0, BATCH) as i:
                pe.wait_ge(staged, i + 1)
                for n, (wt, src) in enumerate(((w["q"], x), (w["k"], ctx))):
                    for o in range(KC):
                        if n > 0:
                            pe.wait_ge(qk_kept, 4 * i + 2 * n + o - 1)
                        for k in range(KC):
                            mm = pe.matmul(qk_ps[:, o, :], wt[:, k, o * P:(o + 1) * P], src[:, k, :],
                                           start=(k == 0), stop=(k == KC - 1))
                        mm.then_inc(qk_ready, 1)
                for c in range(SC):
                    if c >= 2:
                        pe.wait_ge(v_kept, SC * i + c - 1)
                    for k in range(KC):
                        mm = pe.matmul(turn_ps[:, c % 2, 0:DIM], ctx[:, k, c * P:(c + 1) * P], w["v"][:, k, :],
                                       start=(k == 0), stop=(k == KC - 1))
                    mm.then_inc(v_ready, 1)
                pe.wait_ge(qk_kept, 4 * i + 4)
                for c in range(QC):
                    if c >= 2:
                        pe.wait_ge(exp_ready, QC * i + c - 1)
                    for k in range(KC):
                        mm = pe.matmul(score_ps[:, c % 2, :], q[:, k, c * P:(c + 1) * P], k_[:, k, :],
                                       start=(k == 0), stop=(k == KC - 1))
                    mm.then_inc(scores_ready, 1)
                pe.wait_ge(v_kept, SC * i + SC)
                for c in range(QC):
                    pe.wait_ge(prob_ready, QC * i + c + 1)
                    if c >= 2:
                        pe.wait_ge(turn_kept, QC * i + c - 1)
                    for kc in range(SC):
                        mm = pe.transpose(turn_ps[:, c % 2, kc * P:(kc + 1) * P], prob[:, c, kc * P:(kc + 1) * P], ident[:, :])
                    mm.then_inc(turned, 1)
                pe.wait_ge(turn_kept, QC * i + QC)
                for o in range(KC):
                    for kc in range(SC):
                        mm = pe.matmul(out_ps[:, o, :], v[:, kc, o * P:(o + 1) * P], prob_t[:, kc, :],
                                       start=(kc == 0), stop=(kc == SC - 1))
                mm.then_inc(out_ready, 1)

        @block.scalar
        def _(act):
            act.wait_ge(loaded, 16 * LOADS)
            with act.Fori(0, BATCH) as i:
                for n, (m, dst) in enumerate((("q", q), ("k", k_))):
                    for o in range(KC):
                        act.wait_ge(qk_ready, 4 * i + 2 * n + o + 1)
                        act.activation(dst[:, o, :], qk_ps[:, o, :], ACT.Identity, bias=b[m][:, o:o + 1]).then_inc(qk_kept, 1)
                for c in range(SC):
                    act.wait_ge(v_ready, SC * i + c + 1)
                    act.copy(v[:, c, :], turn_ps[:, c % 2, 0:DIM]).then_inc(v_kept, 1)
                for c in range(QC):
                    act.wait_ge(max_ready, QC * i + c + 1)
                    act.mul(neg_max[:, c:c + 1], neg_max[:, c:c + 1], SCALE).then_inc(scaled_max, 1)
                    act.wait_ge(scaled_max, QC * i + c + 1)
                    act.activation(prob[:, c, :], score_ps[:, c % 2, :], ACT.Exp, bias=neg_max[:, c:c + 1], scale=SCALE,
                                   accum_out=total[:, c:c + 1]).then_inc(exp_ready, 1)
                for c in range(QC):
                    act.wait_ge(turned, QC * i + c + 1)
                    act.copy(prob_t[:, :, c * P:(c + 1) * P], turn_ps[:, c % 2, :].rearrange("p (s q) -> p s q", s=SC))\
                       .then_inc(turn_kept, 1)

        @block.vector
        def _(dve):
            dve.wait_ge(loaded, 16 * LOADS)
            dve.sem_inc(x_done, 1)
            with dve.Fori(0, BATCH) as i:
                for c in range(QC):
                    dve.wait_ge(scores_ready, QC * i + c + 1)
                    dve.tensor_reduce(neg_max[:, c:c + 1], score_ps[:, c % 2, :], AX_X, ALU.max, negate=True).then_inc(max_ready, 1)
                    dve.wait_ge(exp_ready, QC * i + c + 1)
                    dve.reciprocal(total[:, c:c + 1], total[:, c:c + 1]).then_inc(inverse_ready, 1)
                    dve.wait_ge(inverse_ready, QC * i + c + 1)
                    dve.tensor_scalar(prob[:, c, :], prob[:, c, :], total[:, c:c + 1], None, ALU.mult).then_inc(prob_ready, 1)
                dve.wait_ge(out_ready, i + 1)
                for o in range(KC):
                    ins = dve.scalar_tensor_tensor(out=x_of(i)[:, o, :], in0=out_ps[:, o, :], scalar=b["v"][:, o:o + 1],
                                                   in1=x[:, o, :], op0=ALU.add, op1=ALU.add)
                ins.then_inc(x_done, 1)



MIXTURE0 = Experts("mix", routed=8, shared=0, inner=256, softmax_first=False)
MIXTURE1 = Experts("sm", routed=4, shared=1, inner=688, softmax_first=True)


class Shared:
    pass


def decoder_program(nc, d):
    with Scope(nc) as s:
        g = Shared()
        g.xT = s.sb("xT", [P, KC, SHIFT + TOK])
        g.mean_mat = s.sb("mean_mat", [P, P])
        g.eps = s.sb("eps", [P, 1])
        g.consts = s.sem("consts")
        with Scope(nc) as m:
            raw = RawWeights(m, d, MIXTURE0)
            with Scope(nc) as c:
                g.ctxT = c.sb("ctxT", [P, KC, BATCH * SRC])
                recurrence_phase(nc, d, g)
                norm_phase(nc, g, "ln_recurrence")
                attention_lstm_phase(nc, d, g, raw)
            norm_phase(nc, g, "ln_lstm")
            mixture_phase(nc, d, g, MIXTURE0, raw)
        norm_phase(nc, g, "ln_mixture0")
        rwkv_phase(nc, d, g)
        norm_phase(nc, g, "ln_rwkv")
        with Scope(nc) as m:
            raw = RawWeights(m, d, MIXTURE1)
            cross_attention_phase(nc, d, g, raw)
            norm_phase(nc, g, "ln_cross")
            mixture_phase(nc, d, g, MIXTURE1, raw)
        norm_phase(nc, g, "ln_mixture1", d["out"])



def feature_major(x):
    return np.ascontiguousarray(x.transpose(2, 1, 0).reshape(KC, P, TOK).transpose(1, 0, 2))


def rows_on_partitions(w):
    return np.ascontiguousarray(w.reshape(-1, P, w.shape[1]).transpose(1, 0, 2))


def on_partitions(b):
    return np.ascontiguousarray(b.reshape(-1, P).T)


def each(f, ws):
    return np.ascontiguousarray(np.stack([f(w) for w in ws]))


def by_quarter(w):
    w = w.reshape(*w.shape[:-1], GATES, QUARTERS, QW)[..., [3, 0, 1, 2], :, :]
    return np.ascontiguousarray(np.moveaxis(w, -2, -3).reshape(*w.shape[:-3], GATE_W))


def hidden_order(w):
    return np.ascontiguousarray(w.reshape(QUARTERS, KC, STRIP, -1).swapaxes(0, 1).reshape(HID, -1))


def laid_out(inputs):
    i = {name: np.asarray(a) for name, a in inputs.items()}
    d = {"xT": feature_major(i["x"]),
         "ctxT": np.ascontiguousarray(i["ctx_1024"].transpose(2, 0, 1).reshape(KC, P, BATCH * SRC).transpose(1, 0, 2))}
    for m in ("in", "gate", "lam", "out"):
        d[f"rec_w_{m}"] = rows_on_partitions(i[f"L0_attn_W_{m}"].T)
        d[f"rec_b_{m}"] = on_partitions(i[f"L0_attn_b_{m}"])
    d["rec_gamma"] = on_partitions(i["L0_attn_gamma"])
    d["rec_beta"] = on_partitions(i["L0_attn_beta"])

    w_ih, w_out = i["L0_xattn_W_ih"], i["L0_xattn_Wout"]
    d["lstm_w_x"] = rows_on_partitions(by_quarter(w_ih[:, :DIM].T))
    d["lstm_w_attn"] = rows_on_partitions(by_quarter(w_ih[:, DIM:].T))
    d["lstm_w_hid"] = rows_on_partitions(hidden_order(by_quarter(i["L0_xattn_W_hh"].T)))
    d["lstm_w_q"] = rows_on_partitions(hidden_order(i["L0_xattn_Wq"].T).T)
    d["lstm_w_out_c"] = rows_on_partitions(w_out[:, :DIM].T)
    d["lstm_w_out_h"] = rows_on_partitions(hidden_order(w_out[:, DIM:].T))
    d["lstm_b_ih"], d["lstm_b_hh"] = (by_quarter(i[f"L0_xattn_{b}"]) for b in ("b_ih", "b_hh"))
    d["lstm_b_out"] = i["L0_xattn_b_out"]

    d["mix_w_router"] = rows_on_partitions(i["L0_ffn_router_w"])
    d["mix_b_router"] = np.ascontiguousarray(i["L0_ffn_router_b"].reshape(-1, 1))
    d["mix_w_down"] = i["L0_ffn_we_down"]
    for m in ("gate", "up"):
        d[f"mix_w_{m}"] = each(rows_on_partitions, i[f"L0_ffn_we_{m}"])

    rw = {name[len("L1_attn_"):]: a for name, a in i.items() if name.startswith("L1_attn_")}
    d["rw_mix_w"] = np.ascontiguousarray(np.stack([on_partitions(rw[f"x_{m}"]) for m in "rwkva"], 1))
    for m in ("r", "k", "v", "o"):
        d[f"rw_w_{m}"] = rows_on_partitions(rw[f"W_{m}"])
    for m in ("w", "a", "g"):
        d[f"rw_wa_{m}"] = rows_on_partitions(rw[f"{m}_lora_a"])
        d[f"rw_wb_{m}"] = rw[f"{m}_lora_b"]
        d[f"rw_{m}_bias"] = rw[f"{m}_lora_bias"]
    d["rw_k_k"], d["rw_k_a"], d["rw_r_k"] = rw["k_k"], rw["k_a"], rw["r_k"].reshape(-1)
    d["rw_gn_w"], d["rw_gn_b"] = rw["gn_weight"], rw["gn_bias"]

    for m in ("q", "k", "v"):
        d[f"ca_w_{m}"] = rows_on_partitions(i[f"L1_xattn_W{m}"].T)
        d[f"ca_b_{m}"] = on_partitions(i[f"L1_xattn_b{m}"])

    d["sm_w_router"] = rows_on_partitions(i["L1_ffn_gate_w"].T)
    d["sm_w_gate"] = each(lambda w: rows_on_partitions(w.T), [*i["L1_ffn_eg"], i["L1_ffn_sg"]])
    d["sm_w_up"] = each(lambda w: rows_on_partitions(w.T), [*i["L1_ffn_eu"], i["L1_ffn_su"]])
    d["sm_w_down"] = each(lambda w: w.T, [*i["L1_ffn_ed"], i["L1_ffn_sd"]])

    sel_batch = np.zeros((P, BATCH), np.float32)
    sel_batch[np.arange(BATCH) * STRIP, np.arange(BATCH)] = 1
    d["sel_batch"] = sel_batch
    d["ident"] = np.eye(P, dtype=np.float32)
    most = max(MIXTURE0.routed, MIXTURE1.routed)
    pick = np.zeros((most, most, P), np.float32)
    pick[np.arange(most), np.arange(most)] = 1
    d["pick"] = pick
    return d


def kernel(**inputs):
    import concourse.bacc as bacc
    from concourse.bass_utils import run_bass_kernel_spmd

    nc = bacc.Bacc("TRN2", target_bir_lowering=False, num_devices=1)
    arrays, d = {}, {}
    for name, a in laid_out(inputs).items():
        arrays[f"in_{name}"] = np.ascontiguousarray(a)
        d[name] = nc.dram_tensor(f"in_{name}", a.shape, F32, kind="ExternalInput").ap()
    d["out"] = nc.dram_tensor("out_xT", (P, KC, TOK), F32, kind="ExternalOutput").ap()
    decoder_program(nc, d)
    r = run_bass_kernel_spmd(nc, [arrays], core_ids=[0])
    got = np.asarray(r.results[0]["out_xT"])
    return np.ascontiguousarray(got.transpose(1, 0, 2).reshape(DIM, SEQ, BATCH).transpose(2, 1, 0))
```

```python
import math
from contextlib import ExitStack

import numpy as np

import concourse.bass as bass
from concourse import mybir

F32 = mybir.dt.float32
F32R = mybir.dt.float32r
ALU = mybir.AluOpType
ACT = mybir.ActivationFunctionType
AX_X = mybir.AxisListType.X

P = 128
BATCH, SEQ, DIM = 4, 512, 256
KC = DIM // P
TOK = BATCH * SEQ
NB = 512
BLOCKS = TOK // NB
QUARTERS = 4
STRIP = P // QUARTERS
SHIFT = BATCH
LN_EPS = 1e-5


class Scope:

    def __init__(self, nc):
        self.nc = nc
        self.stack = ExitStack()
        self.running = ExitStack()
        self.sems = []

    def __enter__(self):
        return self

    def __exit__(self, *exc):
        self.running.close()
        if self.sems:
            numbers = sorted(x.num for x in self.sems)
            with self.nc.Block() as block:
                @block.sync
                def _(sp):
                    first = numbers[0]
                    for n, after in zip(numbers, [*numbers[1:], None]):
                        if after != n + 1:
                            sp.sem_clear(range(first, n + 1))
                            first = after
        return self.stack.__exit__(*exc)

    def sb(self, name, shape, dtype=F32):
        return self.stack.enter_context(self.nc.sbuf_tensor(name, shape, dtype))

    def ps(self, name, shape):
        return self.stack.enter_context(self.nc.psum_tensor(name, shape, F32))

    def sem(self, name):
        self.sems.append(self.stack.enter_context(self.nc.semaphore(name)))
        return self.sems[-1]

    def block(self):
        return self.running.enter_context(self.nc.Block())


def over_chunks(ap, n=KC):
    return ap.unsqueeze(1).to_broadcast([ap.shape[0], n, ap.shape[1]])


class LayerNorm:

    def __init__(self, s, name, mean_ps, var_ps, width=NB):
        self.mean_ps, self.var_ps = mean_ps, var_ps
        self.d = s.sb(f"{name}_d", [P, KC, width])
        self.sq = s.sb(f"{name}_sq", [P, KC, width])
        self.rstd = s.sb(f"{name}_rstd", [P, width])
        self.y_ready = s.sem(f"{name}_y_ready")
        self.mean_ready = s.sem(f"{name}_mean_ready")
        self.d_ready = s.sem(f"{name}_d_ready")
        self.sq_ready = s.sem(f"{name}_sq_ready")
        self.var_ready = s.sem(f"{name}_var_ready")
        self.std_ready = s.sem(f"{name}_std_ready")
        self.rstd_ready = s.sem(f"{name}_rstd_ready")

    def mean(self, pe, n, y, ones):
        pe.wait_ge(self.y_ready, n + 1)
        for k in range(KC):
            mm = pe.matmul(self.mean_ps, ones, y(k), start=(k == 0), stop=(k == KC - 1))
        mm.then_inc(self.mean_ready, 1)

    def deviation(self, dve, n, y):
        dve.wait_ge(self.mean_ready, n + 1)
        dve.tensor_tensor(self.d[:, :, :], y, over_chunks(self.mean_ps), ALU.subtract)\
           .then_inc(self.d_ready, 1)

    def squares(self, act, n):
        act.wait_ge(self.d_ready, n + 1)
        act.activation(self.sq[:, :, :], self.d[:, :, :], ACT.Square).then_inc(self.sq_ready, 1)

    def variance(self, pe, n, ones):
        pe.wait_ge(self.sq_ready, n + 1)
        for k in range(KC):
            mm = pe.matmul(self.var_ps, ones, self.sq[:, k, :], start=(k == 0), stop=(k == KC - 1))
        mm.then_inc(self.var_ready, 1)

    def root(self, act, n, eps):
        act.wait_ge(self.var_ready, n + 1)
        act.activation(self.rstd[:, :], self.var_ps, ACT.Sqrt, bias=eps).then_inc(self.std_ready, 1)

    def result(self, dve, n, out):
        dve.wait_ge(self.std_ready, n + 1)
        dve.reciprocal(self.rstd[:, :], self.rstd[:, :]).then_inc(self.rstd_ready, 1)
        dve.wait_ge(self.rstd_ready, n + 1)
        return dve.tensor_tensor(out, self.d[:, :, :], over_chunks(self.rstd[:, :]), ALU.mult)


def recurrence_phase(nc, d, g):
    with Scope(nc) as s:
        w = {m: s.sb(f"rec_w_{m}", [P, KC, DIM]) for m in ("in", "gate", "lam", "out")}
        b = {m: s.sb(f"rec_b_{m}", [P, KC]) for m in ("in", "gate", "lam", "out")}
        gamma = s.sb("rec_gamma", [P, KC])
        beta = s.sb("rec_beta", [P, KC])
        inp = s.sb("rec_inp", [P, KC, NB])
        gate = s.sb("rec_gate", [P, KC, NB])
        lam = s.sb("rec_lam", [P, KC, NB])
        neg_u = s.sb("rec_neg_u", [P, KC, NB])
        hid = s.sb("rec_hid", [P, KC, NB])
        hn = s.sb("rec_hn", [P, KC, NB])
        hg = s.sb("rec_hg", [P, KC, NB])
        in_lam_ps = s.ps("rec_in_lam_ps", [P, KC, NB])
        gate_ps = s.ps("rec_gate_ps", [P, KC, NB])
        stat_ps = s.ps("rec_stat_ps", [P, 2, NB])
        out_ps = s.ps("rec_out_ps", [P, KC, NB])
        x_loaded = s.sem("rec_x_loaded")
        more_x_loaded = s.sem("rec_more_x_loaded")
        ctx_loaded = s.sem("rec_ctx_loaded")
        loaded = s.sem("rec_loaded")
        proj_ready = {m: s.sem(f"rec_{m}_ready") for m in ("in", "gate", "lam")}
        kept = {m: s.sem(f"rec_{m}_kept") for m in ("in", "gate", "lam")}
        neg_u_done = s.sem("rec_neg_u_done")
        lam_zeroed = s.sem("rec_lam_zeroed")
        affine = s.sem("rec_affine")
        hg_ready = s.sem("rec_hg_ready")
        out_ready = s.sem("rec_out_ready")
        ln_h = LayerNorm(s, "rec_lnh", stat_ps[:, 0, :], stat_ps[:, 1, :])
        LOADS = 10
        block = s.block()

        def x_cols(i):
            return bass.ds(SHIFT + i * NB, NB)

        @block.sync
        def _(sp):
            sp.dma_start(g.xT[:, :, x_cols(0)], d["xT"][:, :, 0:NB]).then_inc(x_loaded, 16)
            sp.dma_start(g.xT[:, :, SHIFT + NB:], d["xT"][:, :, NB:]).then_inc(more_x_loaded, 16)
            sp.dma_start(g.ctxT[:, :, :], d["ctxT"]).then_inc(ctx_loaded, 16)
            sp.wait_ge(ctx_loaded, 16)

        @block.tensor
        def _(pe):
            def project(i, m):
                ps = gate_ps if m == "gate" else in_lam_ps
                for o in range(KC):
                    for k in range(KC):
                        mm = pe.matmul(ps[:, o, :], w[m][:, k, o * P:(o + 1) * P], g.xT[:, k, x_cols(i)],
                                       start=(k == 0), stop=(k == KC - 1))
                mm.then_inc(proj_ready[m], 1)

            def output(i):
                pe.wait_ge(hg_ready, i + 1)
                for o in range(KC):
                    for k in range(KC):
                        mm = pe.matmul(out_ps[:, o, :], w["out"][:, k, o * P:(o + 1) * P], hg[:, k, :],
                                       start=(k == 0), stop=(k == KC - 1))
                mm.then_inc(out_ready, 1)

            def hid_chunk(k):
                return hid[:, k, :]

            pe.wait_ge(loaded, 16 * LOADS)
            pe.wait_ge(x_loaded, 16)
            project(0, "in")
            project(0, "gate")
            pe.wait_ge(kept["in"], 1)
            project(0, "lam")
            pe.wait_ge(g.consts, 1)
            pe.wait_ge(more_x_loaded, 16)
            with pe.Fori(0, BLOCKS - 1) as i:
                pe.wait_ge(kept["lam"], i + 1)
                project(i + 1, "in")
                ln_h.mean(pe, i, hid_chunk, g.mean_mat[:, :])
                pe.wait_ge(kept["gate"], i + 1)
                project(i + 1, "gate")
                ln_h.variance(pe, i, g.mean_mat[:, :])
                pe.wait_ge(kept["in"], i + 2)
                project(i + 1, "lam")
                output(i)
            ln_h.mean(pe, BLOCKS - 1, hid_chunk, g.mean_mat[:, :])
            ln_h.variance(pe, BLOCKS - 1, g.mean_mat[:, :])
            output(BLOCKS - 1)

        @block.scalar
        def _(act):
            def keep(i, m, dst, ps, f):
                act.wait_ge(proj_ready[m], i + 1)
                for o in range(KC):
                    a = act.activation(dst[:, o, :], ps[:, o, :], f, bias=b[m][:, o:o + 1])
                a.then_inc(kept[m], 1)

            for m in ("in", "gate", "lam", "out"):
                act.dma_start(w[m][:, :, :], d[f"rec_w_{m}"]).then_inc(loaded, 16)
                act.dma_start(b[m][:, :], d[f"rec_b_{m}"]).then_inc(loaded, 16)
            act.dma_start(gamma[:, :], d["rec_gamma"]).then_inc(loaded, 16)
            act.dma_start(beta[:, :], d["rec_beta"]).then_inc(loaded, 16)
            act.wait_ge(loaded, 16 * LOADS)
            act.wait_ge(g.consts, 2)
            keep(0, "in", inp, in_lam_ps, ACT.Silu)
            keep(0, "gate", gate, gate_ps, ACT.Silu)
            keep(0, "lam", lam, in_lam_ps, ACT.Sigmoid)
            with act.Fori(0, BLOCKS - 1) as i:
                act.wait_ge(neg_u_done, i + 1)
                keep(i + 1, "in", inp, in_lam_ps, ACT.Silu)
                ln_h.squares(act, i)
                ln_h.root(act, i, g.eps[:, :])
                keep(i + 1, "lam", lam, in_lam_ps, ACT.Sigmoid)
                act.wait_ge(hg_ready, i + 1)
                keep(i + 1, "gate", gate, gate_ps, ACT.Silu)
            ln_h.squares(act, BLOCKS - 1)
            ln_h.root(act, BLOCKS - 1, g.eps[:, :])

        @block.vector
        def _(dve):
            def recurrence(i):
                dve.wait_ge(kept["in"], i + 1)
                dve.wait_ge(kept["lam"], i + 1)
                dve.scalar_tensor_tensor(out=neg_u[:, :, :], in0=lam[:, :, :], scalar=1.0, in1=inp[:, :, :],
                                         op0=ALU.subtract, op1=ALU.mult).then_inc(neg_u_done, 1)
                dve.wait_ge(neg_u_done, i + 1)
                dve.memset(lam[:, :, :].rearrange("p k (t b) -> p k t b", b=BATCH)[:, :, :, 0:1], 0.0)\
                   .then_inc(lam_zeroed, 1)
                dve.wait_ge(lam_zeroed, i + 1)
                dve.tensor_tensor_scan(hid[:, :, :].rearrange("p k n -> p (k n)"),
                                       lam[:, :, :].rearrange("p k n -> p (k n)"),
                                       neg_u[:, :, :].rearrange("p k n -> p (k n)"),
                                       0.0, ALU.mult, ALU.subtract).then_inc(ln_h.y_ready, 1)

            def normed(i):
                ln_h.deviation(dve, i, hid[:, :, :])
                ln_h.result(dve, i, hn[:, :, :]).then_inc(affine, 1)
                dve.wait_ge(affine, 2 * i + 1)
                for o in range(KC):
                    a = dve.tensor_scalar(hn[:, o, :], hn[:, o, :], gamma[:, o:o + 1], beta[:, o:o + 1],
                                          ALU.mult, ALU.add)
                a.then_inc(affine, 1)
                dve.wait_ge(affine, 2 * i + 2)
                dve.wait_ge(kept["gate"], i + 1)
                dve.tensor_tensor(hg[:, :, :], hn[:, :, :], gate[:, :, :], ALU.mult).then_inc(hg_ready, 1)

            def add_output(i):
                dve.wait_ge(out_ready, i + 1)
                for o in range(KC):
                    cols = g.xT[:, o, x_cols(i)]
                    dve.scalar_tensor_tensor(out=cols, in0=out_ps[:, o, :], scalar=b["out"][:, o:o + 1],
                                                 in1=cols, op0=ALU.add, op1=ALU.add)

            dve.memset(g.xT[:, :, 0:SHIFT], 0.0)
            dve.wait_ge(loaded, 16 * LOADS)
            recurrence(0)
            with dve.Fori(0, BLOCKS - 1) as i:
                normed(i)
                recurrence(i + 1)
                add_output(i)
            normed(BLOCKS - 1)
            add_output(BLOCKS - 1)

        @block.gpsimd
        def _(pool):
            pool.memset(g.mean_mat[:, :], 1.0 / DIM).then_inc(g.consts, 1)
            pool.memset(g.eps[:, :], LN_EPS).then_inc(g.consts, 1)
            pool.memset(g.spread[:, :, :], 0.0).then_inc(g.consts, 1)
            pool.wait_ge(g.consts, 3)
            for q in range(QUARTERS):
                pool.memset(g.spread[q * STRIP:q * STRIP + 1, q, :], 1.0)


HID = 256
GATES = 4
SRC = 512
SC = SRC // P
QW = HID // QUARTERS
UNROLL = 4
TILES = TOK // P
GATE_W = GATES * HID
ROWS = 1 + BATCH
XROWS = TOK + UNROLL * BATCH


def quarters(ap):
    return ap.rearrange("p (j c) -> p j c", j=QUARTERS)


def attention_lstm_phase(nc, d, g, next_weights):
    xg_dram = nc.dram_tensor("xg_rows", [XROWS, GATE_W], F32, kind="Internal").ap()
    with Scope(nc) as s:
        w_attn = s.sb("lstm_w_attn", [P, KC, GATE_W])
        w_hid = s.sb("lstm_w_hid", [P, KC, GATE_W])
        w_out_h = s.sb("lstm_w_out_h", [P, KC, DIM])
        keys = s.sb("lstm_keys", [P, KC, TOK])
        values = s.sb("lstm_values", [P, BATCH * SC, DIM])
        ident = s.sb("lstm_ident", [P, P])
        sel_batch = s.sb("lstm_sel_batch", [P, BATCH])

        with Scope(nc) as q:
            w_x = q.sb("lstm_w_x", [P, KC, GATE_W])
            w_q = q.sb("lstm_w_q", [P, KC, HID])
            w_out_c = q.sb("lstm_w_out_c", [P, KC, DIM])
            b_out = q.sb("lstm_b_out", [P, DIM])
            b_x = q.sb("lstm_b_x", [P, GATE_W])
            b_h = q.sb("lstm_b_h", [P, GATE_W])
            x_tile = q.sb("lstm_x_tile", [P, 2, KC, P])
            xg_tile = q.sb("lstm_xg_tile", [P, 2, GATE_W])
            loaded = q.sem("lstm_loaded")
            LOADS = 11

            def load(sp):
                loads = [(w_q[:, :, :], d["lstm_w_q"]), (w_out_c[:, :, :], d["lstm_w_out_c"]),
                         (b_out[:, :], d["lstm_b_out"].partition_broadcast(P)),
                         (b_x[:, :], d["lstm_b_ih"].partition_broadcast(P)),
                         (b_h[:, :], d["lstm_b_hh"].partition_broadcast(P)),
                         (w_x[:, :, :], d["lstm_w_x"]), (w_attn[:, :, :], d["lstm_w_attn"]),
                         (w_hid[:, :, :], d["lstm_w_hid"]), (w_out_h[:, :, :], d["lstm_w_out_h"]),
                         (sel_batch[:, :], d["sel_batch"]),
                         (ident[:, :], d["ident"])]
                for dst, src in loads:
                    sp.dma_start(dst, src).then_inc(loaded, 16)
                assert len(loads) == LOADS

            norm_phase(nc, g, "ln_recurrence", load)
            big_ps = q.ps("lstm_big_ps", [P, 2, NB])
            xg_ps = q.ps("lstm_xg_ps", [P, 2, GATE_W])
            scaled = q.sem("lstm_scaled")
            bias_sum = q.sem("lstm_bias_sum")
            kv_ready = q.sem("lstm_kv_ready")
            keys_read = q.sem("lstm_keys_read")
            values_read = q.sem("lstm_values_read")
            x_copied = q.sem("lstm_x_copied")
            xg_ready = q.sem("lstm_xg_ready")
            xg_read = q.sem("lstm_xg_read")
            xg_stored = [q.sem(f"lstm_xg_stored{n}") for n in range(2)]
            bias_stored = q.sem("lstm_bias_stored")
            block = q.block()

            @block.sync
            def _(sp):
                sp.wait_ge(bias_sum, 2)
                sp.dma_start(xg_dram[TOK:XROWS, :], b_x[0:XROWS - TOK, :]).then_inc(bias_stored, 16)
                for u in range(2):
                    sp.sem_inc(xg_stored[u], 16)
                with sp.Fori(0, TILES // 2) as i:
                    for u in range(2):
                        sp.wait_ge(xg_read, 2 * i + u + 3)
                        sp.dma_start(xg_dram[bass.ds((2 * i + u) * P, P), :], xg_tile[:, u, :])\
                          .then_inc(xg_stored[u], 16)
                for u in range(2):
                    sp.wait_ge(xg_stored[u], 16 * (TILES // 2 + 1))
                sp.wait_ge(bias_stored, 16)

            @block.tensor
            def _(pe):
                pe.wait_ge(loaded, 16 * LOADS)
                n = 0
                for o in range(KC):
                    for b in range(BATCH):
                        if n >= 2:
                            pe.wait_ge(keys_read, n - 1)
                        for k in range(KC):
                            mm = pe.matmul(big_ps[:, n % 2, :], w_q[:, k, o * P:(o + 1) * P],
                                           g.ctxT[:, k, b * SRC:(b + 1) * SRC], start=(k == 0), stop=(k == KC - 1))
                        mm.then_inc(kv_ready, 1)
                        n += 1
                for c in range(BATCH * SC):
                    if c < 2:
                        pe.wait_ge(keys_read, n - 1)
                    else:
                        pe.wait_ge(values_read, c - 1)
                    for k in range(KC):
                        mm = pe.matmul(big_ps[:, n % 2, 0:DIM], g.ctxT[:, k, c * P:(c + 1) * P], w_out_c[:, k, :],
                                       start=(k == 0), stop=(k == KC - 1))
                    mm.then_inc(kv_ready, 1)
                    n += 1
                pe.wait_ge(scaled, 1)
                pe.sem_inc(xg_ready, 2)
                with pe.Fori(0, TILES // 2) as i:
                    for u in range(2):
                        pe.wait_ge(x_copied, 2 * i + u + 1)
                        pe.wait_ge(xg_read, 2 * i + 2)
                        for half in range(2):
                            for k in range(KC):
                                mm = pe.matmul(xg_ps[:, u, half * NB:(half + 1) * NB], x_tile[:, u, k, :],
                                               w_x[:, k, half * NB:(half + 1) * NB],
                                               start=(k == 0), stop=(k == KC - 1))
                        mm.then_inc(xg_ready, 1)

            @block.scalar
            def _(act):
                for n in range(KC * BATCH):
                    o, b = n // BATCH, n % BATCH
                    act.wait_ge(kv_ready, n + 1)
                    act.mul(keys[:, o, b * SRC:(b + 1) * SRC], big_ps[:, n % 2, :], 0.5).then_inc(keys_read, 1)

            @block.gpsimd
            def _(pool):
                with pool.Fori(0, TILES // 2) as i:
                    for u in range(2):
                        pool.wait_ge(xg_ready, 2 * i + 2)
                        pool.tensor_copy(x_tile[:, u, :, :], g.xT[:, :, bass.ds(SHIFT + (2 * i + u) * P, P)])\
                            .then_inc(x_copied, 1)

            @block.vector
            def _(dve):
                dve.wait_ge(loaded, 16 * LOADS)
                dve.tensor_tensor(b_x[:, :], b_x[:, :], b_h[:, :], ALU.add).then_inc(bias_sum, 1)
                for w, f in ((w_x, 0.5), (w_attn, 0.5), (w_hid, 0.25)):
                    for k in range(KC):
                        cols = quarters(w[:, k, :])[:, :, 0:3 * QW]
                        dve.tensor_scalar(cols, cols, f, None, ALU.mult)
                for k in range(KC):
                    cols = quarters(w_hid[:, k, :])[:, :, 3 * QW:]
                    dve.tensor_scalar(cols, cols, 0.5, None, ALU.mult)
                dve.tensor_scalar(w_out_h[:, :, :], w_out_h[:, :, :], 0.5 * SRC, None, ALU.mult).then_inc(scaled, 1)
                dve.wait_ge(bias_sum, 1)
                cols = quarters(b_x[:, :])[:, :, 0:3 * QW]
                dve.tensor_scalar(cols, cols, 0.5, None, ALU.mult).then_inc(bias_sum, 1)
                for c in range(BATCH * SC):
                    n = KC * BATCH + c
                    dve.wait_ge(kv_ready, n + 1)
                    dve.tensor_tensor(values[:, c, :], big_ps[:, n % 2, 0:DIM], b_out[:, :], ALU.add).then_inc(values_read, 1)
                dve.wait_ge(bias_sum, 2)
                dve.sem_inc(xg_read, 2)
                with dve.Fori(0, TILES // 2) as i:
                    for u in range(2):
                        dve.wait_ge(xg_ready, 2 * i + u + 3)
                        dve.wait_ge(xg_stored[u], 16 * (i + 1))
                        dve.tensor_tensor(xg_tile[:, u, :], xg_ps[:, u, :], b_x[:, :], ALU.add).then_inc(xg_read, 1)

        HALF_SRC = SRC // 2
        with Scope(nc) as q:
            xg = q.sb("lstm_xg", [P, UNROLL, GATE_W])
            attn = q.sb("lstm_attn", [P, KC, ROWS])  
            hid = q.sb("lstm_hid", [P, KC, STRIP])
            cell = q.sb("lstm_cell", [P, GATES + 1, QW])
            uv = q.sb("lstm_uv", [P, 2, QW])
            tanh_c = q.sb("lstm_tanh_c", [P, QW])
            h_row = q.sb("lstm_h_row", [P, QW])
            neg_max = q.sb("lstm_neg_max", [P, 2])
            neg_max_all = q.sb("lstm_neg_max_all", [P, 1])
            expo = q.sb("lstm_expo", [P, 2, HALF_SRC])
            total = q.sb("lstm_total", [P, 2])
            shrink = q.sb("lstm_shrink", [P, 2])
            shrunk = q.sb("lstm_shrunk", [P, 2])
            total_sum = q.sb("lstm_total_sum", [P, 1])
            inverse = q.sb("lstm_inverse", [P, 1])
            factor = q.sb("lstm_factor", [P, 2])
            first_row = q.sb("lstm_first_row", [P, DIM])
            alpha = q.sb("lstm_alpha", [P, SC, BATCH])
            out_row = q.sb("lstm_out_row", [P, DIM])
            ifg_ps = q.ps("lstm_ifg_ps", [P, NB])[:, 0:3 * QW]
            attn_bank = q.ps("lstm_attn_ps", [P, NB])
            attn_ps = attn_bank[:, 0:KC * BATCH].rearrange("p (k b) -> p k b", k=KC)
            score_ps = q.ps("lstm_score_ps", [P, 2, NB])
            alpha_ps = q.ps("lstm_alpha_ps", [P, NB])
            first_ps = q.ps("lstm_first_ps", [P, NB])
            second_ps = q.ps("lstm_second_ps", [P, KC, NB])
            turned_ps = [alpha_ps[:, 0:P], attn_bank[:, P:2 * P], alpha_ps[:, 2 * P:3 * P], alpha_ps[:, 3 * P:4 * P]]
            second_turned_ps = alpha_ps[:, 2 * P:4 * P]
            TURNS = ((0,), (1,), (2, 3))
            o_gate_ps = first_ps[:, DIM:DIM + QW]
            xg_zeroed = q.sem("lstm_xg_zeroed")
            zeroed = q.sem("lstm_zeroed")
            xg_loaded = [q.sem(f"lstm_xg_loaded{n}") for n in range(UNROLL)]
            xg_used = q.sem("lstm_xg_used")
            ifg_ready = q.sem("lstm_ifg_ready")
            ifg_tanh = q.sem("lstm_ifg_tanh")
            o_ready = q.sem("lstm_o_ready")
            o_tanh = q.sem("lstm_o_tanh")
            uv_ready = q.sem("lstm_uv_ready")
            c_ready = q.sem("lstm_c_ready")
            c_tanh = q.sem("lstm_c_tanh")
            h_row_ready = q.sem("lstm_h_row_ready")
            h_ready = q.sem("lstm_h_ready")
            scores_ready = q.sem("lstm_scores_ready")
            max_ready = q.sem("lstm_max_ready")
            exp_ready = q.sem("lstm_exp_ready")
            max_all_ready = q.sem("lstm_max_all_ready")
            shrink_ready = q.sem("lstm_shrink_ready")
            shrunk_ready = q.sem("lstm_shrunk_ready")
            factor_ready = q.sem("lstm_factor_ready")
            first_row_ready = q.sem("lstm_first_row_ready")
            total_ready = q.sem("lstm_total_ready")
            inverse_ready = q.sem("lstm_inverse_ready")
            alpha_turned = q.sem("lstm_alpha_turned")
            alpha_ready = q.sem("lstm_alpha_ready")
            out_ready = q.sem("lstm_out_ready")
            out_row_ready = q.sem("lstm_out_row_ready")
            attn_turned = q.sem("lstm_attn_turned")
            attn_ready = q.sem("lstm_attn_ready")
            attn_kept = q.sem("lstm_attn_kept")
            block = q.block()

            def x_rows(t):
                return xg_dram[bass.ds(t * BATCH, BATCH), :]

            @block.sync
            def _(sp):
                sp.wait_ge(xg_zeroed, 1)
                for u in range(UNROLL):
                    sp.dma_start(xg[1:ROWS, u, :], x_rows(u)).then_inc(xg_loaded[u], 16)
                for ei in range(2):
                    next_weights.load(sp, ei)
                with sp.Fori(0, SEQ // UNROLL) as i:
                    for u in range(UNROLL):
                        t = i * UNROLL + u
                        sp.wait_ge(xg_used, t + 1)
                        sp.dma_start(xg[1:ROWS, u, :], x_rows(t + UNROLL)).then_inc(xg_loaded[u], 16)
                for u in range(UNROLL):
                    sp.wait_ge(xg_loaded[u], 16 * (SEQ // UNROLL + 1))

            @block.tensor
            def _(pe):
                def rows_of(ps, j):
                    return ps[j * STRIP:j * STRIP + ROWS, :]

                WHOLE = (0, 3 * QW)
                HALVES = ((0, 3 * QW // 2), (3 * QW // 2, 3 * QW))

                def ifg(j, part=WHOLE):
                    return slice(j * HID + QW + part[0], j * HID + QW + part[1])

                def o_gate(j):
                    return slice(j * HID, j * HID + QW)

                def x_part(u):
                    for j in range(QUARTERS):
                        pe.matmul(rows_of(ifg_ps, j), ident[:, 0:ROWS], xg[:, u % UNROLL, ifg(j)],
                                  start=True, stop=False)

                def gate_part(w, col, k, last, part=WHOLE):
                    for j in range(QUARTERS):
                        mm = pe.matmul(rows_of(ifg_ps[:, part[0]:part[1]], j), col[:, k, 0:ROWS], w[:, k, ifg(j, part)],
                                       start=False, stop=last)
                    return mm

                def o_sums(u):
                    for j in range(QUARTERS):
                        mm = pe.matmul(rows_of(o_gate_ps, j), ident[:, 0:ROWS], xg[:, u, o_gate(j)], start=True, stop=False)
                    mm.then_inc(xg_used, 1)
                    for w, col in ((w_hid, hid), (w_attn, attn)):
                        for k in range(KC):
                            for j in range(QUARTERS):
                                mm = pe.matmul(rows_of(o_gate_ps, j), col[:, k, 0:ROWS], w[:, k, o_gate(j)],
                                               start=False, stop=w is w_attn and k == KC - 1)
                    mm.then_inc(o_ready, 1)

                def batch_rows(ps, n, b):
                    return ps[b * STRIP:b * STRIP + 1, 0:n]

                def hidden_part(o):
                    cols = slice(o * P, (o + 1) * P)
                    for k in range(KC):
                        pe.matmul(rows_of(first_ps[:, cols], k), hid[:, k, 0:ROWS], w_out_h[:, k, cols], start=(o == 0), stop=False)

                def turn(n):
                    for c in TURNS[n]:
                        mm = pe.transpose(turned_ps[c], expo[:, c // 2, c % 2 * P:(c % 2 + 1) * P], ident[:, :])
                    mm.then_inc(alpha_turned, 1)

                def context_first(c):
                    for b in range(BATCH):
                        mm = pe.matmul(batch_rows(first_ps, DIM, b), alpha[:, c, b:b + 1],
                                       values[:, b * SC + c, :], start=(c == 0 and b >= KC), stop=(c == 1))
                    return mm

                def context_second(o):
                    for c in (2, 3):
                        for b in range(BATCH):
                            mm = pe.matmul(batch_rows(second_ps[:, o, :], P, b), alpha[:, c, b:b + 1],
                                           values[:, b * SC + c, o * P:(o + 1) * P], start=(c == 2), stop=(c == 3))
                    return mm

                pe.wait_ge(zeroed, 1)
                pe.wait_ge(xg_loaded[0], 16)
                x_part(0)
                for k in range(KC):
                    gate_part(w_hid, hid, k, False)
                with pe.Fori(0, SEQ // UNROLL) as i:
                    for u in range(UNROLL):
                        t = i * UNROLL + u
                        pe.wait_ge(attn_ready, t + 1)
                        gate_part(w_attn, attn, 0, False)
                        gate_part(w_attn, attn, 1, True).then_inc(ifg_ready, 1)
                        o_sums(u)
                        nxt = (u + 1) % UNROLL
                        pe.wait_ge(xg_loaded[nxt], 16 * (i + (2 if nxt == 0 else 1)))
                        pe.wait_ge(ifg_tanh, t + 1)
                        x_part(u + 1)
                        pe.wait_ge(h_ready, t + 1)
                        for half in range(2):
                            for k in range(KC):
                                for b in range(BATCH):
                                    lo = b * SRC + half * HALF_SRC
                                    mm = pe.matmul(batch_rows(score_ps[:, half, :], HALF_SRC, b), hid[:, k, 1 + b:2 + b],
                                                   keys[:, k, lo:lo + HALF_SRC], start=(k == 0), stop=(k == KC - 1))
                            mm.then_inc(scores_ready, 1)
                        hidden_part(0)
                        pe.wait_ge(exp_ready, 2 * t + 1)
                        turn(0)
                        turn(1)
                        hidden_part(1)
                        pe.wait_ge(alpha_ready, 3 * t + 1)
                        context_first(0)
                        pe.wait_ge(exp_ready, 2 * t + 2)
                        turn(2)
                        pe.wait_ge(alpha_ready, 3 * t + 2)
                        context_first(1).then_inc(out_ready, 1)
                        pe.wait_ge(alpha_ready, 3 * t + 3)
                        for o in range(KC):
                            context_second(o).then_inc(out_ready, 1)
                        gate_part(w_hid, hid, 0, False, HALVES[0])
                        for o in range(KC):
                            pe.wait_ge(out_row_ready, 2 * t + o + 1)
                            mm = pe.matmul(attn_ps[:, o, :], out_row[:, o * P:(o + 1) * P], sel_batch[:, :],
                                           start=True, stop=True)
                            if o == 0:
                                gate_part(w_hid, hid, 0, False, HALVES[1])
                        mm.then_inc(attn_turned, 1)
                        gate_part(w_hid, hid, 1, False)
                pe.wait_ge(attn_ready, SEQ + 1)
                for k in range(KC):
                    gate_part(w_attn, attn, k, k == KC - 1)

            @block.scalar
            def _(act):
                act.wait_ge(zeroed, 1)
                act.activation(tanh_c[:, :], cell[:, GATES, :], ACT.Tanh)
                act.sem_inc(attn_ready, 1)
                with act.Fori(0, SEQ // UNROLL) as i:
                    for u in range(UNROLL):
                        t = i * UNROLL + u
                        act.wait_ge(ifg_ready, t + 1)
                        act.activation(cell[:, 1:GATES, :].rearrange("p n q -> p (n q)"), ifg_ps, ACT.Tanh)\
                           .then_inc(ifg_tanh, 1)
                        act.wait_ge(o_ready, t + 1)
                        act.activation(cell[:, 0, :], o_gate_ps, ACT.Tanh).then_inc(o_tanh, 1)
                        act.wait_ge(c_ready, t + 1)
                        act.activation(tanh_c[:, :], cell[:, GATES, :], ACT.Tanh, scale=0.5).then_inc(c_tanh, 1)
                        for half in range(2):
                            act.wait_ge(max_ready, 2 * t + half + 1)
                            act.activation(expo[:, half, :], score_ps[:, half, 0:HALF_SRC], ACT.Exp, bias=neg_max[:, half:half + 1],
                                           accum_out=total[:, half:half + 1]).then_inc(exp_ready, 1)
                        act.wait_ge(max_all_ready, t + 1)
                        act.activation(shrink[:, :], neg_max[:, :], ACT.Exp, scale=-1.0, bias=neg_max_all[:, :])\
                           .then_inc(shrink_ready, 1)
                        act.wait_ge(out_ready, 3 * t + 1)
                        act.wait_ge(factor_ready, t + 1)
                        for k in range(KC):
                            cols = slice(k * P, (k + 1) * P)
                            act.mul(first_row[:, cols], first_ps[:, cols], factor[:, 0:1]).then_inc(first_row_ready, 1)
                        act.wait_ge(attn_turned, t + 1)
                        act.wait_ge(attn_kept, t + 1)
                        act.activation(attn[:, :, 1:ROWS], attn_ps, ACT.Tanh).then_inc(attn_ready, 1)

            @block.vector
            def _(dve):
                def keep_turned(t, n):
                    dve.wait_ge(alpha_turned, 3 * t + n + 1)
                    c, many = TURNS[n][0], len(TURNS[n])
                    turned = (second_turned_ps if many > 1 else turned_ps[c]).rearrange("p (c b r) -> p c b r", b=BATCH, r=STRIP)
                    dve.tensor_copy(alpha[:, c:c + many, :], turned[:, :, :, 0]).then_inc(alpha_ready, 1)

                for ps in (ifg_ps, score_ps[:, :, :], first_ps[:, :], second_ps[:, :, :]):
                    dve.memset(ps, 0.0)
                dve.memset(cell[:, :, :], 0.0)
                dve.memset(hid[:, :, :], 0.0)
                dve.memset(attn[:, :, :], 0.0).then_inc(zeroed, 1)
                with dve.Fori(0, SEQ // UNROLL) as i:
                    for u in range(UNROLL):
                        t = i * UNROLL + u
                        dve.wait_ge(ifg_tanh, t + 1)
                        dve.scalar_tensor_tensor(out=uv[:, :, :], in0=cell[:, 1:3, :], scalar=1.0,
                                                 in1=cell[:, 3:5, :], op0=ALU.add, op1=ALU.mult).then_inc(uv_ready, 1)
                        dve.wait_ge(uv_ready, t + 1)
                        dve.scalar_tensor_tensor(out=cell[:, GATES, :], in0=uv[:, 1, :], scalar=0.5,
                                                 in1=uv[:, 0, :], op0=ALU.mult, op1=ALU.add).then_inc(c_ready, 1)
                        dve.wait_ge(c_tanh, t + 1)
                        dve.wait_ge(o_tanh, t + 1)
                        dve.scalar_tensor_tensor(out=h_row[:, :], in0=cell[:, 0, :], scalar=1.0,
                                                 in1=tanh_c[:, :], op0=ALU.add, op1=ALU.mult).then_inc(h_row_ready, 1)
                        dve.wait_ge(h_row_ready, t + 1)
                        dve.transpose(hid[:, :, :], h_row[:, :].rearrange("p (k c) -> p k c", k=KC)).then_inc(h_ready, 1)
                        for half in range(2):
                            dve.wait_ge(scores_ready, 2 * t + half + 1)
                            dve.tensor_reduce(neg_max[:, half:half + 1], score_ps[:, half, 0:HALF_SRC], AX_X, ALU.max, negate=True)\
                               .then_inc(max_ready, 1)
                        keep_turned(t, 0)
                        keep_turned(t, 1)
                        dve.wait_ge(max_ready, 2 * t + 2)
                        dve.tensor_tensor(neg_max_all[:, :], neg_max[:, 0:1], neg_max[:, 1:2], ALU.min).then_inc(max_all_ready, 1)
                        dve.wait_ge(shrink_ready, t + 1)
                        dve.tensor_tensor(shrunk[:, :], total[:, :], shrink[:, :], ALU.mult).then_inc(shrunk_ready, 1)
                        dve.wait_ge(shrunk_ready, t + 1)
                        dve.tensor_tensor(total_sum[:, :], shrunk[:, 0:1], shrunk[:, 1:2], ALU.add).then_inc(total_ready, 1)
                        keep_turned(t, 2)
                        dve.wait_ge(total_ready, t + 1)
                        dve.reciprocal(inverse[:, :], total_sum[:, :]).then_inc(inverse_ready, 1)
                        dve.wait_ge(inverse_ready, t + 1)
                        dve.tensor_scalar(factor[:, :], shrink[:, :], inverse[:, 0:1], None, ALU.mult).then_inc(factor_ready, 1)
                        for k in range(KC):
                            cols = slice(k * P, (k + 1) * P)
                            dve.wait_ge(out_ready, 3 * t + k + 2)
                            dve.wait_ge(first_row_ready, 2 * t + k + 1)
                            dve.scalar_tensor_tensor(out=out_row[:, cols], in0=second_ps[:, k, 0:P], scalar=factor[:, 1:2],
                                                     in1=first_row[:, cols], op0=ALU.mult, op1=ALU.add).then_inc(out_row_ready, 1)

            @block.gpsimd
            def _(pool):
                pool.memset(xg[:, :, :], 0.0).then_inc(xg_zeroed, 1)
                pool.sem_inc(attn_kept, 1)
                with pool.Fori(0, SEQ // UNROLL) as i:
                    for u in range(UNROLL):
                        t = i * UNROLL + u
                        cols = g.xT[:, :, bass.ds(SHIFT + t * BATCH, BATCH)]
                        pool.wait_ge(attn_ready, t + 2)
                        pool.tensor_tensor(cols, cols, attn[:, :, 1:ROWS], ALU.add).then_inc(attn_kept, 1)


def norm_phase(nc, g, name, load=None, out=None):
    QT = NB // QUARTERS
    with Scope(nc) as s:
        mean_ps = s.ps(f"{name}_mean_ps", [P, BLOCKS, NB])
        var_ps = s.ps(f"{name}_var_ps", [P, 2, NB])[:, :, 0:QT]
        rstd_ps = s.ps(f"{name}_rstd_ps", [P, 2, NB])
        d = s.sb(f"{name}_d", [P, BLOCKS, KC, NB])
        sq = s.sb(f"{name}_sq", [P, BLOCKS, KC, NB])
        rstd = s.sb(f"{name}_rstd", [P, BLOCKS, QT])
        mean_ready = s.sem(f"{name}_mean_ready")
        d_ready = s.sem(f"{name}_d_ready")
        sq_ready = s.sem(f"{name}_sq_ready")
        var_ready = s.sem(f"{name}_var_ready")
        std_ready = s.sem(f"{name}_std_ready")
        rstd_ready = s.sem(f"{name}_rstd_ready")
        spread = s.sem(f"{name}_spread")
        x_done = s.sem(f"{name}_x_done")
        stored = s.sem(f"{name}_stored")
        block = s.block()

        def x_cols(i):
            return g.xT[:, :, SHIFT + i * NB:SHIFT + (i + 1) * NB]

        @block.sync
        def _(sp):
            if load is not None:
                load(sp)
            if out is not None:
                for i in range(BLOCKS):
                    sp.wait_ge(x_done, i + 1)
                    sp.dma_start(out[:, :, i * NB:(i + 1) * NB], x_cols(i)).then_inc(stored, 16)
                sp.wait_ge(stored, 16 * BLOCKS)

        @block.tensor
        def _(pe):
            def means(i):
                for k in range(KC):
                    mm = pe.matmul(mean_ps[:, i, :], g.mean_mat[:, :], x_cols(i)[:, k, :], start=(k == 0), stop=(k == KC - 1))
                mm.then_inc(mean_ready, 1)

            def variances(i):
                pe.wait_ge(sq_ready, i + 1)
                if i >= 2:
                    pe.wait_ge(std_ready, i - 1)
                for k in range(KC):
                    for q in range(QUARTERS):
                        mm = pe.matmul(var_ps[q * STRIP:(q + 1) * STRIP, i % 2, :], g.mean_mat[:, 0:STRIP],
                                       sq[:, i, k, q * QT:(q + 1) * QT], start=(k == 0), stop=(k == KC - 1))
                mm.then_inc(var_ready, 1)

            def spread_rstd(i):
                pe.wait_ge(rstd_ready, i + 1)
                if i >= 2:
                    pe.wait_ge(x_done, i - 1)
                for q in range(QUARTERS):
                    mm = pe.matmul(rstd_ps[:, i % 2, q * QT:(q + 1) * QT], g.spread[:, q, :], rstd[:, i, :], start=True, stop=True)
                mm.then_inc(spread, 1)

            means(0)
            for i in range(BLOCKS):
                if i + 1 < BLOCKS:
                    means(i + 1)
                variances(i)
                if i > 0:
                    spread_rstd(i - 1)
            spread_rstd(BLOCKS - 1)

        @block.scalar
        def _(act):
            def squares(i):
                act.wait_ge(d_ready, i + 1)
                act.activation(sq[:, i, :, :], d[:, i, :, :], ACT.Square).then_inc(sq_ready, 1)

            squares(0)
            for i in range(BLOCKS):
                if i + 1 < BLOCKS:
                    squares(i + 1)
                act.wait_ge(var_ready, i + 1)
                act.activation(rstd[:, i, :], var_ps[:, i % 2, :], ACT.Sqrt, bias=g.eps[:, :]).then_inc(std_ready, 1)

        @block.vector
        def _(dve):
            def deviation(i):
                dve.wait_ge(mean_ready, i + 1)
                dve.tensor_tensor(d[:, i, :, :], x_cols(i), over_chunks(mean_ps[:, i, :]), ALU.subtract).then_inc(d_ready, 1)

            def result(i):
                dve.wait_ge(spread, i + 1)
                dve.tensor_tensor(x_cols(i), d[:, i, :, :], over_chunks(rstd_ps[:, i % 2, :]), ALU.mult).then_inc(x_done, 1)

            deviation(0)
            for i in range(BLOCKS):
                if i + 1 < BLOCKS:
                    deviation(i + 1)
                if i > 0:
                    result(i - 1)
                dve.wait_ge(std_ready, i + 1)
                dve.reciprocal(rstd[:, i, :], rstd[:, i, :]).then_inc(rstd_ready, 1)
            result(BLOCKS - 1)


TOP = 2
TB = NB // P


class Router:

    def __init__(self, s, name, experts, softmax_first, rows_ps, cols_ps):
        E = self.n = experts
        self.softmax_first = softmax_first
        self.rows_ps, self.cols_ps = rows_ps, cols_ps
        self.logit_rows = s.sb(f"{name}_logit_rows", [E, NB])
        self.logits = s.sb(f"{name}_logits", [P, TB, E])
        self.expo = s.sb(f"{name}_expo", [P, TB, E])
        self.above = s.sb(f"{name}_above", [P, TB, E, E])
        self.same = s.sb(f"{name}_same", [P, TB, E, E])
        self.before = s.sb(f"{name}_before", [P, E, E])
        self.rank = s.sb(f"{name}_rank", [P, TB, E])
        self.total = s.sb(f"{name}_total", [P, TB])
        self.weights = s.sb(f"{name}_weights", [P, TB, E])
        self.weight_rows = s.sb(f"{name}_weight_rows", [E, TOK])
        self.filled = s.sem(f"{name}_filled")
        self.logit_rows_summed = s.sem(f"{name}_logit_rows_summed")
        self.logit_rows_ready = s.sem(f"{name}_logit_rows_ready")
        self.logits_turned = s.sem(f"{name}_logits_turned")
        self.shifted = s.sem(f"{name}_shifted")
        self.expo_ready = s.sem(f"{name}_expo_ready")
        self.step = s.sem(f"{name}_step")
        self.weights_ready = s.sem(f"{name}_weights_ready")
        self.weights_turned = s.sem(f"{name}_weights_turned")
        self.weight_rows_ready = s.sem(f"{name}_weight_rows_ready")
        self.STEPS = 14 if softmax_first else 10

    def gpsimd(self, pool):
        pool.memset(self.before[:, :, :], 0.0).then_inc(self.filled, 1)
        pool.wait_ge(self.filled, 1)
        for e in range(1, self.n):
            ins = pool.memset(self.before[:, e, 0:e], 1.0)
        ins.then_inc(self.filled, 1)

    def sum_logits(self, pe, n, w, x):
        for k in range(KC):
            mm = pe.matmul(self.rows_ps, w[:, k, :], x(k), start=(k == 0), stop=(k == KC - 1))
        mm.then_inc(self.logit_rows_summed, 1)

    def turn_logits(self, pe, n, ident):
        pe.wait_ge(self.logit_rows_ready, n + 1)
        for c in range(TB):
            mm = pe.matmul(self.cols_ps[:, c, :], self.logit_rows[:, c * P:(c + 1) * P],
                           ident[0:self.n, 0:self.n], start=True, stop=True)
        mm.then_inc(self.logits_turned, 1)

    def turn_weights(self, pe, n, ident):
        pe.wait_ge(self.weights_ready, n + 1)
        for c in range(TB):
            mm = pe.matmul(self.rows_ps[:, c * P:(c + 1) * P], self.weights[:, c, :], ident, start=True, stop=True)
        mm.then_inc(self.weights_turned, 1)

    def keep_logits(self, act, n, bias):
        act.wait_ge(self.logit_rows_summed, n + 1)
        act.activation(self.logit_rows[:, :], self.rows_ps, ACT.Identity, bias=bias).then_inc(self.logit_rows_ready, 1)

    def keep_weights(self, act, n):
        act.wait_ge(self.shifted, n + 1)
        act.activation(self.expo[:, :, :], self.expo[:, :, :], ACT.Exp).then_inc(self.expo_ready, 1)
        act.wait_ge(self.weights_turned, n + 1)
        act.copy(self.weight_rows[:, bass.ds(n * NB, NB)], self.rows_ps).then_inc(self.weight_rows_ready, 1)

    def vector(self, dve, n):
        E, at = self.n, [0]

        def then(ins):
            at[0] += 1
            ins.then_inc(self.step, 1)
            dve.wait_ge(self.step, n * self.STEPS + at[0])

        def spread(ap):
            return ap.unsqueeze(2).to_broadcast([P, TB, E])

        def own(ap):
            return ap.unsqueeze(3).to_broadcast([P, TB, E, E])

        def other(ap):
            return ap.unsqueeze(2).to_broadcast([P, TB, E, E])

        dve.wait_ge(self.logits_turned, n + 1)
        then(dve.tensor_copy(self.logits[:, :, :], self.cols_ps))
        then(dve.tensor_reduce(self.total[:, :], self.logits[:, :, :], AX_X, ALU.max))
        dve.tensor_tensor(self.expo[:, :, :], self.logits[:, :, :], spread(self.total[:, :]), ALU.subtract)\
           .then_inc(self.shifted, 1)
        dve.wait_ge(self.expo_ready, n + 1)
        if self.softmax_first:
            then(dve.tensor_reduce(self.total[:, :], self.expo[:, :, :], AX_X, ALU.add))
            then(dve.reciprocal(self.total[:, :], self.total[:, :]))
            then(dve.tensor_tensor(self.expo[:, :, :], self.expo[:, :, :], spread(self.total[:, :]), ALU.mult))
        ranked = self.expo[:, :, :] if self.softmax_first else self.logits[:, :, :]
        dve.tensor_tensor(self.above[:, :, :, :], other(ranked), own(ranked), ALU.is_gt)
        then(dve.tensor_tensor(self.same[:, :, :, :], other(ranked), own(ranked), ALU.is_equal))
        then(dve.tensor_tensor(self.same[:, :, :, :], self.same[:, :, :, :],
                               self.before[:, :, :].unsqueeze(1).to_broadcast([P, TB, E, E]), ALU.mult))
        then(dve.tensor_tensor(self.above[:, :, :, :], self.above[:, :, :, :], self.same[:, :, :, :], ALU.add))
        then(dve.tensor_reduce(self.rank[:, :, :], self.above[:, :, :, :], AX_X, ALU.add))
        then(dve.tensor_scalar(self.rank[:, :, :], self.rank[:, :, :], float(TOP), None, ALU.is_lt))
        then(dve.tensor_tensor(self.weights[:, :, :], self.rank[:, :, :], self.expo[:, :, :], ALU.mult))
        then(dve.tensor_reduce(self.total[:, :], self.weights[:, :, :], AX_X, ALU.add))
        if self.softmax_first:
            then(dve.tensor_scalar(self.total[:, :], self.total[:, :], 1e-20, None, ALU.add))
        then(dve.reciprocal(self.total[:, :], self.total[:, :]))
        dve.tensor_tensor(self.weights[:, :, :], self.weights[:, :, :], spread(self.total[:, :]), ALU.mult)\
           .then_inc(self.weights_ready, 1)
        assert at[0] == self.STEPS


class Experts:

    def __init__(self, name, routed, shared, inner, softmax_first):
        self.name, self.routed, self.softmax_first, self.inner = name, routed, softmax_first, inner
        self.order = [routed] * shared + list(range(routed))
        self.chunks = -(-inner // P)
        self.rows = -(-inner // self.chunks)
        self.last_rows = inner - (self.chunks - 1) * self.rows

    def rows_of(self, c):
        return self.rows if c < self.chunks - 1 else self.last_rows


class RawWeights:

    LOADS = 4

    def __init__(self, s, d, x):
        self.d, self.x = d, x
        self.gu = s.sb(f"{x.name}_raw_gu", [P, 2, 2, KC * x.inner])
        self.down = s.sb(f"{x.name}_raw_down", [P, 2, x.chunks * DIM])
        self.loaded = [s.sem(f"{x.name}_raw_loaded{n}") for n in range(2)]

    def load(self, sp, ei):
        x, buf, e = self.x, ei % 2, self.x.order[ei]
        for m, name in enumerate(("gate", "up")):
            sp.dma_start(self.gu[:, buf, m, :].rearrange("p (k n) -> p k n", k=KC), self.d[f"{x.name}_w_{name}"][e])\
              .then_inc(self.loaded[buf], 16)
        full = (x.chunks - 1) * x.rows
        down = self.d[f"{x.name}_w_down"][e]
        kept = self.down[:, buf, :].rearrange("p (c n) -> p c n", c=x.chunks)
        sp.dma_start(kept[0:x.rows, 0:x.chunks - 1, :], down[0:full, :].rearrange("(c p) n -> p c n", p=x.rows))\
          .then_inc(self.loaded[buf], 16)
        sp.dma_start(kept[0:x.last_rows, x.chunks - 1, :], down[full:x.inner, :]).then_inc(self.loaded[buf], 16)


def mixture_phase(nc, d, g, x, raw):
    E, IC, INNER = x.routed, x.chunks, x.inner
    PAIRS = BLOCKS // 2
    NP = 2 * IC
    HI, LO = range(2)
    with Scope(nc) as s:
        w_router = s.sb(f"{x.name}_w_router", [P, KC, E])
        b_router = s.sb(f"{x.name}_b_router", [E, 1])
        pick = s.sb(f"{x.name}_pick", [E, E, P])
        ident = s.sb(f"{x.name}_ident", [P, P])
        loaded = s.sem(f"{x.name}_loaded")
        LOADS = 4 if f"{x.name}_b_router" in d else 3

        def load(sp):
            sp.dma_start(w_router[:, :, :], d[f"{x.name}_w_router"]).then_inc(loaded, 16)
            sp.dma_start(pick[:, :, :], d["pick"][0:E, 0:E, :]).then_inc(loaded, 16)
            sp.dma_start(ident[:, :], d["ident"]).then_inc(loaded, 16)
            if LOADS == 4:
                sp.dma_start(b_router[:, :], d[f"{x.name}_b_router"]).then_inc(loaded, 16)

        norm_phase(nc, g, f"{x.name}_ln", load)
        w_gu = s.sb(f"{x.name}_w_gu", [P, 2, 2, 2, KC * INNER], F32R)
        w_down = s.sb(f"{x.name}_w_down", [P, 2, 2, IC * DIM], F32R)
        x_in = s.sb(f"{x.name}_x_in", [P, 2, KC, TOK], F32R)
        gu = s.sb(f"{x.name}_gu", [P, 2, NB])
        gu_in = s.sb(f"{x.name}_gu_in", [P, 2, 2, NB], F32R)
        spread = s.sb(f"{x.name}_spread", [P, NB])
        part = s.sb(f"{x.name}_part", [P, KC, NB])
        gate_ps = s.ps(f"{x.name}_gate_ps", [P, 2, NB])
        up_ps = s.ps(f"{x.name}_up_ps", [P, 2, NB])
        down_ps = s.ps(f"{x.name}_down_ps", [P, KC, NB])
        aux_ps = s.ps(f"{x.name}_aux_ps", [P, 2, NB])
        zeroed = s.sem(f"{x.name}_zeroed")
        w_hi = s.sem(f"{x.name}_w_hi")
        gu_w_lo = s.sem(f"{x.name}_gu_w_lo")
        down_w_lo = s.sem(f"{x.name}_down_w_lo")
        x_hi = s.sem(f"{x.name}_x_hi")
        x_lo = s.sem(f"{x.name}_x_lo")
        gate_ready = s.sem(f"{x.name}_gate_ready")
        up_ready = s.sem(f"{x.name}_up_ready")
        silu_ready = s.sem(f"{x.name}_silu_ready")
        gu_ready = s.sem(f"{x.name}_gu_ready")
        gu_hi = s.sem(f"{x.name}_gu_hi")
        gu_lo = s.sem(f"{x.name}_gu_lo")
        spread_turned = s.sem(f"{x.name}_spread_turned")
        spread_ready = s.sem(f"{x.name}_spread_ready")
        down_ready = s.sem(f"{x.name}_down_ready")
        down_used = s.sem(f"{x.name}_down_used")
        x_done = s.sem(f"{x.name}_x_done")
        router = Router(s, f"{x.name}_router", E, x.softmax_first, aux_ps[0:E, 0, :],
                        aux_ps[:, 1, 0:TB * E].rearrange("p (c e) -> p c e", e=E))
        spread_ps = aux_ps[:, 1, :]
        block = s.block()

        def down_parts(ap):
            full = (IC - 1) * DIM
            return ap[0:x.rows, 0:full], ap[0:x.last_rows, full:]

        def weighted(ei):
            return x.order[ei] < E

        def before(ei):
            return sum(weighted(n) for n in range(ei))

        def x_cols(i):
            return g.xT[:, :, bass.ds(SHIFT + i * NB, NB)]

        @block.sync
        def _(sp):
            for ei in range(2, len(x.order)):
                sp.wait_ge(gu_w_lo, 2 * (ei - 1))
                sp.wait_ge(down_w_lo, ei - 1)
                raw.load(sp, ei)

        @block.tensor
        def _(pe):
            PASSES = ((HI, HI), (HI, LO), (LO, HI))

            pe.wait_ge(loaded, 16 * LOADS)
            for ei, e in enumerate(x.order):
                buf = ei % 2

                def up_and_gate(i, n, gn):
                    c = n % IC
                    m = x.rows_of(c)
                    pe.wait_ge(gu_ready, gn + 1)
                    for which, ps, ready in ((0, gate_ps, gate_ready), (1, up_ps, up_ready)):
                        for w_part, x_part in PASSES:
                            for k in range(KC):
                                lo = k * INNER + c * x.rows
                                mm = pe.matmul(ps[0:m, n % 2, :], w_gu[:, buf, w_part, which, lo:lo + m],
                                               x_in[:, x_part, k, bass.ds(i * NB, NB)],
                                               start=(w_part == HI and x_part == HI and k == 0),
                                               stop=(w_part == LO and k == KC - 1))
                        mm.then_inc(ready, 1)

                def down(n, gn, blk):
                    c = n % IC
                    m = x.rows_of(c)
                    if c == 0:
                        pe.wait_ge(down_used, blk + 1)
                    pe.wait_ge(gu_hi, gn + 1)
                    for w_part, x_part in ((HI, HI), (LO, HI), (HI, LO)):
                        if x_part == LO:
                            pe.wait_ge(gu_lo, gn + 3)
                        for o in range(KC):
                            lo = c * DIM + o * P
                            mm = pe.matmul(down_ps[:, o, :], w_down[0:m, buf, w_part, lo:lo + P], gu_in[0:m, n % 2, x_part, :],
                                           start=(c == 0 and w_part == HI and x_part == HI),
                                           stop=(c == IC - 1 and x_part == LO))
                    if c == IC - 1:
                        mm.then_inc(down_ready, 1)

                def spread_weights(i, blk):
                    pe.wait_ge(spread_ready, blk + 1)
                    pe.matmul(spread_ps, pick[:, e, :], router.weight_rows[:, bass.ds(i * NB, NB)], start=True, stop=True)\
                      .then_inc(spread_turned, 1)

                pe.wait_ge(gu_w_lo, 2 * (ei + 1))
                pe.wait_ge(down_w_lo, ei + 1)
                with pe.Fori(0, PAIRS) as ii:
                    for u in range(2):
                        i = 2 * ii + u
                        blk = ei * BLOCKS + i
                        w_blk = before(ei) * BLOCKS + i
                        if ei == 0:
                            pe.wait_ge(x_lo, i + 1)
                        elif weighted(ei):
                            spread_weights(i, w_blk)
                        for c in range(IC):
                            n = u * IC + c
                            gn = (ei * PAIRS + ii) * NP + n
                            up_and_gate(i, n, gn)
                            if n > 0 and (ei > 0 or c > 0):
                                down(n - 1, gn - 1, blk if c > 0 else blk - 1)
                            if ei == 0 and c == 0:
                                router.sum_logits(pe, i, w_router, lambda k: g.xT[:, k, bass.ds(SHIFT + i * NB, NB)])
                            if ei == 0 and c == 1:
                                router.turn_logits(pe, i, ident[:, :])
                        if u == 1 or ei == 0:
                            down(u * IC + IC - 1, (ei * PAIRS + ii) * NP + u * IC + IC - 1, blk)
                        if ei == 0:
                            router.turn_weights(pe, i, ident[:, :])
                            pe.wait_ge(router.weight_rows_ready, i + 1)
                            if weighted(0):
                                spread_weights(i, w_blk)

        @block.scalar
        def _(act):
            def split_weights(ei):
                buf = ei % 2
                act.wait_ge(raw.loaded[buf], 16 * raw.LOADS * (ei // 2 + 1))
                for m in range(2):
                    act.copy(w_gu[:, buf, HI, m, :], raw.gu[:, buf, m, :]).then_inc(w_hi, 1)
                for high, of in zip(down_parts(w_down[:, buf, HI, :]), down_parts(raw.down[:, buf, :])):
                    ins = act.copy(high, of)
                ins.then_inc(w_hi, 1)

            split_weights(0)
            act.wait_ge(loaded, 16 * LOADS)
            act.wait_ge(zeroed, 1)
            act.sem_inc(spread_ready, 1)
            for ei in range(len(x.order)):
                def keep_spread(i):
                    w_blk = before(ei) * BLOCKS + i
                    act.wait_ge(spread_turned, w_blk + 1)
                    act.wait_ge(down_used, ei * BLOCKS + i + 1)
                    act.copy(spread[:, :], spread_ps).then_inc(spread_ready, 1)

                if ei + 1 < len(x.order):
                    if ei > 0:
                        act.wait_ge(down_used, ei * BLOCKS + 1)
                    split_weights(ei + 1)
                with act.Fori(0, PAIRS) as ii:
                    for u in range(2):
                        i = 2 * ii + u
                        for c in range(IC):
                            n = u * IC + c
                            m = x.rows_of(c)
                            gn = (ei * PAIRS + ii) * NP + n
                            act.wait_ge(gu_lo, gn + 1)
                            act.wait_ge(gate_ready, gn + 1)
                            act.activation(gu[0:m, n % 2, :], gate_ps[0:m, n % 2, :], ACT.Silu).then_inc(silu_ready, 1)
                            if ei == 0 and c == 0:
                                router.keep_logits(act, i, b_router[:, :])
                            if ei > 0 and weighted(ei) and c == 1:
                                keep_spread(i)
                        if ei == 0:
                            router.keep_weights(act, i)
                            if weighted(ei):
                                keep_spread(i)

        @block.vector
        def _(dve):
            def split_weights(ei):
                buf = ei % 2
                for m in range(2):
                    dve.wait_ge(w_hi, 3 * ei + m + 1)
                    dve.tensor_tensor(w_gu[:, buf, LO, m, :], raw.gu[:, buf, m, :], w_gu[:, buf, HI, m, :].bitcast(F32), ALU.subtract)\
                       .then_inc(gu_w_lo, 1)

            dve.sem_inc(gu_ready, 2)
            dve.sem_inc(down_used, 1)
            def split_x(i):
                cols = slice(i * NB, (i + 1) * NB)
                whole = g.xT[:, :, SHIFT + i * NB:SHIFT + (i + 1) * NB]
                dve.tensor_copy(x_in[:, HI, :, cols], whole).then_inc(x_hi, 1)
                dve.wait_ge(x_hi, i + 1)
                dve.tensor_tensor(x_in[:, LO, :, cols], whole, x_in[:, HI, :, cols].bitcast(F32), ALU.subtract).then_inc(x_lo, 1)

            split_x(0)
            split_weights(0)
            for i in range(1, BLOCKS):
                split_x(i)
            dve.wait_ge(router.filled, 2)
            for ei in range(len(x.order)):
                def add_block(i):
                    blk = ei * BLOCKS + i
                    dve.wait_ge(down_ready, blk + 1)
                    if weighted(ei):
                        w_blk = before(ei) * BLOCKS + i
                        dve.wait_ge(spread_ready, w_blk + 2)
                        dve.wait_ge(x_done, w_blk + 1)
                        dve.tensor_tensor(part[:, :, :], down_ps[:, :, :], over_chunks(spread[:, :]), ALU.mult).then_inc(down_used, 1)
                    else:
                        dve.tensor_tensor(x_cols(i), down_ps[:, :, :], x_cols(i), ALU.add).then_inc(down_used, 1)

                if ei + 1 < len(x.order):
                    split_weights(ei + 1)
                with dve.Fori(0, PAIRS) as ii:
                    for u in range(2):
                        i = 2 * ii + u
                        for c in range(IC):
                            n = u * IC + c
                            m = x.rows_of(c)
                            gn = (ei * PAIRS + ii) * NP + n
                            dve.wait_ge(silu_ready, gn + 1)
                            dve.wait_ge(up_ready, gn + 1)
                            dve.tensor_tensor(gu[0:m, n % 2, :], gu[0:m, n % 2, :], up_ps[0:m, n % 2, :], ALU.mult)\
                               .then_inc(gu_ready, 1)
                            dve.wait_ge(gu_ready, gn + 3)
                            dve.tensor_copy(gu_in[0:m, n % 2, HI, :], gu[0:m, n % 2, :]).then_inc(gu_hi, 1)
                            if u == 1 and c == 0 and ei > 0:
                                add_block(i - 1)
                        if ei == 0:
                            router.vector(dve, i)
                        if u == 1 or ei == 0:
                            add_block(i)

        @block.gpsimd
        def _(pool):
            def low_part(low, whole, high):
                return pool.tensor_tensor(low, whole, high.bitcast(F32), ALU.subtract)

            def split_weights(ei):
                buf = ei % 2
                pool.wait_ge(w_hi, 3 * ei + 3)
                for parts in zip(*(down_parts(ap) for ap in (w_down[:, buf, LO, :], raw.down[:, buf, :], w_down[:, buf, HI, :]))):
                    ins = low_part(*parts)
                ins.then_inc(down_w_lo, 1)

            if LOADS == 3:
                pool.memset(b_router[:, :], 0.0).then_inc(zeroed, 1)
            else:
                pool.sem_inc(zeroed, 1)
            router.gpsimd(pool)
            pool.sem_inc(gu_lo, 2)
            pool.sem_inc(x_done, 1)
            split_weights(0)
            for ei in range(len(x.order)):
                def add_block(i):
                    blk = ei * BLOCKS + i
                    pool.wait_ge(down_used, blk + 2)
                    pool.tensor_tensor(x_cols(i), x_cols(i), part[:, :, :], ALU.add).then_inc(x_done, 1)

                if ei + 1 < len(x.order):
                    split_weights(ei + 1)
                with pool.Fori(0, PAIRS) as ii:
                    for u in range(2):
                        i = 2 * ii + u
                        for c in range(IC):
                            n = u * IC + c
                            m = x.rows_of(c)
                            gn = (ei * PAIRS + ii) * NP + n
                            pool.wait_ge(gu_hi, gn + 1)
                            low_part(gu_in[0:m, n % 2, LO, :], gu[0:m, n % 2, :], gu_in[0:m, n % 2, HI, :]).then_inc(gu_lo, 1)
                            if u == 1 and c == 0 and ei > 0 and weighted(ei):
                                add_block(i - 1)
                        if (u == 1 or ei == 0) and weighted(ei):
                            add_block(i)


HEADS, HD = 16, 16
HALF = HD // 2
LORA = 64
LORA_G = 128
STEPS = P // BATCH
UNIT_KEY, DECAY, B_IN, KEY, RECV, VALUE = range(6)
SCAN_IN = 6
MIXES = "rwkva"
OWN, LAST = range(2)


def heads(ap):
    return ap.rearrange("p (h j) -> p h j", j=HD)


def per_head(ap):
    return ap.unsqueeze(2).to_broadcast([P, HEADS, HD])


def each_row(ap):
    shape = list(ap.shape)
    return ap.unsqueeze(len(shape) - 1).to_broadcast([*shape[:-1], HALF, HD])


def rwkv_phase(nc, d, g):
    with Scope(nc) as s:
        mix_w = s.sb("rw_mix_w", [P, len(MIXES), KC])
        w = {m: s.sb(f"rw_w_{m}", [P, 2, KC, DIM]) for m in ("r", "k", "v", "kk")}
        wa = {m: s.sb(f"rw_wa_{m}", [P, 2, KC, LORA]) for m in "wa"}
        wa_g = s.sb("rw_wa_g", [P, KC, LORA_G])
        wb = {m: s.sb(f"rw_wb_{m}", [n, DIM]) for m, n in (("w", LORA), ("a", LORA), ("g", LORA_G))}
        w_o = s.sb("rw_w_o", [P, KC, DIM])
        rows = s.sb("rw_rows", [P, 8, DIM])
        W_BIAS, A_BIAS, G_BIAS, K_K, K_A, R_K, GN_W, GN_B = range(8)
        less_k_a = s.sb("rw_less_k_a", [P, DIM])
        ident = s.sb("rw_ident", [P, P])
        loaded = s.sem("rw_loaded")
        LOADS = 1 + 3 + 3 + 3 + 1 + 8 + 1

        def load(sp):
            sp.dma_start(mix_w[:, :, :], d["rw_mix_w"]).then_inc(loaded, 16)
            for m in "rkv":
                sp.dma_start(w[m][:, OWN, :, :], d[f"rw_w_{m}"]).then_inc(loaded, 16)
            for m in "wa":
                sp.dma_start(wa[m][:, OWN, :, :], d[f"rw_wa_{m}"]).then_inc(loaded, 16)
            sp.dma_start(wa_g[:, :, :], d["rw_wa_g"]).then_inc(loaded, 16)
            for m in "wag":
                sp.dma_start(wb[m][:, :], d[f"rw_wb_{m}"]).then_inc(loaded, 16)
            sp.dma_start(w_o[:, :, :], d["rw_w_o"]).then_inc(loaded, 16)
            for n, m in enumerate(("w_bias", "a_bias", "g_bias", "k_k", "k_a", "r_k", "gn_w", "gn_b")):
                sp.dma_start(rows[:, n, :], d[f"rw_{m}"].partition_broadcast(P)).then_inc(loaded, 16)
            sp.dma_start(ident[:, :], d["ident"]).then_inc(loaded, 16)

        norm_phase(nc, g, "ln_mixture0", load)
        first = s.sb("rw_first", [P, P])
        x_in = s.sb("rw_x_in", [P, 2, KC, P])
        r_col = s.sb("rw_r_col", [P, KC, P])
        lora_w = s.sb("rw_lora_w", [LORA, P])
        lora_a = s.sb("rw_lora_a", [LORA, P])
        lora_g = s.sb("rw_lora_g", [P, P])
        sig = s.sb("rw_sig", [P, 2, DIM])
        k = s.sb("rw_k", [P, DIM])
        kk = s.sb("rw_kk", [P, DIM])
        kk_sq = s.sb("rw_kk_sq", [P, DIM])
        kk_norm = s.sb("rw_kk_norm", [P, HEADS])
        k_scale = s.sb("rw_k_scale", [P, DIM])
        rk = s.sb("rw_rk", [P, DIM])
        rk_sum = s.sb("rw_rk_sum", [P, HEADS])
        q = s.sb("rw_q", [P, SCAN_IN, DIM])
        gate = s.sb("rw_gate", [P, 2, DIM])
        bonus = s.sb("rw_bonus", [P, 2, DIM])
        sc = s.sb("rw_sc", [P, 2, SCAN_IN - 1, HD, STEPS])
        sc_value = s.sb("rw_sc_value", [P, 2, HALF, STEPS])
        vk = s.sb("rw_vk", [P, 2, STEPS, HALF, HD])
        state = s.sb("rw_state", [P, 2, STEPS + 1, HALF, HD])
        sa_terms = s.sb("rw_sa_terms", [P, HALF, HD])
        decayed = s.sb("rw_decayed", [P, HALF, HD])
        sa = s.sb("rw_sa", [P, HALF])
        sab = s.sb("rw_sab", [P, HALF, HD])
        kept = s.sb("rw_kept", [P, HALF, HD])
        o_terms = s.sb("rw_o_terms", [P, STEPS, HALF, HD])
        o_scan = s.sb("rw_o_scan", [P, HALF, STEPS])
        o = s.sb("rw_o", [P, DIM])
        mean = s.sb("rw_mean", [P, HEADS])
        dev = s.sb("rw_dev", [P, DIM])
        dev_sq = s.sb("rw_dev_sq", [P, DIM])
        var = s.sb("rw_var", [P, HEADS])
        gated = s.sb("rw_gated", [P, DIM])
        o_col = s.sb("rw_o_col", [P, KC, P])
        rv_ps = s.ps("rw_rv_ps", [P, 2, DIM])
        k_ps = s.ps("rw_k_ps", [P, 2, DIM])
        wa_ps = s.ps("rw_wa_ps", [P, 2, DIM])
        g_ps = s.ps("rw_g_ps", [P, NB])
        col_ps = s.ps("rw_col_ps", [P, 4, P])
        lg_ps = s.ps("rw_lg_ps", [P, NB])
        o_col_ps = s.ps("rw_o_col_ps", [P, KC, P])
        y_ps = s.ps("rw_y_ps", [P, KC, P])
        w_step = s.sem("rw_w_step")
        w_mixed = s.sem("rw_w_mixed")
        x_copied = s.sem("rw_x_copied")
        cols_ready = s.sem("rw_cols_ready")
        rkv_ready = s.sem("rw_rkv_ready")
        inner_ready = s.sem("rw_inner_ready")
        outer_ready = s.sem("rw_outer_ready")
        lg_ready = s.sem("rw_lg_ready")
        lg_act = s.sem("rw_lg_act")
        g_ready = s.sem("rw_g_ready")
        zeroed = s.sem("rw_zeroed")
        sig_ready = s.sem("rw_sig_ready")
        decay_ready = s.sem("rw_decay_ready")
        rv_ready = s.sem("rw_rv_ready")
        kk_ready = s.sem("rw_kk_ready")
        kk_sq_ready = s.sem("rw_kk_sq_ready")
        kk_sum_ready = s.sem("rw_kk_sum_ready")
        kk_floored = s.sem("rw_kk_floored")
        kk_norm_ready = s.sem("rw_kk_norm_ready")
        kk_inverse = s.sem("rw_kk_inverse")
        k_step = s.sem("rw_k_step")
        key_ready = s.sem("rw_key_ready")
        unit_key_ready = s.sem("rw_unit_key_ready")
        b_in_ready = s.sem("rw_b_in_ready")
        rk_ready = s.sem("rw_rk_ready")
        rk_summed = s.sem("rw_rk_summed")
        bonus_ready = s.sem("rw_bonus_ready")
        kv_turned = s.sem("rw_kv_turned")
        q_turned = s.sem("rw_q_turned")
        gate_ready = s.sem("rw_gate_ready")
        vk_ready = s.sem("rw_vk_ready")
        sa_terms_ready = s.sem("rw_sa_terms_ready")
        decayed_ready = s.sem("rw_decayed_ready")
        sa_ready = s.sem("rw_sa_ready")
        sab_ready = s.sem("rw_sab_ready")
        state_ready = s.sem("rw_state_ready")
        o_terms_ready = s.sem("rw_o_terms_ready")
        o_summed = s.sem("rw_o_summed")
        o_turned = s.sem("rw_o_turned")
        o_sum_ready = s.sem("rw_o_sum_ready")
        mean_ready = s.sem("rw_mean_ready")
        dev_ready = s.sem("rw_dev_ready")
        dev_sq_ready = s.sem("rw_dev_sq_ready")
        var_ready = s.sem("rw_var_ready")
        std_ready = s.sem("rw_std_ready")
        std_inverse = s.sem("rw_std_inverse")
        normed = s.sem("rw_normed")
        affine = s.sem("rw_affine")
        gated_ready = s.sem("rw_gated_ready")
        gated_turned = s.sem("rw_gated_turned")
        o_col_ready = s.sem("rw_o_col_ready")
        y_ready = s.sem("rw_y_ready")
        x_done = s.sem("rw_x_done")
        block = s.block()

        def tiles(engine, tile):
            tile(0, 0, True, False)
            with engine.Fori(0, TILES // 2 - 1) as i:
                for u in (1, 2):
                    tile(2 * i + u, u % 2, True, True)
            tile(TILES - 1, 1, False, True)

        def tokens(c, before=0):
            cols = g.xT[:, :, bass.ds(SHIFT * (1 - before) + c * P, P)]
            return cols.rearrange("p k (t b) -> p k b t", b=BATCH)

        def by_batch(ap):
            return ap.rearrange("p k (b t) -> p k b t", b=BATCH)

        @block.tensor
        def _(pe):
            def sums(out, lhs, rhs):
                for part in (OWN, LAST):
                    for k in range(KC):
                        mm = pe.matmul(out, lhs(part, k), rhs(part, k), start=(part == OWN and k == 0),
                                       stop=(part == LAST and k == KC - 1))
                return mm

            def x(part, k):
                return x_in[:, part, k, :]

            def project(m):
                pe.wait_ge(x_copied, m + 1)
                for o_ in range(KC):
                    sums(col_ps[:, o_, :], lambda part, k: w["r"][:, part, k, o_ * P:(o_ + 1) * P], x)
                sums(col_ps[0:LORA, 2, :], lambda part, k: wa["w"][:, part, k, :], x)
                sums(col_ps[0:LORA, 3, :], lambda part, k: wa["a"][:, part, k, :], x).then_inc(cols_ready, 1)
                for ps, name in ((k_ps[:, 0, :], "k"), (k_ps[:, 1, :], "kk"), (rv_ps[:, 0, :], "r"), (rv_ps[:, 1, :], "v")):
                    mm = sums(ps, x, lambda part, k: w[name][:, part, k, :])
                mm.then_inc(rkv_ready, 1)
                pe.wait_ge(inner_ready, m + 1)
                for k in range(KC):
                    mm = pe.matmul(lg_ps[:, 0:P], wa_g[:, k, :], r_col[:, k, :], start=(k == 0), stop=(k == KC - 1))
                mm.then_inc(lg_ready, 1)
                for n, (inner, m_) in enumerate(((lora_w, "w"), (lora_a, "a"))):
                    pe.matmul(wa_ps[:, n, :], first[:, :], rows[:, (W_BIAS, A_BIAS)[n], :], start=True, stop=False)
                    mm = pe.matmul(wa_ps[:, n, :], inner[:, :], wb[m_][:, :], start=False, stop=True)
                mm.then_inc(outer_ready, 1)
                pe.wait_ge(lg_act, m + 1)
                pe.matmul(g_ps[:, 0:DIM], first[:, :], rows[:, G_BIAS, :], start=True, stop=False)
                pe.matmul(g_ps[:, 0:DIM], lora_g[:, :], wb["g"][:, :], start=False, stop=True).then_inc(g_ready, 1)

            def output(c):
                pe.wait_ge(gated_ready, c + 1)
                for k in range(KC):
                    mm = pe.transpose(o_col_ps[:, k, :], gated[:, k * P:(k + 1) * P], ident[:, :])
                mm.then_inc(gated_turned, 1)
                pe.wait_ge(o_col_ready, c + 1)
                for o_ in range(KC):
                    for k in range(KC):
                        mm = pe.matmul(y_ps[:, o_, :], w_o[:, k, o_ * P:(o_ + 1) * P], o_col[:, k, :],
                                       start=(k == 0), stop=(k == KC - 1))
                mm.then_inc(y_ready, 1)

            def tile(c, parity, has_next, has_last):
                if has_next:
                    pe.wait_ge(gate_ready, c + 1)
                    project(c + 1)
                if has_last:
                    output(c - 1)

            pe.wait_ge(loaded, 16 * LOADS)
            pe.wait_ge(zeroed, 2)
            pe.wait_ge(w_mixed, 1)
            project(0)
            tiles(pe, tile)
            output(TILES - 1)

        @block.scalar
        def _(act):
            def copy_x(m):
                act.copy(by_batch(x_in[:, LAST, :, :]), tokens(m, before=1))
                act.copy(by_batch(x_in[:, OWN, :, :]), tokens(m)).then_inc(x_copied, 1)

            def project_products(m):
                act.wait_ge(cols_ready, m + 1)
                act.copy(r_col[:, :, :], col_ps[:, 0:KC, :])
                act.copy(lora_a[:, :], col_ps[0:LORA, 3, :])
                act.activation(lora_w[:, :], col_ps[0:LORA, 2, :], ACT.Tanh).then_inc(inner_ready, 1)
                act.wait_ge(rkv_ready, m + 1)
                act.copy(q[:, RECV, :], rv_ps[:, 0, :])
                act.copy(q[:, VALUE, :], rv_ps[:, 1, :]).then_inc(rv_ready, 1)
                act.activation(kk_sq[:, :], k_ps[:, 1, :], ACT.Square).then_inc(kk_sq_ready, 1)
                act.copy(k[:, :], k_ps[:, 0, :])
                act.copy(kk[:, :], k_ps[:, 1, :]).then_inc(kk_ready, 1)
                act.wait_ge(lg_ready, m + 1)
                act.activation(lora_g[:, :], lg_ps[:, 0:P], ACT.Sigmoid).then_inc(lg_act, 1)
                act.wait_ge(outer_ready, m + 1)
                act.activation(sig[:, :, :], wa_ps[:, :, :], ACT.Sigmoid).then_inc(sig_ready, 1)
                act.wait_ge(sig_ready, m + 1)
                act.mul(q[:, DECAY, :], sig[:, 0, :], math.exp(-0.5)).then_inc(decay_ready, 1)

            def project_norm(m):
                act.wait_ge(kk_floored, m + 1)
                act.activation(kk_norm[:, :], kk_norm[:, :], ACT.Sqrt).then_inc(kk_norm_ready, 1)

            def project_gate(m, parity):
                act.wait_ge(g_ready, m + 1)
                act.copy(gate[:, parity, :], g_ps[:, 0:DIM]).then_inc(gate_ready, 1)

            def output_square(c):
                act.wait_ge(o_sum_ready, c + 1)
                act.mul(mean[:, :], mean[:, :], 1.0 / HD).then_inc(mean_ready, 1)
                act.wait_ge(dev_ready, c + 1)
                act.activation(dev_sq[:, :], dev[:, :], ACT.Square).then_inc(dev_sq_ready, 1)

            def output_std(c):
                act.wait_ge(var_ready, c + 1)
                act.activation(var[:, :], var[:, :], ACT.Sqrt, scale=1.0 / HD, bias=g.eps[:, :]).then_inc(std_ready, 1)

            def output_columns(c):
                act.wait_ge(gated_turned, c + 1)
                act.copy(o_col[:, :, :], o_col_ps[:, :, :]).then_inc(o_col_ready, 1)

            def tile(c, parity, has_next, has_last):
                if has_next:
                    copy_x(c + 1)
                    act.wait_ge(q_turned, c + 1)
                    act.wait_ge(bonus_ready, c + 1)
                    project_products(c + 1)
                    project_norm(c + 1)
                if has_last:
                    output_square(c - 1)
                    output_std(c - 1)
                    output_columns(c - 1)
                if has_next:
                    project_gate(c + 1, 1 - parity)

            copy_x(0)
            project_products(0)
            project_norm(0)
            project_gate(0, 0)
            tiles(act, tile)
            output_square(TILES - 1)
            output_std(TILES - 1)
            output_columns(TILES - 1)

        @block.gpsimd
        def _(pool):
            FOLDS = (8, 4, 2, 1)
            assert 2 * FOLDS[0] == HD

            def output_terms(c, parity, part):
                t = slice(part * STEPS // 2, (part + 1) * STEPS // 2)
                pool.wait_ge(state_ready, c * STEPS + t.stop + 1)
                after = state[:, parity, t.start + 1:t.stop + 1, :, :]
                pool.tensor_tensor(o_terms[:, t, :, :], after, each_row(sc[:, parity, RECV, :, t].rearrange("p j t -> p t j")),
                                   ALU.mult).then_inc(o_terms_ready, 1)
                for n, half in enumerate(FOLDS):
                    pool.wait_ge(o_terms_ready, (2 * c + part) * len(FOLDS) + n + 1)
                    low, high = o_terms[:, t, :, 0:half], o_terms[:, t, :, half:2 * half]
                    if half > 1:
                        pool.tensor_tensor(low, low, high, ALU.add).then_inc(o_terms_ready, 1)
                    else:
                        sums = o_scan[:, :, t].rearrange("p i t -> p t i").unsqueeze(3)
                        pool.tensor_tensor(sums, low, high, ALU.add).then_inc(o_summed, 1)

            def output_dev(c):
                pool.wait_ge(mean_ready, c + 1)
                pool.tensor_tensor(heads(dev[:, :]), heads(o[:, :]), per_head(mean[:, :]), ALU.subtract).then_inc(dev_ready, 1)

            def output_gate(c, parity):
                pool.wait_ge(std_inverse, c + 1)
                pool.tensor_tensor(heads(dev[:, :]), heads(dev[:, :]), per_head(var[:, :]), ALU.mult).then_inc(normed, 1)
                pool.wait_ge(normed, c + 1)
                steps = ((dev, dev, rows[:, GN_W, :], ALU.mult), (dev, dev, rows[:, GN_B, :], ALU.add),
                         (dev, dev, bonus[:, parity, :], ALU.add), (gated, dev, gate[:, parity, :], ALU.mult))
                for n, (out, a, b, op) in enumerate(steps):
                    ins = pool.tensor_tensor(out[:, :], a[:, :], b, op)
                    if n < len(steps) - 1:
                        ins.then_inc(affine, 1)
                        pool.wait_ge(affine, c * (len(steps) - 1) + n + 1)
                ins.then_inc(gated_ready, 1)

            def project_key(m):
                pool.wait_ge(sig_ready, m + 1)
                pool.tensor_tensor(k_scale[:, :], sig[:, 1, :], rows[:, K_A, :], ALU.mult).then_inc(k_step, 1)
                pool.wait_ge(k_step, 2 * m + 1)
                pool.tensor_tensor(k_scale[:, :], k_scale[:, :], less_k_a[:, :], ALU.add).then_inc(k_step, 1)
                pool.wait_ge(k_step, 2 * m + 2)
                pool.wait_ge(kk_ready, m + 1)
                pool.tensor_tensor(q[:, KEY, :], k_scale[:, :], k[:, :], ALU.mult).then_inc(key_ready, 1)
                pool.wait_ge(key_ready, m + 1)
                pool.wait_ge(rv_ready, m + 1)
                pool.tensor_tensor(rk[:, :], q[:, RECV, :], q[:, KEY, :], ALU.mult).then_inc(rk_ready, 1)
                pool.wait_ge(rk_ready, 2 * m + 1)
                pool.tensor_tensor(rk[:, :], rk[:, :], rows[:, R_K, :], ALU.mult).then_inc(rk_ready, 1)

            def project_unit_key(m):
                pool.wait_ge(kk_inverse, m + 1)
                pool.tensor_tensor(heads(q[:, UNIT_KEY, :]), heads(kk[:, :]), per_head(kk_norm[:, :]), ALU.mult).then_inc(unit_key_ready, 1)
                pool.wait_ge(unit_key_ready, m + 1)
                pool.tensor_tensor(q[:, B_IN, :], q[:, UNIT_KEY, :], sig[:, 1, :], ALU.mult).then_inc(b_in_ready, 1)

            def project_bonus(m, parity):
                pool.wait_ge(rk_summed, m + 1)
                pool.tensor_tensor(heads(bonus[:, parity, :]), heads(q[:, VALUE, :]), per_head(rk_sum[:, :]), ALU.mult)\
                    .then_inc(bonus_ready, 1)

            def project_vk(m, parity):
                pool.wait_ge(kv_turned, m + 1)
                for part in range(2):
                    t = slice(part * STEPS // 2, (part + 1) * STEPS // 2)
                    pool.tensor_tensor(vk[:, parity, t, :, :],
                                       sc_value[:, parity, :, t].rearrange("p i t -> p t i").unsqueeze(3)
                                       .to_broadcast([P, STEPS // 2, HALF, HD]),
                                       each_row(sc[:, parity, KEY, :, t].rearrange("p j t -> p t j")), ALU.mult).then_inc(vk_ready, 1)

            def tile(c, parity, has_next, has_last):
                if has_last:
                    output_terms(c - 1, 1 - parity, 1)
                if has_next:
                    project_key(c + 1)
                if has_last:
                    output_dev(c - 1)
                if has_next:
                    project_unit_key(c + 1)
                    project_vk(c + 1, 1 - parity)
                if has_last:
                    output_gate(c - 1, 1 - parity)
                if has_next:
                    project_bonus(c + 1, 1 - parity)
                output_terms(c, parity, 0)

            pool.memset(first[:, :], 0.0).then_inc(zeroed, 1)
            pool.wait_ge(zeroed, 1)
            pool.memset(first[0:1, :], 1.0).then_inc(zeroed, 1)
            pool.wait_ge(w_mixed, 1)
            project_key(0)
            project_unit_key(0)
            project_vk(0, 0)
            project_bonus(0, 0)
            tiles(pool, tile)
            output_terms(TILES - 1, 1, 1)
            output_dev(TILES - 1)
            output_gate(TILES - 1, 1)

        @block.vector
        def _(dve):
            def turn_blocks(parity, n):
                rows_of = q[:, n, :].rearrange("p (h j) -> p j h", j=HD).unsqueeze(2).to_broadcast([P, HD, 2, HEADS])
                return dve.transpose(sc[:, parity, n, :, :].rearrange("p j (f h) -> p j f h", f=2), rows_of)

            def project(t, m, parity):
                if t == 6:
                    dve.wait_ge(kk_sq_ready, m + 1)
                    dve.tensor_reduce(kk_norm[:, :], heads(kk_sq[:, :]), AX_X, ALU.add).then_inc(kk_sum_ready, 1)
                elif t == 7:
                    dve.wait_ge(kk_sum_ready, m + 1)
                    dve.tensor_scalar(kk_norm[:, :], kk_norm[:, :], 1e-24, None, ALU.max).then_inc(kk_floored, 1)
                elif t == 9:
                    dve.wait_ge(rv_ready, m + 1)
                    turn_blocks(parity, RECV)
                elif t == 10:
                    dve.wait_ge(kk_norm_ready, m + 1)
                    dve.reciprocal(kk_norm[:, :], kk_norm[:, :]).then_inc(kk_inverse, 1)
                elif t == 11:
                    rows_of = q[:, VALUE, :].rearrange("p (h f i) -> p i f h", f=2, i=HALF)
                    dve.transpose(sc_value[:, parity, :, :].rearrange("p i (f h) -> p i f h", f=2), rows_of)
                elif t == 12:
                    dve.wait_ge(key_ready, m + 1)
                    turn_blocks(parity, KEY).then_inc(kv_turned, 1)
                elif t == 13:
                    dve.wait_ge(rk_ready, 2 * m + 2)
                    dve.tensor_reduce(rk_sum[:, :], heads(rk[:, :]), AX_X, ALU.add).then_inc(rk_summed, 1)
                elif t == 15:
                    dve.wait_ge(decay_ready, m + 1)
                    turn_blocks(parity, DECAY)
                elif t == 17:
                    dve.wait_ge(b_in_ready, m + 1)
                    turn_blocks(parity, UNIT_KEY)
                elif t == 18:
                    turn_blocks(parity, B_IN).then_inc(q_turned, 1)

            def output(t, c):
                if t == 8:
                    dve.wait_ge(o_summed, 2 * c + 2)
                    dve.transpose(o[:, :].rearrange("p (h f i) -> p i f h", f=2, i=HALF),
                                  o_scan[:, :, :].rearrange("p i (f h) -> p i f h", f=2)).then_inc(o_turned, 1)
                elif t == 9:
                    dve.wait_ge(o_turned, c + 1)
                    dve.tensor_reduce(mean[:, :], heads(o[:, :]), AX_X, ALU.add).then_inc(o_sum_ready, 1)
                elif t == 14:
                    dve.wait_ge(dev_sq_ready, c + 1)
                    dve.tensor_reduce(var[:, :], heads(dev_sq[:, :]), AX_X, ALU.add).then_inc(var_ready, 1)
                elif t == 17:
                    dve.wait_ge(std_ready, c + 1)
                    dve.reciprocal(var[:, :], var[:, :]).then_inc(std_inverse, 1)
                elif t == 31:
                    dve.wait_ge(y_ready, c + 1)
                    x = tokens(c)
                    dve.tensor_tensor(x, x, by_batch(y_ps[:, :, :]), ALU.add).then_inc(x_done, 1)

            def tile(c, parity, has_next, has_last):
                dve.wait_ge(q_turned, c + 1)
                for t in range(STEPS):
                    if t % (STEPS // 2) == 0:
                        dve.wait_ge(vk_ready, 2 * c + t // (STEPS // 2) + 1)
                    n = c * STEPS + t
                    before = state[:, 1 - parity, STEPS, :, :] if t == 0 else state[:, parity, t, :, :]
                    if has_next:
                        project(t, c + 1, 1 - parity)
                    dve.wait_ge(state_ready, n + 1)
                    dve.tensor_tensor(sa_terms[:, :, :], before, each_row(sc[:, parity, UNIT_KEY, :, t]), ALU.mult)\
                       .then_inc(sa_terms_ready, 1)
                    dve.tensor_tensor(decayed[:, :, :], before, each_row(sc[:, parity, DECAY, :, t]), ALU.mult)\
                       .then_inc(decayed_ready, 1)
                    dve.wait_ge(sa_terms_ready, n + 1)
                    dve.tensor_reduce(sa[:, :], sa_terms[:, :, :], AX_X, ALU.add).then_inc(sa_ready, 1)
                    dve.wait_ge(decayed_ready, n + 1)
                    dve.tensor_tensor(kept[:, :, :], decayed[:, :, :], vk[:, parity, t, :, :], ALU.add)
                    dve.wait_ge(sa_ready, n + 1)
                    dve.tensor_tensor(sab[:, :, :], sa[:, :].unsqueeze(2).to_broadcast([P, HALF, HD]),
                                      each_row(sc[:, parity, B_IN, :, t]), ALU.mult).then_inc(sab_ready, 1)
                    if has_last:
                        output(t, c - 1)
                    dve.wait_ge(sab_ready, n + 1)
                    dve.tensor_tensor(state[:, parity, t + 1, :, :], kept[:, :, :], sab[:, :, :], ALU.subtract).then_inc(state_ready, 1)

            dve.wait_ge(loaded, 16 * LOADS)
            for n, name in enumerate(MIXES):
                of = w[name] if name in w else wa[name]
                for k_ in range(KC):
                    dve.tensor_scalar(of[:, LAST, k_, :], of[:, OWN, k_, :], mix_w[:, n, k_:k_ + 1], None, ALU.mult)
            dve.tensor_scalar(less_k_a[:, :], rows[:, K_A, :], -1.0, 1.0, ALU.mult, ALU.add).then_inc(w_step, 1)
            dve.wait_ge(w_step, 1)
            for name in MIXES:
                of = w[name] if name in w else wa[name]
                ins = dve.tensor_tensor(of[:, OWN, :, :], of[:, OWN, :, :], of[:, LAST, :, :], ALU.subtract)
            ins.then_inc(w_step, 1)
            dve.wait_ge(w_step, 2)
            ins = dve.tensor_tensor(w["kk"][:, :, :, :].rearrange("p a k n -> p (a k) n"), w["k"][:, :, :, :].rearrange("p a k n -> p (a k) n"),
                                    over_chunks(rows[:, K_K, :], 2 * KC), ALU.mult)
            ins.then_inc(w_mixed, 1)
            dve.memset(state[:, 1, STEPS, :, :], 0.0).then_inc(state_ready, 1)
            for t in range(STEPS):
                project(t, 0, 0)
            tiles(dve, tile)
            for t in range(STEPS):
                output(t, TILES - 1)


QC = SEQ // P
SCALE = float(DIM) ** -0.5


def cross_attention_phase(nc, d, g, next_weights):
    with Scope(nc) as s:
        w = {m: s.sb(f"ca_w_{m}", [P, KC, DIM]) for m in ("q", "k", "v")}
        b = {m: s.sb(f"ca_b_{m}", [P, KC]) for m in ("q", "k", "v")}
        ident = s.sb("ca_ident", [P, P])
        ctx_all = s.sb("ca_ctx_all", [P, KC, BATCH * SRC])
        ctx = s.sb("ca_ctx", [P, KC, SRC])
        x = s.sb("ca_x", [P, KC, SEQ])
        q = s.sb("ca_q", [P, KC, SEQ])
        k_ = s.sb("ca_k", [P, KC, SRC])
        v = s.sb("ca_v", [P, SC, DIM])
        neg_max = s.sb("ca_neg_max", [P, QC])
        total = s.sb("ca_total", [P, QC])
        prob = s.sb("ca_prob", [P, QC, SRC])
        prob_t = s.sb("ca_prob_t", [P, SC, SEQ])
        loaded = s.sem("ca_loaded")
        LOADS = 8

        def load(sp):
            sp.dma_start(ctx_all[:, :, :], d["ctxT"]).then_inc(loaded, 16)
            for m in ("q", "k", "v"):
                sp.dma_start(w[m][:, :, :], d[f"ca_w_{m}"]).then_inc(loaded, 16)
                sp.dma_start(b[m][:, :], d[f"ca_b_{m}"]).then_inc(loaded, 16)
            sp.dma_start(ident[:, :], d["ident"]).then_inc(loaded, 16)

        norm_phase(nc, g, "ln_rwkv", load)
        qk_ps = s.ps("ca_qk_ps", [P, 2, NB])
        score_ps = s.ps("ca_score_ps", [P, 2, SRC])
        turn_ps = s.ps("ca_turn_ps", [P, 2, NB])
        out_ps = s.ps("ca_out_ps", [P, KC, SEQ])
        staged = s.sem("ca_staged")
        qk_ready = s.sem("ca_qk_ready")
        qk_kept = s.sem("ca_qk_kept")
        v_ready = s.sem("ca_v_ready")
        v_kept = s.sem("ca_v_kept")
        scores_ready = s.sem("ca_scores_ready")
        max_ready = s.sem("ca_max_ready")
        scaled_max = s.sem("ca_scaled_max")
        exp_ready = s.sem("ca_exp_ready")
        inverse_ready = s.sem("ca_inverse_ready")
        prob_ready = s.sem("ca_prob_ready")
        turned = s.sem("ca_turned")
        turn_kept = s.sem("ca_turn_kept")
        out_ready = s.sem("ca_out_ready")
        y_part = s.sem("ca_y_part")
        block = s.block()

        def x_of(i):
            return g.xT[:, :, bass.ds(SHIFT, TOK)].rearrange("p k (t b) -> p k t b", b=BATCH)[:, :, :, bass.ds(i, 1)]\
                    .rearrange("p k t o -> p k (t o)")

        @block.sync
        def _(sp):
            for ei in range(2):
                next_weights.load(sp, ei)

        @block.gpsimd
        def _(pool):
            def stage(i):
                pool.tensor_copy(ctx[:, :, :], ctx_all[:, :, bass.ds(i * SRC, SRC)])
                pool.tensor_copy(x[:, :, :], x_of(i)).then_inc(staged, 1)

            pool.wait_ge(loaded, 16 * LOADS)
            stage(0)
            with pool.Fori(0, BATCH - 1) as i:
                pool.wait_ge(v_ready, SC * (i + 1))
                stage(i + 1)

        @block.tensor
        def _(pe):
            def queries_keys(i):
                pe.wait_ge(staged, i + 1)
                for n, (wt, src) in enumerate(((w["q"], x), (w["k"], ctx))):
                    for o in range(KC):
                        if n > 0:
                            pe.wait_ge(qk_kept, 4 * i + o + 1)
                        for k in range(KC):
                            mm = pe.matmul(qk_ps[:, o, :], wt[:, k, o * P:(o + 1) * P], src[:, k, :],
                                           start=(k == 0), stop=(k == KC - 1))
                        mm.then_inc(qk_ready, 1)

            def values(i):
                for c in range(SC):
                    if c >= 2:
                        pe.wait_ge(v_kept, SC * i + c - 1)
                    for k in range(KC):
                        mm = pe.matmul(turn_ps[:, c % 2, 0:DIM], ctx[:, k, c * P:(c + 1) * P], w["v"][:, k, :],
                                       start=(k == 0), stop=(k == KC - 1))
                    mm.then_inc(v_ready, 1)

            def scores(i):
                pe.wait_ge(qk_kept, 4 * i + 4)
                for c in range(QC):
                    if c >= 2:
                        pe.wait_ge(exp_ready, QC * i + c - 1)
                    for k in range(KC):
                        mm = pe.matmul(score_ps[:, c % 2, :], q[:, k, c * P:(c + 1) * P], k_[:, k, :],
                                       start=(k == 0), stop=(k == KC - 1))
                    mm.then_inc(scores_ready, 1)

            def output(i):
                pe.wait_ge(v_kept, SC * i + SC)
                for c in range(QC):
                    pe.wait_ge(prob_ready, QC * i + c + 1)
                    if c >= 2:
                        pe.wait_ge(turn_kept, QC * i + c - 1)
                    for kc in range(SC):
                        mm = pe.transpose(turn_ps[:, c % 2, kc * P:(kc + 1) * P], prob[:, c, kc * P:(kc + 1) * P], ident[:, :])
                    mm.then_inc(turned, 1)
                pe.wait_ge(turn_kept, QC * i + QC)
                for o in range(KC):
                    for kc in range(SC):
                        mm = pe.matmul(out_ps[:, o, :], v[:, kc, o * P:(o + 1) * P], prob_t[:, kc, :],
                                       start=(kc == 0), stop=(kc == SC - 1))
                mm.then_inc(out_ready, 1)

            pe.wait_ge(loaded, 16 * LOADS)
            queries_keys(0)
            values(0)
            with pe.Fori(0, BATCH - 1) as i:
                scores(i)
                queries_keys(i + 1)
                output(i)
                values(i + 1)
            scores(BATCH - 1)
            output(BATCH - 1)

        @block.scalar
        def _(act):
            def keep_queries_keys(i):
                for n, (m, dst) in enumerate((("q", q), ("k", k_))):
                    for o in range(KC):
                        act.wait_ge(qk_ready, 4 * i + 2 * n + o + 1)
                        act.activation(dst[:, o, :], qk_ps[:, o, :], ACT.Identity, bias=b[m][:, o:o + 1]).then_inc(qk_kept, 1)

            def keep_values(i):
                for c in range(SC):
                    act.wait_ge(v_ready, SC * i + c + 1)
                    act.copy(v[:, c, :], turn_ps[:, c % 2, 0:DIM]).then_inc(v_kept, 1)

            def exponentials(i):
                for c in range(QC):
                    act.wait_ge(max_ready, QC * i + c + 1)
                    act.mul(neg_max[:, c:c + 1], neg_max[:, c:c + 1], SCALE).then_inc(scaled_max, 1)
                    act.wait_ge(scaled_max, QC * i + c + 1)
                    act.activation(prob[:, c, :], score_ps[:, c % 2, :], ACT.Exp, bias=neg_max[:, c:c + 1], scale=SCALE,
                                   accum_out=total[:, c:c + 1]).then_inc(exp_ready, 1)

            def keep_turned(i):
                for c in range(QC):
                    act.wait_ge(turned, QC * i + c + 1)
                    act.copy(prob_t[:, :, c * P:(c + 1) * P], turn_ps[:, c % 2, :].rearrange("p (s q) -> p s q", s=SC))\
                       .then_inc(turn_kept, 1)

            act.wait_ge(loaded, 16 * LOADS)
            keep_queries_keys(0)
            keep_values(0)
            with act.Fori(0, BATCH - 1) as i:
                exponentials(i)
                keep_queries_keys(i + 1)
                keep_turned(i)
                keep_values(i + 1)
            exponentials(BATCH - 1)
            keep_turned(BATCH - 1)

        @block.vector
        def _(dve):
            dve.wait_ge(loaded, 16 * LOADS)
            with dve.Fori(0, BATCH) as i:
                for c in range(QC):
                    dve.wait_ge(scores_ready, QC * i + c + 1)
                    dve.tensor_reduce(neg_max[:, c:c + 1], score_ps[:, c % 2, :], AX_X, ALU.max, negate=True).then_inc(max_ready, 1)
                    dve.wait_ge(exp_ready, QC * i + c + 1)
                    dve.reciprocal(total[:, c:c + 1], total[:, c:c + 1]).then_inc(inverse_ready, 1)
                    dve.wait_ge(inverse_ready, QC * i + c + 1)
                    dve.tensor_scalar(prob[:, c, :], prob[:, c, :], total[:, c:c + 1], None, ALU.mult).then_inc(prob_ready, 1)
                dve.wait_ge(out_ready, i + 1)
                for o in range(KC):
                    cols = x_of(i)[:, o, :]
                    dve.scalar_tensor_tensor(out=cols, in0=out_ps[:, o, :], scalar=b["v"][:, o:o + 1],
                                             in1=cols, op0=ALU.add, op1=ALU.add)


MIXTURE0 = Experts("mix", routed=8, shared=0, inner=256, softmax_first=False)
MIXTURE1 = Experts("sm", routed=4, shared=1, inner=688, softmax_first=True)


class Shared:
    pass


def decoder_program(nc, d):
    with Scope(nc) as s:
        g = Shared()
        g.xT = s.sb("xT", [P, KC, SHIFT + TOK])
        g.mean_mat = s.sb("mean_mat", [P, P])
        g.spread = s.sb("spread", [P, QUARTERS, P])
        g.eps = s.sb("eps", [P, 1])
        g.consts = s.sem("consts")
        with Scope(nc) as m:
            raw = RawWeights(m, d, MIXTURE0)
            with Scope(nc) as c:
                g.ctxT = c.sb("ctxT", [P, KC, BATCH * SRC])
                recurrence_phase(nc, d, g)
                attention_lstm_phase(nc, d, g, raw)
            mixture_phase(nc, d, g, MIXTURE0, raw)
        rwkv_phase(nc, d, g)
        with Scope(nc) as m:
            raw = RawWeights(m, d, MIXTURE1)
            cross_attention_phase(nc, d, g, raw)
            mixture_phase(nc, d, g, MIXTURE1, raw)
        norm_phase(nc, g, "ln_mixture1", out=d["out"])



def feature_major(x):
    return np.ascontiguousarray(x.transpose(2, 1, 0).reshape(KC, P, TOK).transpose(1, 0, 2))


def rows_on_partitions(w):
    return np.ascontiguousarray(w.reshape(-1, P, w.shape[1]).transpose(1, 0, 2))


def on_partitions(b):
    return np.ascontiguousarray(b.reshape(-1, P).T)


def each(f, ws):
    return np.ascontiguousarray(np.stack([f(w) for w in ws]))


def by_quarter(w):
    w = w.reshape(*w.shape[:-1], GATES, QUARTERS, QW)[..., [3, 0, 1, 2], :, :]
    return np.ascontiguousarray(np.moveaxis(w, -2, -3).reshape(*w.shape[:-3], GATE_W))


def hidden_order(w):
    return np.ascontiguousarray(w.reshape(QUARTERS, KC, STRIP, -1).swapaxes(0, 1).reshape(HID, -1))


def laid_out(inputs):
    i = {name: np.asarray(a) for name, a in inputs.items()}
    d = {"xT": feature_major(i["x"]),
         "ctxT": np.ascontiguousarray(i["ctx_1024"].transpose(2, 0, 1).reshape(KC, P, BATCH * SRC).transpose(1, 0, 2))}
    for m in ("in", "gate", "lam", "out"):
        d[f"rec_w_{m}"] = rows_on_partitions(i[f"L0_attn_W_{m}"].T)
        d[f"rec_b_{m}"] = on_partitions(i[f"L0_attn_b_{m}"])
    d["rec_gamma"] = on_partitions(i["L0_attn_gamma"])
    d["rec_beta"] = on_partitions(i["L0_attn_beta"])

    w_ih, w_out = i["L0_xattn_W_ih"], i["L0_xattn_Wout"]
    d["lstm_w_x"] = rows_on_partitions(by_quarter(w_ih[:, :DIM].T))
    d["lstm_w_attn"] = rows_on_partitions(by_quarter(w_ih[:, DIM:].T))
    d["lstm_w_hid"] = rows_on_partitions(hidden_order(by_quarter(i["L0_xattn_W_hh"].T)))
    d["lstm_w_q"] = rows_on_partitions(hidden_order(i["L0_xattn_Wq"].T).T)
    d["lstm_w_out_c"] = rows_on_partitions(w_out[:, :DIM].T)
    d["lstm_w_out_h"] = rows_on_partitions(hidden_order(w_out[:, DIM:].T))
    d["lstm_b_ih"], d["lstm_b_hh"] = (by_quarter(i[f"L0_xattn_{b}"]) for b in ("b_ih", "b_hh"))
    d["lstm_b_out"] = i["L0_xattn_b_out"]

    d["mix_w_router"] = rows_on_partitions(i["L0_ffn_router_w"])
    d["mix_b_router"] = np.ascontiguousarray(i["L0_ffn_router_b"].reshape(-1, 1))
    d["mix_w_down"] = i["L0_ffn_we_down"]
    for m in ("gate", "up"):
        d[f"mix_w_{m}"] = each(rows_on_partitions, i[f"L0_ffn_we_{m}"])

    rw = {name[len("L1_attn_"):]: a for name, a in i.items() if name.startswith("L1_attn_")}
    d["rw_mix_w"] = np.ascontiguousarray(np.stack([on_partitions(rw[f"x_{m}"]) for m in "rwkva"], 1))
    for m in ("r", "k", "v", "o"):
        d[f"rw_w_{m}"] = rows_on_partitions(rw[f"W_{m}"])
    for m in ("w", "a", "g"):
        d[f"rw_wa_{m}"] = rows_on_partitions(rw[f"{m}_lora_a"])
        d[f"rw_wb_{m}"] = rw[f"{m}_lora_b"]
        d[f"rw_{m}_bias"] = rw[f"{m}_lora_bias"]
    d["rw_k_k"], d["rw_k_a"], d["rw_r_k"] = rw["k_k"], rw["k_a"], rw["r_k"].reshape(-1)
    d["rw_gn_w"], d["rw_gn_b"] = rw["gn_weight"], rw["gn_bias"]

    for m in ("q", "k", "v"):
        d[f"ca_w_{m}"] = rows_on_partitions(i[f"L1_xattn_W{m}"].T)
        d[f"ca_b_{m}"] = on_partitions(i[f"L1_xattn_b{m}"])

    d["sm_w_router"] = rows_on_partitions(i["L1_ffn_gate_w"].T)
    d["sm_w_gate"] = each(lambda w: rows_on_partitions(w.T), [*i["L1_ffn_eg"], i["L1_ffn_sg"]])
    d["sm_w_up"] = each(lambda w: rows_on_partitions(w.T), [*i["L1_ffn_eu"], i["L1_ffn_su"]])
    d["sm_w_down"] = each(lambda w: w.T, [*i["L1_ffn_ed"], i["L1_ffn_sd"]])

    sel_batch = np.zeros((P, BATCH), np.float32)
    sel_batch[np.arange(BATCH) * STRIP, np.arange(BATCH)] = 1
    for k in range(KC):
        sel_batch[k * STRIP + 1 + np.arange(BATCH), np.arange(BATCH)] = 1
    d["sel_batch"] = sel_batch
    d["ident"] = np.eye(P, dtype=np.float32)
    most = max(MIXTURE0.routed, MIXTURE1.routed)
    pick = np.zeros((most, most, P), np.float32)
    pick[np.arange(most), np.arange(most)] = 1
    d["pick"] = pick
    return d


def kernel(**inputs):
    import concourse.bacc as bacc
    from concourse.bass_utils import run_bass_kernel_spmd

    nc = bacc.Bacc("TRN2", target_bir_lowering=False, num_devices=1)
    arrays, d = {}, {}
    for name, a in laid_out(inputs).items():
        arrays[f"in_{name}"] = np.ascontiguousarray(a)
        d[name] = nc.dram_tensor(f"in_{name}", a.shape, F32, kind="ExternalInput").ap()
    d["out"] = nc.dram_tensor("out_xT", (P, KC, TOK), F32, kind="ExternalOutput").ap()
    decoder_program(nc, d)
    r = run_bass_kernel_spmd(nc, [arrays], core_ids=[0])
    got = np.asarray(r.results[0]["out_xT"])
    return np.ascontiguousarray(got.transpose(1, 0, 2).reshape(DIM, SEQ, BATCH).transpose(2, 1, 0))
```
